# Optimizing a Trainium2 kernel written in Bass

```python
import numpy as np
import jax
import jax.numpy as jnp

def _softmax(x, axis=-1):
    return jax.nn.softmax(x, axis=axis)

def _gelu(x):
    return jax.nn.gelu(x, approximate=True)

def _silu(x):
    return jax.nn.silu(x)

def _sigmoid(x):
    return jax.nn.sigmoid(x)

def _layernorm(x, axis=-1, eps=1e-05):
    m = jnp.mean(x, axis=axis, keepdims=True)
    v = jnp.var(x, axis=axis, keepdims=True)
    return (x - m) / jnp.sqrt(v + eps)

def _scatter_add(tgt, idx, src, axis=0):
    return tgt.at[idx].add(src)

def _segment_sum(src, seg, n):
    return jax.ops.segment_sum(src, seg, n)
kernel_name = 'mk_gnn_resnorm_d2_gnn_r32_7be6f5'

def setup_inputs(seed: int=0):
    np.random.seed(seed)
    _w = jnp.asarray

    def _rec_inputs():
        import jax
        import jax.numpy as jnp
        _gk = jax.random.key(seed)
        x = -0.000202 + 1 * jax.random.normal(jax.random.fold_in(_gk, 1), (50000, 128), jnp.float32)
        src = jax.random.randint(jax.random.fold_in(_gk, 2), (50000,), 0, 50000, jnp.int32)
        dst = jnp.minimum((50000 * jax.random.uniform(jax.random.fold_in(_gk, 3), (50000,)) ** 2.0).astype(jnp.int32), 49999)
        _o = jnp.argsort(dst, stable=True)
        src = src[_o]
        dst = dst[_o]
        edge_attr_128 = 5.93493e-05 + 1.00006 * jax.random.normal(jax.random.fold_in(_gk, 12), (50000, 128), jnp.float32)
        return (x, src, dst, edge_attr_128)
    x, src, dst, edge_attr_128 = _rec_inputs()

    def _L0_gnn_setup():
        import jax, jax.numpy as jnp
        import numpy as np
        N_NODES = 50000
        N_EDGES = 25000
        D = 128
        key = jax.random.key(seed)
        ks = jax.random.split(key, 8)
        s = 0.05
        return {'h': jax.random.normal(ks[0], (N_NODES, D), dtype=jnp.float32), 'src': jax.random.randint(ks[1], (N_EDGES,), 0, N_NODES, dtype=jnp.int32), 'dst': jax.random.randint(ks[2], (N_EDGES,), 0, N_NODES, dtype=jnp.int32), 'Wm1': jax.random.normal(ks[3], (2 * D, 2 * D), dtype=jnp.float32) * s, 'bm1': jnp.zeros((2 * D,), dtype=jnp.float32), 'Wm2': jax.random.normal(ks[4], (2 * D, D), dtype=jnp.float32) * s, 'bm2': jnp.zeros((D,), dtype=jnp.float32), 'Wn': jax.random.normal(ks[5], (2 * D, D), dtype=jnp.float32) * s, 'bn': jnp.zeros((D,), dtype=jnp.float32), 'num_steps': 3}
    _L0_gnn_all = _L0_gnn_setup()
    _L0_gnn_in = {k: v for k, v in _L0_gnn_all.items() if k in ('Wm1', 'bm1', 'Wm2', 'bm2', 'Wn', 'bn')}
    del _L0_gnn_all

    def _L1_gnn_setup():
        import jax, jax.numpy as jnp
        import numpy as np
        NUM_HEADS = 8
        BN_EPS = 1e-05
        ATTN_EPS = 1e-06

        def batch_norm(x, gamma, beta):
            mu = jnp.mean(x, axis=0)
            var = jnp.var(x, axis=0)
            return gamma * (x - mu) * jax.lax.rsqrt(var + BN_EPS) + beta
        key = jax.random.key(seed)
        ks = jax.random.split(key, 16)
        N, E, D = (50000, 18750, 128)
        s = 1.0 / np.sqrt(D)
        inp = {'x': jax.random.normal(ks[0], (N, D), jnp.float32), 'edge_index': jax.random.randint(ks[1], (2, E), 0, N, dtype=jnp.int64), 'edge_attr': jax.random.normal(ks[2], (E, D), jnp.float32), 'WQ': jax.random.normal(ks[3], (D, D), jnp.float32) * s, 'WK': jax.random.normal(ks[4], (D, D), jnp.float32) * s, 'WV': jax.random.normal(ks[5], (D, D), jnp.float32) * s, 'WE': jax.random.normal(ks[6], (D, D), jnp.float32) * s, 'gamma1': jnp.ones((D,), jnp.float32), 'beta1': jnp.zeros((D,), jnp.float32), 'gamma2': jnp.ones((D,), jnp.float32), 'beta2': jnp.zeros((D,), jnp.float32), 'W1': jax.random.normal(ks[7], (D, 2 * D), jnp.float32) * s, 'b1': jnp.zeros((2 * D,), jnp.float32), 'W2': jax.random.normal(ks[8], (2 * D, D), jnp.float32) * (1.0 / np.sqrt(2 * D)), 'b2': jnp.zeros((D,), jnp.float32)}
        return inp
    _L1_gnn_all = _L1_gnn_setup()
    _L1_gnn_in = {k: v for k, v in _L1_gnn_all.items() if k in ('WQ', 'WK', 'WV', 'WE', 'gamma1', 'beta1', 'gamma2', 'beta2', 'W1', 'b1', 'W2', 'b2')}
    del _L1_gnn_all
    return {'x': x, 'src': src, 'dst': dst, 'edge_attr_128': edge_attr_128, 'L0_gnn_Wm1': _L0_gnn_in['Wm1'], 'L0_gnn_bm1': _L0_gnn_in['bm1'], 'L0_gnn_Wm2': _L0_gnn_in['Wm2'], 'L0_gnn_bm2': _L0_gnn_in['bm2'], 'L0_gnn_Wn': _L0_gnn_in['Wn'], 'L0_gnn_bn': _L0_gnn_in['bn'], 'L1_gnn_WQ': _L1_gnn_in['WQ'], 'L1_gnn_WK': _L1_gnn_in['WK'], 'L1_gnn_WV': _L1_gnn_in['WV'], 'L1_gnn_WE': _L1_gnn_in['WE'], 'L1_gnn_gamma1': _L1_gnn_in['gamma1'], 'L1_gnn_beta1': _L1_gnn_in['beta1'], 'L1_gnn_gamma2': _L1_gnn_in['gamma2'], 'L1_gnn_beta2': _L1_gnn_in['beta2'], 'L1_gnn_W1': _L1_gnn_in['W1'], 'L1_gnn_b1': _L1_gnn_in['b1'], 'L1_gnn_W2': _L1_gnn_in['W2'], 'L1_gnn_b2': _L1_gnn_in['b2']}

def reference(x, src, dst, edge_attr_128, L0_gnn_Wm1, L0_gnn_bm1, L0_gnn_Wm2, L0_gnn_bm2, L0_gnn_Wn, L0_gnn_bn, L1_gnn_WQ, L1_gnn_WK, L1_gnn_WV, L1_gnn_WE, L1_gnn_gamma1, L1_gnn_beta1, L1_gnn_gamma2, L1_gnn_beta2, L1_gnn_W1, L1_gnn_b1, L1_gnn_W2, L1_gnn_b2):
    import jax
    import jax.numpy as jnp

    def _L0_gnn_ref(h, src, dst, Wm1, bm1, Wm2, bm2, Wn, bn, num_steps):
        import jax, jax.numpy as jnp
        import numpy as np
        N_NODES = 50000
        N_EDGES = 25000
        D = 128
        n_nodes = h.shape[0]
        for _ in range(num_steps):
            e = jnp.concatenate([h[src], h[dst]], axis=-1)
            e = jax.nn.relu(e @ Wm1 + bm1)
            e = e @ Wm2 + bm2
            m = jax.ops.segment_sum(e, dst, num_segments=n_nodes)
            h = jax.nn.relu(jnp.concatenate([h, m], axis=-1) @ Wn + bn)
        return h

    def _L1_gnn_ref(x, edge_index, edge_attr, WQ, WK, WV, WE, gamma1, beta1, gamma2, beta2, W1, b1, W2, b2):
        import jax, jax.numpy as jnp
        import numpy as np
        NUM_HEADS = 8
        BN_EPS = 1e-05
        ATTN_EPS = 1e-06

        def batch_norm(x, gamma, beta):
            mu = jnp.mean(x, axis=0)
            var = jnp.var(x, axis=0)
            return gamma * (x - mu) * jax.lax.rsqrt(var + BN_EPS) + beta
        N, D = x.shape
        H = NUM_HEADS
        dh = D // H
        src = edge_index[0]
        dst = edge_index[1]
        Q = (x @ WQ).reshape(N, H, dh)
        K = (x @ WK).reshape(N, H, dh)
        V = (x @ WV).reshape(N, H, dh)
        Eh = (edge_attr @ WE).reshape(-1, H, dh)
        score = K[src] * Q[dst] * (1.0 / np.sqrt(dh)) * Eh
        s = jnp.exp(jnp.clip(jnp.sum(score, axis=-1), -5.0, 5.0))
        msg = V[src] * s[:, :, None]
        wV = jax.ops.segment_sum(msg, dst, num_segments=N)
        Z = jax.ops.segment_sum(s, dst, num_segments=N)
        h_attn = (wV / (Z[:, :, None] + ATTN_EPS)).reshape(N, D)
        h = batch_norm(x + h_attn, gamma1, beta1)
        ff = jax.nn.relu(h @ W1 + b1) @ W2 + b2
        h = batch_norm(h + ff, gamma2, beta2)
        return h
    edge_index = jnp.stack([src, dst])
    x = _layernorm(x + _L0_gnn_ref(x, src, dst, L0_gnn_Wm1, L0_gnn_bm1, L0_gnn_Wm2, L0_gnn_bm2, L0_gnn_Wn, L0_gnn_bn, 3), axis=-1)
    x = _layernorm(x + _L1_gnn_ref(x, edge_index, edge_attr_128, L1_gnn_WQ, L1_gnn_WK, L1_gnn_WV, L1_gnn_WE, L1_gnn_gamma1, L1_gnn_beta1, L1_gnn_gamma2, L1_gnn_beta2, L1_gnn_W1, L1_gnn_b1, L1_gnn_W2, L1_gnn_b2), axis=-1)
    return x

_drawn_inputs = setup_inputs


def setup_inputs(seed=0):
    import zlib

    import numpy as np

    out = dict(_drawn_inputs(seed))
    spreads = {'L0_gnn_bm1': (0.0, 0.305),
     'L0_gnn_bm2': (0.0, 0.1),
     'L0_gnn_bn': (0.0, 0.1),
     'L1_gnn_gamma1': (1.0, 0.2),
     'L1_gnn_beta1': (0.0, 0.325),
     'L1_gnn_gamma2': (1.0, 0.2),
     'L1_gnn_beta2': (0.0, 0.1),
     'L1_gnn_b1': (0.0, 0.349),
     'L1_gnn_b2': (0.0, 0.8)}
    factors = {}
    for name, (base, spread) in spreads.items():
        noise = np.random.default_rng([zlib.crc32(name.encode()), seed]).standard_normal(out[name].shape)
        drawn = base * np.exp(spread * noise) if base else spread * noise
        out[name] = jnp.asarray(drawn.astype(out[name].dtype))
    for name, factor in factors.items():
        out[name] = (out[name] * factor).astype(out[name].dtype)
    return out
```

```python
from contextlib import ExitStack

import concourse.bass as bass
from concourse import mybir

F32 = mybir.dt.float32
I32 = mybir.dt.int32
ALU = mybir.AluOpType
ACT = mybir.ActivationFunctionType
AX = mybir.AxisListType

P = 128
D = 128
ROWS = 8
BLOCK = P * ROWS
HALF = BLOCK // 2
TILES = 4
GROUP = P * TILES
HEADS = 8
DH = D // HEADS
AT = D + HEADS
LN_EPS = 1e-5
BN_EPS = 1e-5
ATTN_EPS = 1e-6
CLIP = 5.0


def rows_of(table, first, n=BLOCK, rows=ROWS):
    return table[bass.ds(first, n), :].rearrange("(p r) c -> p (r c)", r=rows)


def parts_of(n):
    whole = n - n % 16
    return [(a, b) for a, b in ((0, whole), (whole, n)) if b > a]


def gate(g, eng):
    eng.sem_inc(g.gates[eng.engine], 1)


class Graph:

    def __init__(self, nc, ctx, args):
        self.nc = nc
        self.x = args["x"]
        self.src = args["src"]
        self.dst = args["dst"]
        self.edge_attr_128 = args["edge_attr_128"]
        self.L0_gnn_Wm1 = args["L0_gnn_Wm1"]
        self.L0_gnn_bm1 = args["L0_gnn_bm1"]
        self.L0_gnn_Wm2 = args["L0_gnn_Wm2"]
        self.L0_gnn_bm2 = args["L0_gnn_bm2"]
        self.L0_gnn_Wn = args["L0_gnn_Wn"]
        self.L0_gnn_bn = args["L0_gnn_bn"]
        self.L1_gnn_WQ = args["L1_gnn_WQ"]
        self.L1_gnn_WK = args["L1_gnn_WK"]
        self.L1_gnn_WV = args["L1_gnn_WV"]
        self.L1_gnn_WE = args["L1_gnn_WE"]
        self.L1_gnn_gamma1 = args["L1_gnn_gamma1"]
        self.L1_gnn_beta1 = args["L1_gnn_beta1"]
        self.L1_gnn_gamma2 = args["L1_gnn_gamma2"]
        self.L1_gnn_beta2 = args["L1_gnn_beta2"]
        self.L1_gnn_W1 = args["L1_gnn_W1"]
        self.L1_gnn_b1 = args["L1_gnn_b1"]
        self.L1_gnn_W2 = args["L1_gnn_W2"]
        self.L1_gnn_b2 = args["L1_gnn_b2"]
        self.out = args["out"]
        self.N = self.x.shape[0]
        self.E = self.src.shape[0]
        self.BLOCKS = -(-self.N // BLOCK)
        self.GROUPS = -(-self.E // GROUP)
        self.NP = self.BLOCKS * BLOCK
        self.EP = self.GROUPS * GROUP
        self.TAIL_PARTS = (self.N - (self.BLOCKS - 1) * BLOCK) // ROWS
        self.TAIL_EDGES = self.E - (self.GROUPS - 1) * GROUP
        self.SPARE = self.N + P
        assert self.N % ROWS == 0 and self.BLOCKS % 2 == 1 and self.BLOCKS > 2
        assert self.GROUPS == 2 * self.BLOCKS and self.TAIL_EDGES % TILES == 0
        assert self.SPARE < self.NP

        def dram(name, shape, dt=F32):
            return nc.dram_tensor(name, shape, dt)

        self.gates = {eng.engine: ctx.enter_context(nc.semaphore(f"gate{n}"))
                      for n, eng in enumerate((nc.gpsimd, nc.sync, nc.vector))}
        self.h_table = dram("h_table", (self.NP, D))
        self.sums = dram("sums", (self.NP, D))
        self.attn_sums = dram("attn_sums", (self.NP, AT))
        self.x1_table = dram("x1_table", (self.NP, D))
        self.q_table = dram("q_table", (self.NP, D))
        self.kv_table = dram("kv_table", (self.NP, 2 * D))
        self.turned_table = dram("turned_table", (self.BLOCKS * P, BLOCK))
        self.dst_padded = dram("dst_padded", (self.EP,), I32)

        def sb(name, shape, dt=F32):
            return ctx.enter_context(nc.sbuf_tensor(name, shape, dt))

        self.ident = sb("ident", [P, P])
        self.Wm1_sb = sb("Wm1_sb", [P, 2, 2 * D])
        self.Wm2n_sb = sb("Wm2n_sb", [P, 2, D])
        self.Wna_sb = sb("Wna_sb", [P, D])
        self.Wqkv_sb = sb("Wqkv_sb", [P, 3 * D])
        self.WE_sb = sb("WE_sb", [P, D])
        self.W1_sb = sb("W1_sb", [P, 2 * D])
        self.W2_sb = sb("W2_sb", [P, 2, D])
        self.bm1_col = sb("bm1_col", [P, 2])
        self.b1_col = sb("b1_col", [P, 2])
        self.b2_col = sb("b2_col", [P, 1])
        self.bn_all = sb("bn_all", [P, D])
        self.bm2n_all = sb("bm2n_all", [P, D])
        self.gammas = sb("gammas", [P, 2])
        self.betas = sb("betas", [P, 2])
        self.eps_col = sb("eps_col", [P, 1])
        self.gather_rows = sb("gather_rows", [P, self.GROUPS + 2, 2 * TILES], I32)
        self.scatter_rows = sb("scatter_rows", [P, self.GROUPS, TILES], I32)
        self.dst_col = sb("dst_col", [P, self.GROUPS, TILES])
        self.feature_stats = sb("feature_stats", [P, self.GROUPS, 6])


def setup(g):
    nc = g.nc
    G = g.GROUPS
    with ExitStack() as ctx:
        def sb(name, shape, dt=F32):
            return ctx.enter_context(nc.sbuf_tensor(name, shape, dt))

        sems = []

        def sem(name):
            sems.append(nc.alloc_semaphore(name))
            return sems[-1]

        Wm2_rows = sb("Wm2_rows", [P, 2, D])
        Wm2_turned = sb("Wm2_turned", [P, 2 * D])
        Wnb = sb("Wnb", [P, D])
        bm2_col = sb("bm2_col", [P, 1])
        bm2_wide = sb("bm2_wide", [P, P])
        ones = sb("ones", [P, P])
        edge_rows = sb("edge_rows", [P, 2, GROUP], I32)
        edge_rows_f = sb("edge_rows_f", [P, 2, GROUP])
        clipped = sb("clipped", [P, TILES, G])
        ps_edges = ctx.enter_context(nc.psum_tensor("ps_edges", [P, 2, TILES, P], F32))
        ps_turn = ctx.enter_context(nc.psum_tensor("ps_turn", [P, 512], F32))
        ps_fold = ctx.enter_context(nc.psum_tensor("ps_fold", [P, 512], F32))

        filled = sem("filled")
        ones_ready = sem("ones_ready")
        ident_ready = sem("ident_ready")
        ends_loaded = sem("ends_loaded")
        dst_stored = sem("dst_stored")
        weights_loaded = sem("weights_loaded")
        ends_converted = sem("ends_converted")
        ends_turned = sem("ends_turned")
        dst_clipped = sem("dst_clipped")
        rows_ready = sem("rows_ready")
        wm2_turned = sem("wm2_turned")
        fold_inputs = sem("fold_inputs")
        folded = sem("folded")
        fold_copied = sem("fold_copied")
        block = ctx.enter_context(nc.Block())

        def column(v):
            return v.rearrange("(a p) -> p a", p=P)

        loads = [
            (Wm2_rows[:, :, :], g.L0_gnn_Wm2.rearrange("(a p) n -> p a n", p=P)),
            (Wnb[:, :], g.L0_gnn_Wn[D:2 * D, :]),
            (bm2_col[:, :], column(g.L0_gnn_bm2)),
            (g.Wna_sb[:, :], g.L0_gnn_Wn[0:D, :]),
            (g.Wm1_sb[:, :, :], g.L0_gnn_Wm1.rearrange("(a p) n -> p a n", p=P)),
            (g.bm1_col[:, :], column(g.L0_gnn_bm1)),
            (g.bn_all[:, :], g.L0_gnn_bn.partition_broadcast(P)),
            (g.Wqkv_sb[:, 0:D], g.L1_gnn_WQ),
            (g.Wqkv_sb[:, D:2 * D], g.L1_gnn_WK),
            (g.Wqkv_sb[:, 2 * D:3 * D], g.L1_gnn_WV),
            (g.WE_sb[:, :], g.L1_gnn_WE),
            (g.W1_sb[:, :], g.L1_gnn_W1),
            (g.W2_sb[:, :, :], g.L1_gnn_W2.rearrange("(a p) n -> p a n", p=P)),
            (g.b1_col[:, :], column(g.L1_gnn_b1)),
            (g.b2_col[:, :], column(g.L1_gnn_b2)),
            (g.gammas[:, 0:1], column(g.L1_gnn_gamma1)),
            (g.gammas[:, 1:2], column(g.L1_gnn_gamma2)),
            (g.betas[:, 0:1], column(g.L1_gnn_beta1)),
            (g.betas[:, 1:2], column(g.L1_gnn_beta2)),
        ]

        @block.sync
        def _(sp):
            sp.wait_ge(filled, 2)
            whole = (G - 1) * GROUP
            for k, ends in enumerate((g.src, g.dst)):
                sp.dma_start(edge_rows[0:G - 1, k, :],
                             ends[0:whole].rearrange("(g e) -> g e", e=GROUP)).then_inc(ends_loaded, 16)
                sp.dma_start(edge_rows[G - 1:G, k, 0:g.TAIL_EDGES],
                             ends[whole:g.E].rearrange("(g e) -> g e", g=1)).then_inc(ends_loaded, 16)
            sp.dma_start(g.dst_padded[0:g.E], g.dst).then_inc(dst_stored, 16)
            if g.EP > g.E:
                sp.wait_ge(ends_loaded, 64)
                gate(g, sp)
                sp.dma_start(g.dst_padded[g.E:g.EP].rearrange("(a e) -> a e", a=1),
                             edge_rows[G - 1:G, 1, g.TAIL_EDGES:GROUP]).then_inc(dst_stored, 16)
            sp.wait_ge(dst_stored, 32 if g.EP > g.E else 16)

        @block.gpsimd
        def _(pool):
            pool.memset(ones[:, :], 1.0).then_inc(ones_ready, 1)
            pool.wait_ge(ones_ready, 1)
            pool.affine_select(out=g.ident[:, :], in_=ones[:, :], compare_op=ALU.is_equal, fill=0.0, base=0,
                               pattern=[[-1, P]], channel_multiplier=1).then_inc(ident_ready, 1)

        @block.scalar
        def _(act):
            for to, of in loads:
                act.dma_start(to, of, allow_slow_non_contiguous=True).then_inc(weights_loaded, 16)
            act.wait_ge(weights_loaded, 16 * len(loads))
            act.wait_ge(ones_ready, 1)
            act.activation(bm2_wide[:, :], ones[:, :], ACT.Copy, scale=bm2_col[:, 0:1]).then_inc(fold_inputs, 1)
            act.wait_ge(wm2_turned, 1)
            act.copy(Wm2_turned[:, :], ps_turn[:, 0:2 * D]).then_inc(fold_inputs, 1)

        @block.tensor
        def _(pe):
            pe.wait_ge(ident_ready, 1)
            pe.wait_ge(ends_converted, 1)
            for k in range(2):
                for j in range(TILES):
                    last = pe.transpose(ps_edges[:, k, j, 0:G], edge_rows_f[0:G, k, j:GROUP:TILES],
                                        g.ident[0:G, 0:G])
            last.then_inc(ends_turned, 1)
            pe.wait_ge(weights_loaded, 16 * len(loads))
            for m in range(2):
                last = pe.transpose(ps_turn[:, m * D:(m + 1) * D], Wm2_rows[:, m, :], g.ident[:, :])
            last.then_inc(wm2_turned, 1)
            pe.wait_ge(fold_inputs, 2)
            for m in range(2):
                pe.matmul(ps_fold[:, m * D:(m + 1) * D], Wm2_turned[:, m * D:(m + 1) * D], Wnb[:, :],
                          start=True, stop=True)
            pe.matmul(ps_fold[:, 2 * D:3 * D], bm2_wide[:, :], Wnb[:, :], start=True, stop=True).then_inc(folded, 1)

        @block.vector
        def _(dve):
            dve.memset(edge_rows[:, 0, :], 0).then_inc(filled, 1)
            dve.memset(edge_rows[:, 1, :], g.SPARE).then_inc(filled, 1)
            dve.memset(g.eps_col[:, :], LN_EPS)
            dve.memset(g.gather_rows[:, :, :], 0).then_inc(rows_ready, 1)
            dve.wait_ge(ends_loaded, 64)
            dve.tensor_copy(edge_rows_f[0:G, :, :], edge_rows[0:G, :, :]).then_inc(ends_converted, 1)
            dve.wait_ge(ends_turned, 1)
            dve.wait_ge(rows_ready, 1)
            by_tile = g.gather_rows[:, 0:G, :].rearrange("p g t -> p t g")
            dve.tensor_copy(by_tile[:, 0:TILES, :], ps_edges[:, 0, :, 0:G])
            dve.tensor_copy(g.dst_col[:, :, :].rearrange("p g t -> p t g"), ps_edges[:, 1, :, 0:G])
            dve.tensor_scalar(clipped[:, :, :], ps_edges[:, 1, :, 0:G], float(g.N - 1), None,
                              ALU.min).then_inc(dst_clipped, 1)
            dve.wait_ge(dst_clipped, 1)
            dve.tensor_copy(by_tile[:, TILES:2 * TILES, :], clipped[:, :, :])
            dve.wait_ge(folded, 1)
            dve.tensor_copy(g.Wm2n_sb[:, :, :], ps_fold[:, 0:2 * D].rearrange("p (a n) -> p a n", a=2))
            dve.tensor_copy(g.bm2n_all[:, :], ps_fold[:, 2 * D:3 * D]).then_inc(fold_copied, 1)
    nc.clear_and_free_semaphores(sems)
    nc.all_engine_barrier()


def start_sums(g):
    nc = g.nc
    with ExitStack() as ctx:
        def sb(name, shape, dt=F32):
            return ctx.enter_context(nc.sbuf_tensor(name, shape, dt))

        sems = []

        def sem(name):
            sems.append(nc.alloc_semaphore(name))
            return sems[-1]

        x_in = [sb(f"x_in{b}", [P, BLOCK]) for b in range(2)]
        turned = [sb(f"turned{h}", [P, HALF]) for h in range(2)]
        new_sums = [sb(f"new_sums{b}", [P, BLOCK]) for b in range(2)]
        targets = [sb(f"targets{h}", [P, GROUP], I32) for h in range(2)]
        earlier = sb("earlier", [P, P])
        ones = sb("ones_a", [P, P])
        spare_i = sb("spare_i", [P, 1], I32)
        spare = sb("spare", [P, 1])
        matches = sb("matches", [P, TILES, P])
        repeats = sb("repeats", [P, g.GROUPS, TILES])
        shift = sb("shift", [P, g.GROUPS, TILES])
        moved = sb("moved", [P, g.GROUPS, TILES])
        ps_turn = [ctx.enter_context(nc.psum_tensor(f"ps_turn_a{h}", [P, 512], F32)) for h in range(2)]
        ps_sum = [ctx.enter_context(nc.psum_tensor(f"ps_sum_a{h}", [P, 512], F32)) for h in range(2)]

        x_loaded = [sem(f"x_loaded{b}") for b in range(2)]
        x_turned = [[sem(f"x_turned{b}{h}") for h in range(2)] for b in range(2)]
        x_copied = [sem(f"x_copied{h}") for h in range(2)]
        projected = [sem(f"projected{h}") for h in range(2)]
        bias_added = [sem(f"bias_added{h}") for h in range(2)]
        sums_stored = [sem(f"sums_stored{b}") for b in range(2)]
        targets_loaded = [sem(f"targets_loaded{h}") for h in range(2)]
        counted = [sem(f"counted{h}") for h in range(2)]
        earlier_ready = sem("earlier_ready")
        spare_ready = sem("spare_ready")
        pieces = parts_of(g.TAIL_PARTS)
        block = ctx.enter_context(nc.Block())

        @block.sync
        def _(sp):
            def load(i, b, last=False):
                n = i * 2 + b
                sp.wait_ge(x_turned[b][1], i)
                gate(g, sp)
                if last:
                    for a, z in pieces:
                        sp.dma_start(x_in[b][a:z, :], rows_of(g.x, n * BLOCK + a * ROWS, (z - a) * ROWS)
                                     ).then_inc(x_loaded[b], 16)
                else:
                    sp.dma_start(x_in[b][:, :], rows_of(g.x, n * BLOCK)).then_inc(x_loaded[b], 16)
                for h in range(2):
                    sp.wait_ge(counted[h], n)
                    gate(g, sp)
                    sp.dma_start(targets[h][:, :], g.dst_padded[bass.ds(n * BLOCK + h * GROUP, GROUP)]
                                 .partition_broadcast(P)).then_inc(targets_loaded[h], 16)

            with sp.Fori(0, g.BLOCKS // 2) as i:
                load(i, 0)
                load(i, 1)
            load(g.BLOCKS // 2, 0, last=True)

        @block.tensor
        def _(pe):
            def body(i, b, last=False):
                n = i * 2 + b
                pe.wait_ge(x_loaded[b], i * 16 + 16 * (len(pieces) if last else 1))
                for h in range(2):
                    pe.wait_ge(x_copied[h], n)
                    for r in range(4):
                        at = (4 * h + r) * D
                        mm = pe.transpose(ps_turn[h][:, r * P:(r + 1) * P], x_in[b][:, at:at + D], g.ident[:, :])
                    mm.then_inc(x_turned[b][h], 1)
                for h in range(2):
                    pe.wait_ge(x_copied[h], n + 1)
                    pe.wait_ge(bias_added[h], n)
                    for r in range(4):
                        mm = pe.matmul(ps_sum[h][:, r * D:(r + 1) * D], turned[h][:, r * P:(r + 1) * P],
                                       g.Wna_sb[:, :], start=True, stop=True)
                    mm.then_inc(projected[h], 1)

            with pe.Fori(0, g.BLOCKS // 2) as i:
                body(i, 0)
                body(i, 1)
            body(g.BLOCKS // 2, 0, last=True)

        @block.scalar
        def _(act):
            def body(i, b):
                n = i * 2 + b
                for h in range(2):
                    act.wait_ge(x_turned[b][h], i + 1)
                    act.copy(turned[h][:, :], ps_turn[h][:, :]).then_inc(x_copied[h], 1)

            with act.Fori(0, g.BLOCKS // 2) as i:
                body(i, 0)
                body(i, 1)
            body(g.BLOCKS // 2, 0)

        @block.vector
        def _(dve):
            dve.wait_ge(earlier_ready, 2)

            def body(i, b):
                n = i * 2 + b
                for h in range(2):
                    dve.wait_ge(targets_loaded[h], n * 16 + 16)
                    dve.wait_ge(counted[1 - h], n + h)
                    for j in range(TILES):
                        at = dve.scalar_tensor_tensor(
                            out=matches[:, j, :], in0=targets[h][:, j:GROUP:TILES],
                            scalar=g.dst_col[:, bass.ds(n * 2 + h, 1), j], in1=earlier[:, :],
                            op0=ALU.is_equal, op1=ALU.mult, accum_out=repeats[:, bass.ds(n * 2 + h, 1), j])
                    at.then_inc(counted[h], 1)
                    dve.wait_ge(projected[h], n + 1)
                    dve.wait_ge(sums_stored[b], i * 16)
                    dve.tensor_tensor(
                        new_sums[b][:, h * HALF:(h + 1) * HALF].rearrange("p (r c) -> p r c", c=D),
                        ps_sum[h][:, :].rearrange("p (r c) -> p r c", c=D),
                        g.bn_all[:, :].unsqueeze(1).broadcast_to([P, 4, D]), ALU.add).then_inc(bias_added[h], 1)

            with dve.Fori(0, g.BLOCKS // 2) as i:
                body(i, 0)
                body(i, 1)
            body(g.BLOCKS // 2, 0)
            dve.wait_ge(earlier_ready, 3)
            dve.tensor_copy(spare[:, :], spare_i[:, :]).then_inc(spare_ready, 1)
            dve.wait_ge(spare_ready, 1)
            dve.tensor_scalar(shift[:, :, :], g.dst_col[:, :, :], -1.0, spare[:, 0:1], ALU.mult,
                              ALU.add).then_inc(spare_ready, 1)
            dve.wait_ge(spare_ready, 2)
            dve.wait_ge(counted[1], g.BLOCKS)
            dve.scalar_tensor_tensor(out=moved[:, :, :], in0=repeats[:, :, :], scalar=1.0, in1=shift[:, :, :],
                                     op0=ALU.min, op1=ALU.mult).then_inc(spare_ready, 1)
            dve.wait_ge(spare_ready, 3)
            dve.tensor_tensor(g.scatter_rows[:, :, :], moved[:, :, :], g.dst_col[:, :, :], ALU.add)

        @block.gpsimd
        def _(pool):
            pool.memset(ones[:, :], 1.0).then_inc(earlier_ready, 1)
            pool.wait_ge(earlier_ready, 1)
            pool.affine_select(out=earlier[:, :], in_=ones[:, :], compare_op=ALU.is_gt, fill=0.0, base=0,
                               pattern=[[-1, P]], channel_multiplier=1).then_inc(earlier_ready, 1)
            pool.iota(spare_i[:, :], pattern=[[0, 1]], base=g.N, channel_multiplier=1).then_inc(earlier_ready, 1)

            def store(i, b):
                n = i * 2 + b
                for h in range(2):
                    pool.wait_ge(bias_added[h], n + 1)
                gate(g, pool)
                pool.dma_start(rows_of(g.sums, n * BLOCK), new_sums[b][:, :]).then_inc(sums_stored[b], 16)

            with pool.Fori(0, g.BLOCKS // 2) as i:
                store(i, 0)
                store(i, 1)
            store(g.BLOCKS // 2, 0)
            for b in range(2):
                pool.wait_ge(sums_stored[b], 16 * ((g.BLOCKS + 1 - b) // 2))
    nc.clear_and_free_semaphores(sems)
    nc.all_engine_barrier()


def update_nodes(g, s, k):
    nc = g.nc
    n0 = k * g.BLOCKS
    slot0 = [k * ((g.BLOCKS + 1 - b) // 2) for b in range(2)]
    with ExitStack() as ctx:
        def sb(name, shape):
            return ctx.enter_context(nc.sbuf_tensor(f"{name}_u{k}", shape, F32))

        sums_in = [sb(f"sums_in{b}", [P, BLOCK]) for b in range(2)]
        h_out = [sb(f"h_out{b}", [P, BLOCK]) for b in range(2)]
        turned = [sb(f"turned{h}", [P, HALF]) for h in range(2)]
        new_sums = [sb(f"new_sums{b}", [P, BLOCK]) for b in range(2)]
        ps_turn = [ctx.enter_context(nc.psum_tensor(f"ps_turn_u{k}{h}", [P, 512], F32)) for h in range(2)]
        ps_sum = [ctx.enter_context(nc.psum_tensor(f"ps_sum_u{k}{h}", [P, 512], F32)) for h in range(2)]
        block = ctx.enter_context(nc.Block())

        def over_blocks(eng, body):
            with eng.Fori(0, g.BLOCKS // 2) as i:
                body(i * 2, i, 0)
                body(i * 2 + 1, i, 1)
            body(g.BLOCKS - 1, g.BLOCKS // 2, 0)

        @block.sync
        def _(sp):
            def load(n, i, b):
                sp.wait_ge(s["rectified"][b], i + slot0[b])
                gate(g, sp)
                sp.dma_start(sums_in[b][:, :], rows_of(g.sums, n * BLOCK)).then_inc(s["sums_loaded"][b], 16)

            over_blocks(sp, load)

        @block.scalar
        def _(act):
            def body(n, i, b):
                act.wait_ge(s["sums_loaded"][b], (i + slot0[b]) * 16 + 16)
                act.wait_ge(s["h_stored"][b], (i + slot0[b]) * 16)
                act.activation(h_out[b][:, :], sums_in[b][:, :], ACT.Relu).then_inc(s["rectified"][b], 1)
                for h in range(2):
                    act.wait_ge(s["h_turned"][h], n + n0 + 1)
                    act.copy(turned[h][:, :], ps_turn[h][:, :]).then_inc(s["h_copied"][h], 1)

            over_blocks(act, body)

        @block.tensor
        def _(pe):
            def body(n, i, b):
                pe.wait_ge(s["rectified"][b], i + slot0[b] + 1)
                for h in range(2):
                    pe.wait_ge(s["h_copied"][h], n + n0)
                    for r in range(4):
                        at = (4 * h + r) * D
                        mm = pe.transpose(ps_turn[h][:, r * P:(r + 1) * P], h_out[b][:, at:at + D], g.ident[:, :])
                    mm.then_inc(s["h_turned"][h], 1)
                for h in range(2):
                    pe.wait_ge(s["h_copied"][h], n + n0 + 1)
                    pe.wait_ge(s["sum_ready"][h], n + n0)
                    for r in range(4):
                        mm = pe.matmul(ps_sum[h][:, r * D:(r + 1) * D], turned[h][:, r * P:(r + 1) * P],
                                       g.Wna_sb[:, :], start=True, stop=True)
                    mm.then_inc(s["h_projected"][h], 1)

            over_blocks(pe, body)

        @block.vector
        def _(dve):
            def body(n, i, b):
                for h in range(2):
                    dve.wait_ge(s["h_projected"][h], n + n0 + 1)
                    dve.wait_ge(s["sums_stored"][b], (i + slot0[b]) * 16)
                    dve.tensor_tensor(
                        new_sums[b][:, h * HALF:(h + 1) * HALF].rearrange("p (r c) -> p r c", c=D),
                        ps_sum[h][:, :].rearrange("p (r c) -> p r c", c=D),
                        g.bn_all[:, :].unsqueeze(1).broadcast_to([P, 4, D]), ALU.add).then_inc(s["sum_ready"][h], 1)

            over_blocks(dve, body)

        @block.gpsimd
        def _(pool):
            def store(n, i, b):
                pool.wait_ge(s["rectified"][b], i + slot0[b] + 1)
                gate(g, pool)
                pool.dma_start(rows_of(g.h_table, n * BLOCK), h_out[b][:, :]).then_inc(s["h_stored"][b], 16)
                for h in range(2):
                    pool.wait_ge(s["sum_ready"][h], n + n0 + 1)
                gate(g, pool)
                pool.dma_start(rows_of(g.sums, n * BLOCK), new_sums[b][:, :]).then_inc(s["sums_stored"][b], 16)

            over_blocks(pool, store)
            for b in range(2):
                done = 16 * (slot0[b] + (g.BLOCKS + 1 - b) // 2)
                pool.wait_ge(s["h_stored"][b], done)
                pool.wait_ge(s["sums_stored"][b], done)


def gather_and_scatter(g, s, pool, runs, gathers, scatter, n_pairs):
    def rows(table, index):
        return dict(in_=table, in_offset=bass.IndirectOffsetOnAxis(ap=index, axis=0))

    def gather(b, j):
        for into, table, index in gathers(b, j):
            pool.indirect_dma_start(out=into, out_offset=None, **rows(table, index)).then_inc(s["gathered"][b], 16)

    def scatter_tile(i, b, j):
        if j:
            pool.wait_ge(s["scattered"][b], (i + runs) * 16 * TILES + 16 * j)
        else:
            pool.wait_ge(s["scattered"][1 - b], (i + runs + b) * 16 * TILES)
        gate(g, pool)
        table, index, rows_in = scatter(b, j)
        pool.indirect_dma_start(out=table, out_offset=bass.IndirectOffsetOnAxis(ap=index, axis=0),
                                in_=rows_in, in_offset=None, compute_op=ALU.add).then_inc(s["scattered"][b], 16)

    def step(i, with_scatter):
        for b in range(2):
            pool.wait_ge(s["numbers_ready"][b], i + runs + runs // n_pairs + 1)
            gate(g, pool)
            for j in range(TILES):
                gather(b, j)
                if with_scatter:
                    if j == 0:
                        pool.wait_ge(s["result_ready"][b], i + runs)
                        gate(g, pool)
                    scatter_tile(i - 1, b, j)

    step(0, False)
    with pool.Fori(1, n_pairs) as i:
        step(i, True)
    for b in range(2):
        pool.wait_ge(s["result_ready"][b], n_pairs + runs)
        gate(g, pool)
        for j in range(TILES):
            scatter_tile(n_pairs - 1, b, j)
    for b in range(2):
        pool.wait_ge(s["scattered"][b], 16 * TILES * (n_pairs + runs))


def pass_messages(g, s, k, table, zeros=None):
    nc = g.nc
    PAIRS = g.GROUPS // 2
    runs = k * PAIRS
    with ExitStack() as ctx:
        def sb(name, shape, dt=F32):
            return ctx.enter_context(nc.sbuf_tensor(f"{name}_m{k}", shape, dt))

        def ps(name):
            return ctx.enter_context(nc.psum_tensor(f"{name}_m{k}", [P, 512], F32))

        gathered = [[sb(f"gathered{b}{e}", [P, TILES, D]) for e in range(2)] for b in range(2)]
        numbers = [sb(f"numbers{b}", [P, 2 * TILES], I32) for b in range(2)]
        targets_to = [sb(f"targets_to{b}", [P, TILES], I32) for b in range(2)]
        turned = [sb(f"turned{e}", [P, GROUP]) for e in range(2)]
        hidden = [sb(f"hidden{m}", [P, GROUP]) for m in range(2)]
        messages = sb("messages", [P, TILES, D])
        result = [sb(f"result{b}", [P, TILES, D]) for b in range(2)]
        targets = [sb(f"targets{b}", [P, GROUP], I32) for b in range(2)]
        same = [sb(f"same{b}", [P, TILES, P]) for b in range(2)]
        ps_turn = [ps(f"ps_turn{e}") for e in range(2)]
        ps_hidden = [ps(f"ps_hidden{m}") for m in range(2)]
        ps_msg = ps("ps_msg")
        ps_sum = ps("ps_sum")
        block = ctx.enter_context(nc.Block())

        @block.gpsimd
        def _(pool):
            gather_and_scatter(
                g, s, pool, runs,
                lambda b, j: [(gathered[b][e][:, j, :], table, numbers[b][:, e * TILES + j:e * TILES + j + 1])
                              for e in range(2)],
                lambda b, j: (g.sums[:, :], targets_to[b][:, j:j + 1], result[b][:, j, :]), PAIRS)

        @block.sync
        def _(sp):
            with sp.Fori(0, PAIRS) as i:
                for b in range(2):
                    sp.wait_ge(s["same_ready"][b], i + runs)
                    gate(g, sp)
                    sp.dma_start(targets[b][:, :], g.dst_padded[bass.ds(i * 2 * GROUP + b * GROUP, GROUP)]
                                 .partition_broadcast(P)).then_inc(s["targets_loaded"][b], 16)
                    if zeros is not None:
                        sp.dma_start(rows_of(g.attn_sums, i * 2 * GROUP + b * GROUP, GROUP, TILES),
                                     zeros).then_inc(s["zeros_stored"], 16)
            if zeros is not None:
                sp.wait_ge(s["zeros_stored"], 16 * g.GROUPS)

        @block.tensor
        def _(pe):
            with pe.Fori(0, PAIRS) as i:
                for b in range(2):
                    n = (i + runs) * 2 + b
                    pe.wait_ge(s["gathered"][b], (i + runs) * 128 + 128)
                    for e in range(2):
                        pe.wait_ge(s["turn_copied"][e], n)
                        for j in range(TILES):
                            mm = pe.transpose(ps_turn[e][:, j * P:(j + 1) * P], gathered[b][e][:, j, :],
                                              g.ident[:, :])
                        mm.then_inc(s["ends_turned"][e], 1)
                    for e in range(2):
                        pe.wait_ge(s["turn_copied"][e], n + 1)
                    for m in range(2):
                        pe.wait_ge(s["hidden_ready"][m], n)
                        for e in range(2):
                            mm = pe.matmul(ps_hidden[m][:, :], g.Wm1_sb[:, e, m * D:(m + 1) * D], turned[e][:, :],
                                           start=(e == 0), stop=(e == 1))
                        mm.then_inc(s["hidden_summed"][m], 1)
                    for m in range(2):
                        pe.wait_ge(s["hidden_ready"][m], n + 1)
                    pe.wait_ge(s["messages_ready"], n)
                    for j in range(TILES):
                        for m in range(2):
                            mm = pe.matmul(ps_msg[:, j * D:(j + 1) * D], hidden[m][:, j * P:(j + 1) * P],
                                           g.Wm2n_sb[:, m, :], start=(m == 0), stop=(m == 1))
                    mm.then_inc(s["messages_summed"], 1)
                    pe.wait_ge(s["messages_ready"], n + 1)
                    pe.wait_ge(s["same_ready"][b], i + runs + 1)
                    pe.wait_ge(s["result_ready"][1 - b], i + runs + b)
                    for j in range(TILES):
                        mm = pe.matmul(ps_sum[:, j * D:(j + 1) * D], same[b][:, j, :], messages[:, j, :],
                                       start=True, stop=True)
                    mm.then_inc(s["combined"], 1)

        @block.scalar
        def _(act):
            for b in range(2):
                act.copy(numbers[b][:, :], g.gather_rows[:, b, :]).then_inc(s["numbers_ready"][b], 1)
            with act.Fori(0, PAIRS) as i:
                for b in range(2):
                    n = (i + runs) * 2 + b
                    act.wait_ge(s["ends_turned"][0], n + 1)
                    act.copy(turned[0][:, :], ps_turn[0][:, :]).then_inc(s["turn_copied"][0], 1)
                    act.wait_ge(s["ends_turned"][1], n + 1)
                    act.copy(numbers[b][:, :], g.gather_rows[:, bass.ds(i * 2 + (b + 2), 1), :]
                             .rearrange("p a t -> p (a t)")).then_inc(s["numbers_ready"][b], 1)
                    act.wait_ge(s["hidden_summed"][0], n + 1)
                    act.activation(hidden[0][:, :], ps_hidden[0][:, :], ACT.Relu,
                                   bias=g.bm1_col[:, 0:1]).then_inc(s["hidden_ready"][0], 1)
                    act.wait_ge(s["scattered"][b], (i + runs) * 16 * TILES)
                    act.copy(targets_to[b][:, :], g.scatter_rows[:, bass.ds(i * 2 + b, 1), :]
                             .rearrange("p a t -> p (a t)"))
                    act.wait_ge(s["combined"], n + 1)
                    act.copy(result[b][:, :, :].rearrange("p j c -> p (j c)"),
                             ps_sum[:, :]).then_inc(s["result_ready"][b], 1)

        @block.vector
        def _(dve):
            with dve.Fori(0, PAIRS) as i:
                for b in range(2):
                    n = (i + runs) * 2 + b
                    dve.wait_ge(s["targets_loaded"][b], (i + runs) * 16 + 16)
                    dve.wait_ge(s["result_ready"][b], i + runs)
                    dve.tensor_tensor(same[b][:, :, :], targets[b][:, :].rearrange("p (q j) -> p j q", j=TILES),
                                      g.dst_col[:, bass.ds(i * 2 + b, 1), :].rearrange("p a t -> p (a t)")
                                      .unsqueeze(2).broadcast_to([P, TILES, P]),
                                      ALU.is_equal).then_inc(s["same_ready"][b], 1)
                    dve.wait_ge(s["ends_turned"][1], n + 1)
                    dve.tensor_copy(turned[1][:, :], ps_turn[1][:, :]).then_inc(s["turn_copied"][1], 1)
                    dve.wait_ge(s["hidden_summed"][1], n + 1)
                    dve.tensor_scalar(hidden[1][:, :], ps_hidden[1][:, :], g.bm1_col[:, 1:2], 0.0, ALU.add,
                                      ALU.max).then_inc(s["hidden_ready"][1], 1)
                    dve.wait_ge(s["messages_summed"], n + 1)
                    dve.tensor_tensor(messages[:, :, :], ps_msg[:, :].rearrange("p (j c) -> p j c", c=D),
                                      g.bm2n_all[:, :].unsqueeze(1).broadcast_to([P, TILES, D]),
                                      ALU.add).then_inc(s["messages_ready"], 1)


def over_blocks(g, eng, body):
    with eng.Fori(0, g.BLOCKS // 2) as i:
        body(i * 2, i, 0, False)
        body(i * 2 + 1, i, 1, False)
    body(g.BLOCKS - 1, g.BLOCKS // 2, 0, True)


def row_statistics(g, dve, s, total, stats, moments, n):
    for r in range(ROWS):
        last = dve.bn_stats(stats[:, r, :], total[:, r * D:(r + 1) * D])
    last.then_inc(s["row_stats"], 1)
    dve.wait_ge(s["row_stats"], n + 1)
    gate(g, dve)
    for r in range(ROWS):
        last = dve.bn_aggr(moments[:, r, :], stats[:, r, :])
    last.then_inc(s["row_moments"], 1)


def finish_messages(g, s):
    nc = g.nc
    with ExitStack() as ctx:
        def sb(name, shape, dt=F32):
            return ctx.enter_context(nc.sbuf_tensor(f"{name}_f", shape, dt))

        def ps(name, n=512):
            return ctx.enter_context(nc.psum_tensor(f"{name}_f", [P, n], F32))

        sums_in = [sb(f"sums_in{b}", [P, BLOCK]) for b in range(2)]
        x_in = [sb(f"x_in{b}", [P, BLOCK]) for b in range(2)]
        total = sb("total", [P, BLOCK])
        stats = sb("stats", [P, ROWS, 6])
        moments = sb("moments", [P, ROWS, 2])
        inverse = sb("inverse", [P, ROWS, 1])
        x1 = [sb(f"x1{b}", [P, BLOCK]) for b in range(2)]
        turned = [sb(f"turned{h}", [P, HALF]) for h in range(2)]
        q_out = [sb(f"q_out{b}", [P, BLOCK]) for b in range(2)]
        kv_out = [sb(f"kv_out{b}", [P, 2 * BLOCK]) for b in range(2)]
        ps_turn = [ps(f"ps_turn{h}") for h in range(2)]
        ps_q = [ps(f"ps_q{h}") for h in range(2)]
        ps_kv = [ps(f"ps_kv{h}", 1024) for h in range(2)]
        pieces = parts_of(g.TAIL_PARTS)
        block = ctx.enter_context(nc.Block())

        @block.sync
        def _(sp):
            def load(n, i, b, last):
                sp.wait_ge(s["residual_added"][b], i)
                gate(g, sp)
                sp.dma_start(sums_in[b][:, :], rows_of(g.sums, n * BLOCK)).then_inc(s["sums_loaded"][b], 16)
                for a, z in pieces if last else [(0, P)]:
                    sp.dma_start(x_in[b][a:z, :], rows_of(g.x, n * BLOCK + a * ROWS, (z - a) * ROWS)
                                 ).then_inc(s["x_loaded"][b], 16)

            over_blocks(g, sp, load)

        @block.vector
        def _(dve):
            def body(n, i, b, last):
                dve.wait_ge(s["sums_loaded"][b], i * 16 + 16)
                dve.wait_ge(s["x_loaded"][b], i * 16 + 16 * (len(pieces) if last else 1))
                dve.wait_ge(s["normed"], n)
                dve.scalar_tensor_tensor(out=total[:, :], in0=sums_in[b][:, :], scalar=0.0, in1=x_in[b][:, :],
                                         op0=ALU.max, op1=ALU.add).then_inc(s["residual_added"][b], 1)
                dve.wait_ge(s["x1_stored"][b], i * 16)
                dve.wait_ge(s["x1_turned"][b][1], i)
                dve.wait_ge(s["residual_added"][b], i + 1)
                row_statistics(g, dve, s, total, stats, moments, n)
                dve.wait_ge(s["rooted"], n + 1)
                dve.reciprocal(inverse[:, :, :], inverse[:, :, :]).then_inc(s["inverted"], 1)
                dve.wait_ge(s["inverted"], n + 1)
                for r in range(ROWS):
                    row = slice(r * D, (r + 1) * D)
                    last_row = dve.tensor_scalar(x1[b][:, row], total[:, row], moments[:, r, 0:1],
                                                 inverse[:, r, :], ALU.subtract, ALU.mult)
                last_row.then_inc(s["normed"], 1)

            over_blocks(g, dve, body)

        @block.tensor
        def _(pe):
            def body(n, i, b, last):
                pe.wait_ge(s["normed"], n + 1)
                for h in range(2):
                    pe.wait_ge(s["x1_copied"][h], n)
                    for r in range(4):
                        at = (4 * h + r) * D
                        mm = pe.transpose(ps_turn[h][:, r * P:(r + 1) * P], x1[b][:, at:at + D], g.ident[:, :])
                    mm.then_inc(s["x1_turned"][b][h], 1)
                for h in range(2):
                    pe.wait_ge(s["x1_copied"][h], n + 1)
                    pe.wait_ge(s["q_copied"][h], n)
                    pe.wait_ge(s["kv_copied"][h], n)
                    for r in range(4):
                        lhs = turned[h][:, r * P:(r + 1) * P]
                        pe.matmul(ps_q[h][:, r * D:(r + 1) * D], lhs, g.Wqkv_sb[:, 0:D], start=True, stop=True)
                        mm = pe.matmul(ps_kv[h][:, r * 2 * D:(r + 1) * 2 * D], lhs, g.Wqkv_sb[:, D:3 * D],
                                       start=True, stop=True)
                    mm.then_inc(s["qkv_ready"][h], 1)

            over_blocks(g, pe, body)

        @block.scalar
        def _(act):
            def root(n):
                act.wait_ge(s["row_moments"], n + 1)
                act.wait_ge(s["normed"], n)
                act.activation(inverse[:, :, :], moments[:, :, 1:2], ACT.Sqrt,
                               bias=g.eps_col[:, 0:1]).then_inc(s["rooted"], 1)

            root(0)

            def body(n, i, b, last):
                for h in range(2):
                    act.wait_ge(s["x1_turned"][b][h], i + 1)
                    act.copy(turned[h][:, :], ps_turn[h][:, :]).then_inc(s["x1_copied"][h], 1)
                if not last:
                    root(n + 1)
                for h in range(2):
                    act.wait_ge(s["qkv_ready"][h], n + 1)
                    act.wait_ge(s["q_stored"][b], i * 16)
                    act.copy(q_out[b][:, h * HALF:(h + 1) * HALF], ps_q[h][:, :]).then_inc(s["q_copied"][h], 1)
                    act.wait_ge(s["kv_stored"][b], i * 16)
                    act.copy(kv_out[b][:, h * BLOCK:(h + 1) * BLOCK], ps_kv[h][:, :]).then_inc(s["kv_copied"][h], 1)

            over_blocks(g, act, body)

        @block.gpsimd
        def _(pool):
            def store(n, i, b, last):
                pool.wait_ge(s["normed"], n + 1)
                gate(g, pool)
                pool.dma_start(rows_of(g.x1_table, n * BLOCK), x1[b][:, :]).then_inc(s["x1_stored"][b], 16)
                for h in range(2):
                    pool.wait_ge(s["kv_copied"][h], n + 1)
                gate(g, pool)
                pool.dma_start(rows_of(g.q_table, n * BLOCK), q_out[b][:, :]).then_inc(s["q_stored"][b], 16)
                pool.dma_start(rows_of(g.kv_table, n * BLOCK), kv_out[b][:, :]).then_inc(s["kv_stored"][b], 16)

            over_blocks(g, pool, store)
            for b in range(2):
                done = 16 * ((g.BLOCKS + 1 - b) // 2)
                for name in ("x1_stored", "q_stored", "kv_stored"):
                    pool.wait_ge(s[name][b], done)


def attend(g, s):
    nc = g.nc
    PAIRS = g.GROUPS // 2
    with ExitStack() as ctx:
        def sb(name, shape, dt=F32):
            return ctx.enter_context(nc.sbuf_tensor(f"{name}_t", shape, dt))

        def ps(name, n=512):
            return ctx.enter_context(nc.psum_tensor(f"{name}_t", [P, n], F32))

        q_in = [sb(f"q_in{b}", [P, TILES, D]) for b in range(2)]
        kv_in = [sb(f"kv_in{b}", [P, TILES, 2 * D]) for b in range(2)]
        numbers = [sb(f"numbers{b}", [P, 2 * TILES], I32) for b in range(2)]
        targets_to = [sb(f"targets_to{b}", [P, TILES], I32) for b in range(2)]
        edges_in = [sb(f"edges_in{b}", [P, TILES, D]) for b in range(2)]
        turned = sb("turned", [P, GROUP])
        qk = sb("qk", [P, TILES, D])
        qke = sb("qke", [P, TILES, D])
        score = sb("score", [P, TILES * HEADS])
        low = sb("low", [P, TILES * HEADS])
        clipped = sb("clipped", [P, TILES * HEADS])
        messages = sb("messages", [P, TILES, AT])
        result = [sb(f"result{b}", [P, TILES, AT]) for b in range(2)]
        targets = [sb(f"targets{b}", [P, GROUP], I32) for b in range(2)]
        same = [sb(f"same{b}", [P, TILES, P]) for b in range(2)]
        ps_turn = ps("ps_turn")
        ps_edge = ps("ps_edge")
        ps_sum = [ps(f"ps_sum{u}") for u in range(2)]
        block = ctx.enter_context(nc.Block())

        @block.gpsimd
        def _(pool):
            gather_and_scatter(
                g, s, pool, 0,
                lambda b, j: [(kv_in[b][:, j, :], g.kv_table[:, :], numbers[b][:, j:j + 1]),
                              (q_in[b][:, j, :], g.q_table[:, :], numbers[b][:, TILES + j:TILES + j + 1])],
                lambda b, j: (g.attn_sums[:, :], targets_to[b][:, j:j + 1], result[b][:, j, :]), PAIRS)

        @block.sync
        def _(sp):
            def load(i, b, last=False):
                n = i * 2 + b
                sp.wait_ge(s["same_ready"][b], i)
                gate(g, sp)
                sp.dma_start(targets[b][:, :], g.dst_padded[bass.ds(n * GROUP, GROUP)]
                             .partition_broadcast(P)).then_inc(s["targets_loaded"][b], 16)
                sp.wait_ge(s["edges_turned"], i * 2)
                gate(g, sp)
                count = g.TAIL_EDGES if last else GROUP
                sp.dma_start(edges_in[b][0:count // TILES, :, :].rearrange("p j c -> p (j c)"),
                             rows_of(g.edge_attr_128, n * GROUP, count, TILES)).then_inc(s["edges_loaded"][b], 16)

            with sp.Fori(0, PAIRS - 1) as i:
                load(i, 0)
                load(i, 1)
            load(PAIRS - 1, 0)
            load(PAIRS - 1, 1, last=True)

        @block.tensor
        def _(pe):
            with pe.Fori(0, PAIRS) as i:
                for b in range(2):
                    n = i * 2 + b
                    pe.wait_ge(s["edges_loaded"][b], i * 16 + 16)
                    pe.wait_ge(s["edges_copied"], n)
                    for j in range(TILES):
                        mm = pe.transpose(ps_turn[:, j * P:(j + 1) * P], edges_in[b][:, j, :], g.ident[:, :])
                    mm.then_inc(s["edges_turned"], 1)
                    pe.wait_ge(s["edges_copied"], n + 1)
                    pe.wait_ge(s["edges_used"], n)
                    for j in range(TILES):
                        mm = pe.matmul(ps_edge[:, j * D:(j + 1) * D], turned[:, j * P:(j + 1) * P], g.WE_sb[:, :],
                                       start=True, stop=True)
                    mm.then_inc(s["edges_projected"], 1)
                    pe.wait_ge(s["values_weighted"], n + 1)
                    pe.wait_ge(s["same_ready"][b], i + 1)
                    pe.wait_ge(s["result_ready"][1 - b], i + b)
                    for j in range(TILES):
                        at = (j % 2) * AT
                        mm = pe.matmul(ps_sum[j // 2][:, at:at + AT], same[b][:, j, :], messages[:, j, :],
                                       start=True, stop=True)
                    mm.then_inc(s["combined"], 1)

        @block.scalar
        def _(act):
            for b in range(2):
                act.copy(numbers[b][:, :], g.gather_rows[:, b, :]).then_inc(s["numbers_ready"][b], 1)
            with act.Fori(0, PAIRS) as i:
                for b in range(2):
                    n = i * 2 + b
                    act.wait_ge(s["edges_turned"], n + 1)
                    act.copy(turned[:, :], ps_turn[:, :]).then_inc(s["edges_copied"], 1)
                    act.wait_ge(s["clipped"], n + 1)
                    act.wait_ge(s["combined"], n)
                    act.activation(messages[:, :, D:AT], clipped[:, :].rearrange("p (j h) -> p j h", h=HEADS),
                                   ACT.Exp).then_inc(s["weights_ready"], 1)
                    act.wait_ge(s["values_weighted"], n + 1)
                    act.copy(numbers[b][:, :], g.gather_rows[:, bass.ds(i * 2 + (b + 2), 1), :]
                             .rearrange("p a t -> p (a t)")).then_inc(s["numbers_ready"][b], 1)
                    act.wait_ge(s["scattered"][b], i * 16 * TILES)
                    act.copy(targets_to[b][:, :], g.scatter_rows[:, bass.ds(i * 2 + b, 1), :]
                             .rearrange("p a t -> p (a t)"))
                    act.wait_ge(s["combined"], n + 1)
                    for u in range(2):
                        last = act.copy(result[b][:, 2 * u:2 * u + 2, :].rearrange("p j c -> p (j c)"),
                                        ps_sum[u][:, 0:2 * AT])
                    last.then_inc(s["result_ready"][b], 1)

        @block.vector
        def _(dve):
            with dve.Fori(0, PAIRS) as i:
                for b in range(2):
                    n = i * 2 + b
                    dve.wait_ge(s["targets_loaded"][b], i * 16 + 16)
                    dve.wait_ge(s["result_ready"][b], i)
                    dve.tensor_tensor(same[b][:, :, :], targets[b][:, :].rearrange("p (q j) -> p j q", j=TILES),
                                      g.dst_col[:, bass.ds(i * 2 + b, 1), :].rearrange("p a t -> p (a t)")
                                      .unsqueeze(2).broadcast_to([P, TILES, P]),
                                      ALU.is_equal).then_inc(s["same_ready"][b], 1)
                    dve.wait_ge(s["gathered"][b], i * 128 + 128)
                    dve.wait_ge(s["edges_used"], n)
                    dve.tensor_tensor(qk[:, :, :], q_in[b][:, :, :], kv_in[b][:, :, 0:D],
                                      ALU.mult).then_inc(s["multiplied"], 1)
                    dve.wait_ge(s["multiplied"], n + 1)
                    dve.wait_ge(s["edges_projected"], n + 1)
                    dve.wait_ge(s["scored"], n)
                    dve.tensor_tensor(qke[:, :, :], qk[:, :, :], ps_edge[:, :].rearrange("p (j c) -> p j c", c=D),
                                      ALU.mult).then_inc(s["edges_used"], 1)
                    dve.wait_ge(s["edges_used"], n + 1)
                    dve.wait_ge(s["scaled"], n)
                    dve.tensor_reduce(score[:, :], qke[:, :, :].rearrange("p j (h c) -> p (j h) c", h=HEADS),
                                      AX.X, ALU.add).then_inc(s["scored"], 1)
                    dve.wait_ge(s["scored"], n + 1)
                    dve.wait_ge(s["clipped"], n)
                    dve.tensor_scalar(low[:, :], score[:, :], DH ** -0.5, CLIP, ALU.mult,
                                      ALU.min).then_inc(s["scaled"], 1)
                    dve.wait_ge(s["scaled"], n + 1)
                    dve.wait_ge(s["weights_ready"], n)
                    dve.tensor_scalar(clipped[:, :], low[:, :], -CLIP, None, ALU.max).then_inc(s["clipped"], 1)
                    dve.wait_ge(s["weights_ready"], n + 1)
                    dve.tensor_tensor(
                        messages[:, :, 0:D].rearrange("p j (h c) -> p j h c", h=HEADS),
                        kv_in[b][:, :, D:2 * D].rearrange("p j (h c) -> p j h c", h=HEADS),
                        messages[:, :, D:AT].unsqueeze(3).broadcast_to([P, TILES, HEADS, DH]),
                        ALU.mult).then_inc(s["values_weighted"], 1)


def measure(g, dve, turned, n, h, last):
    half = turned[:, h * HALF:(h + 1) * HALF]
    if last:
        half = half.rearrange("p (r q) -> p r q", q=P)[:, :, 0:g.TAIL_PARTS]
    return dve.bn_stats(g.feature_stats[:, bass.ds(n * 2 + h, 1), :].rearrange("p a k -> p (a k)"), half)


def finish_attention(g, s):
    nc = g.nc
    with ExitStack() as ctx:
        def sb(name, shape, dt=F32):
            return ctx.enter_context(nc.sbuf_tensor(f"{name}_y", shape, dt))

        sums_in = [sb(f"sums_in{b}", [P, ROWS * AT]) for b in range(2)]
        x1_in = [sb(f"x1_in{b}", [P, BLOCK]) for b in range(2)]
        weight = sb("weight", [P, ROWS, HEADS])
        inverse = sb("inverse", [P, ROWS, HEADS])
        mean_v = sb("mean_v", [P, BLOCK])
        y = [sb(f"y{b}", [P, BLOCK]) for b in range(2)]
        turned = [sb(f"turned{b}", [P, BLOCK]) for b in range(2)]
        ps_turn = [ctx.enter_context(nc.psum_tensor(f"ps_turn_y{h}", [P, 512], F32)) for h in range(2)]
        block = ctx.enter_context(nc.Block())

        @block.sync
        def _(sp):
            def load(n, i, b, last):
                sp.wait_ge(s["y_summed"][b], i)
                gate(g, sp)
                sp.dma_start(sums_in[b][:, :], rows_of(g.attn_sums, n * BLOCK)).then_inc(s["sums_loaded"][b], 16)
                sp.dma_start(x1_in[b][:, :], rows_of(g.x1_table, n * BLOCK)).then_inc(s["x1_loaded"][b], 16)

            over_blocks(g, sp, load)

        @block.vector
        def _(dve):
            def body(n, i, b):
                rows = sums_in[b][:, :].rearrange("p (r c) -> p r c", c=AT)
                dve.wait_ge(s["sums_loaded"][b], i * 16 + 16)
                dve.wait_ge(s["mean_ready"], n)
                dve.tensor_scalar(weight[:, :, :], rows[:, :, D:AT], ATTN_EPS, None,
                                  ALU.add).then_inc(s["weights_summed"], 1)
                dve.wait_ge(s["weights_summed"], n + 1)
                dve.reciprocal(inverse[:, :, :], weight[:, :, :]).then_inc(s["inverted"], 1)
                dve.wait_ge(s["inverted"], n + 1)
                dve.wait_ge(s["y_summed"][1 - b], i + b)
                dve.tensor_tensor(mean_v[:, :].rearrange("p (r h c) -> p r h c", r=ROWS, h=HEADS),
                                  rows[:, :, 0:D].rearrange("p r (h c) -> p r h c", h=HEADS),
                                  inverse[:, :, :].unsqueeze(3).broadcast_to([P, ROWS, HEADS, DH]),
                                  ALU.mult).then_inc(s["mean_ready"], 1)
                dve.wait_ge(s["mean_ready"], n + 1)
                dve.wait_ge(s["x1_loaded"][b], i * 16 + 16)
                dve.wait_ge(s["y_turned"][b][1], i)
                dve.tensor_tensor(y[b][:, :], mean_v[:, :], x1_in[b][:, :], ALU.add).then_inc(s["y_summed"][b], 1)

            def measure_block(n, i, b, last=False):
                for h in range(2):
                    dve.wait_ge(s["y_copied"][h], n + 1)
                    measured = measure(g, dve, turned[b], n, h, last)
                measured.then_inc(s["measured"][b], 1)

            body(0, 0, 0)
            with dve.Fori(0, g.BLOCKS // 2) as i:
                body(i * 2 + 1, i, 1)
                measure_block(i * 2, i, 0)
                body(i * 2 + 2, i + 1, 0)
                measure_block(i * 2 + 1, i, 1)
            measure_block(g.BLOCKS - 1, g.BLOCKS // 2, 0, last=True)

        @block.tensor
        def _(pe):
            def body(n, i, b, last):
                pe.wait_ge(s["y_summed"][b], i + 1)
                for h in range(2):
                    pe.wait_ge(s["y_copied"][h], n)
                    for r in range(4):
                        at = (4 * h + r) * D
                        mm = pe.transpose(ps_turn[h][:, r * P:(r + 1) * P], y[b][:, at:at + D], g.ident[:, :])
                    mm.then_inc(s["y_turned"][b][h], 1)

            over_blocks(g, pe, body)

        @block.scalar
        def _(act):
            def body(n, i, b, last):
                for h in range(2):
                    act.wait_ge(s["y_turned"][b][h], i + 1)
                    act.wait_ge(s["y_stored"][b], i * 16)
                    act.wait_ge(s["measured"][b], i)
                    act.copy(turned[b][:, h * HALF:(h + 1) * HALF], ps_turn[h][:, :]).then_inc(s["y_copied"][h], 1)

            over_blocks(g, act, body)

        @block.gpsimd
        def _(pool):
            def store(n, i, b, last):
                for h in range(2):
                    pool.wait_ge(s["y_copied"][h], n + 1)
                gate(g, pool)
                pool.dma_start(g.turned_table[bass.ds(n * P, P), :], turned[b][:, :]).then_inc(s["y_stored"][b], 16)

            over_blocks(g, pool, store)
            for b in range(2):
                pool.wait_ge(s["y_stored"][b], 16 * ((g.BLOCKS + 1 - b) // 2))


def batch_norm_coefficients(g, dve, act, s, which, moments, scale, shift):
    if act is not None:
        act.wait_ge(s["bn_step"], 1)
        act.activation(scale[:, :], moments[:, 1:2], ACT.Sqrt, bias=g.eps_col[:, 0:1]).then_inc(s["bn_step"], 1)
        return
    gamma, beta = g.gammas[:, which:which + 1], g.betas[:, which:which + 1]
    dve.bn_aggr(moments[:, :], g.feature_stats[:, :, :].rearrange("p a k -> p (a k)")).then_inc(s["bn_step"], 1)
    dve.wait_ge(s["bn_step"], 2)
    dve.reciprocal(scale[:, :], scale[:, :]).then_inc(s["bn_step"], 1)
    dve.wait_ge(s["bn_step"], 3)
    dve.tensor_tensor(scale[:, :], scale[:, :], gamma, ALU.mult).then_inc(s["bn_step"], 1)
    dve.wait_ge(s["bn_step"], 4)
    dve.tensor_tensor(shift[:, :], moments[:, 0:1], scale[:, :], ALU.mult).then_inc(s["bn_step"], 1)
    dve.wait_ge(s["bn_step"], 5)
    dve.tensor_tensor(shift[:, :], beta, shift[:, :], ALU.subtract).then_inc(s["bn_step"], 1)


def feed_forward(g, s):
    nc = g.nc
    with ExitStack() as ctx:
        def sb(name, shape, dt=F32):
            return ctx.enter_context(nc.sbuf_tensor(f"{name}_z", shape, dt))

        def ps(name):
            return ctx.enter_context(nc.psum_tensor(f"{name}_z", [P, 512], F32))

        moments = sb("moments", [P, 2])
        scale = sb("scale", [P, 1])
        shift = sb("shift", [P, 1])
        y_in = [sb(f"y_in{b}", [P, BLOCK]) for b in range(2)]
        h_in = [sb(f"h_in{b}", [P, BLOCK]) for b in range(2)]
        hidden = [[sb(f"hidden{h}{m}", [P, HALF]) for m in range(2)] for h in range(2)]
        z = [sb(f"z{b}", [P, BLOCK]) for b in range(2)]
        ps_hidden = [[ps(f"ps_hidden{h}{m}") for m in range(2)] for h in range(2)]
        ps_out = [ps(f"ps_out{h}") for h in range(2)]
        block = ctx.enter_context(nc.Block())

        @block.sync
        def _(sp):
            def load(n, i, b, last):
                sp.wait_ge(s["y_normed"][b], i)
                gate(g, sp)
                sp.dma_start(y_in[b][:, :], g.turned_table[bass.ds(n * P, P), :]).then_inc(s["y_loaded"][b], 16)

            over_blocks(g, sp, load)

        @block.scalar
        def _(act):
            batch_norm_coefficients(g, None, act, s, 0, moments, scale, shift)
            act.wait_ge(s["bn_step"], 6)

            def body(n, i, b, last):
                act.wait_ge(s["y_loaded"][b], i * 16 + 16)
                act.wait_ge(s["z_measured"][b], i)
                act.activation(h_in[b][:, :], y_in[b][:, :], ACT.Identity, bias=shift[:, 0:1],
                               scale=scale[:, 0:1]).then_inc(s["y_normed"][b], 1)
                for h in range(2):
                    act.wait_ge(s["ff_hidden"][h], n + 1)
                    act.activation(hidden[h][0][:, :], ps_hidden[h][0][:, :], ACT.Relu,
                                   bias=g.b1_col[:, 0:1]).then_inc(s["ff_rectified0"][h], 1)

            over_blocks(g, act, body)

        @block.tensor
        def _(pe):
            def body(n, i, b, last):
                pe.wait_ge(s["y_normed"][b], i + 1)
                for h in range(2):
                    pe.wait_ge(s["ff_rectified0"][h], n)
                    pe.wait_ge(s["ff_rectified1"][h], n)
                    for m in range(2):
                        mm = pe.matmul(ps_hidden[h][m][:, :], g.W1_sb[:, m * D:(m + 1) * D],
                                       h_in[b][:, h * HALF:(h + 1) * HALF], start=True, stop=True)
                    mm.then_inc(s["ff_hidden"][h], 1)
                for h in range(2):
                    pe.wait_ge(s["ff_rectified0"][h], n + 1)
                    pe.wait_ge(s["ff_rectified1"][h], n + 1)
                    pe.wait_ge(s["z_ready"][h], n)
                    for m in range(2):
                        mm = pe.matmul(ps_out[h][:, :], g.W2_sb[:, m, :], hidden[h][m][:, :],
                                       start=(m == 0), stop=(m == 1))
                    mm.then_inc(s["ff_out"][h], 1)

            over_blocks(g, pe, body)

        @block.vector
        def _(dve):
            batch_norm_coefficients(g, dve, None, s, 0, moments, scale, shift)

            def body(n, i, b, last):
                for h in range(2):
                    dve.wait_ge(s["ff_hidden"][h], n + 1)
                    dve.tensor_scalar(hidden[h][1][:, :], ps_hidden[h][1][:, :], g.b1_col[:, 1:2], 0.0, ALU.add,
                                      ALU.max).then_inc(s["ff_rectified1"][h], 1)
                for h in range(2):
                    dve.wait_ge(s["ff_out"][h], n + 1)
                    dve.wait_ge(s["z_stored"][b], i * 16)
                    cols = slice(h * HALF, (h + 1) * HALF)
                    dve.scalar_tensor_tensor(out=z[b][:, cols], in0=ps_out[h][:, :], scalar=g.b2_col[:, 0:1],
                                             in1=h_in[b][:, cols], op0=ALU.add,
                                             op1=ALU.add).then_inc(s["z_ready"][h], 1)
                for h in range(2):
                    dve.wait_ge(s["z_ready"][h], n + 1)
                    measured = measure(g, dve, z[b], n, h, last)
                measured.then_inc(s["z_measured"][b], 1)

            over_blocks(g, dve, body)

        @block.gpsimd
        def _(pool):
            def store(n, i, b, last):
                for h in range(2):
                    pool.wait_ge(s["z_ready"][h], n + 1)
                gate(g, pool)
                pool.dma_start(g.turned_table[bass.ds(n * P, P), :], z[b][:, :]).then_inc(s["z_stored"][b], 16)

            over_blocks(g, pool, store)
            for b in range(2):
                pool.wait_ge(s["z_stored"][b], 16 * ((g.BLOCKS + 1 - b) // 2))


def finish_output(g, s):
    nc = g.nc
    with ExitStack() as ctx:
        def sb(name, shape, dt=F32):
            return ctx.enter_context(nc.sbuf_tensor(f"{name}_o", shape, dt))

        moments = sb("bn_moments", [P, 2])
        scale = sb("scale", [P, 1])
        shift = sb("shift", [P, 1])
        z_in = [sb(f"z_in{b}", [P, BLOCK]) for b in range(2)]
        x1_in = [sb(f"x1_in{b}", [P, BLOCK]) for b in range(2)]
        normed = [sb(f"normed{b}", [P, BLOCK]) for b in range(2)]
        total = [sb(f"total{b}", [P, BLOCK]) for b in range(2)]
        stats = sb("stats", [P, ROWS, 6])
        row_moments = sb("moments", [P, ROWS, 2])
        root = sb("root", [P, ROWS, 1])
        inverse = sb("inverse", [P, ROWS, 1])
        minus_mean = sb("minus_mean", [P, ROWS, 1])
        rows_out = [sb(f"rows_out{b}", [P, BLOCK]) for b in range(2)]
        ps_turn = [ctx.enter_context(nc.psum_tensor(f"ps_turn_o{h}", [P, 512], F32)) for h in range(2)]
        pieces = parts_of(g.TAIL_PARTS)
        block = ctx.enter_context(nc.Block())

        @block.sync
        def _(sp):
            def load(n, i, b, last):
                sp.wait_ge(s["z_normed"][b], i)
                gate(g, sp)
                sp.dma_start(z_in[b][:, :], g.turned_table[bass.ds(n * P, P), :]).then_inc(s["z_loaded"][b], 16)
                sp.wait_ge(s["residual_added"][b], i)
                gate(g, sp)
                sp.dma_start(x1_in[b][:, :], rows_of(g.x1_table, n * BLOCK)).then_inc(s["x1_loaded"][b], 16)

            over_blocks(g, sp, load)

        @block.scalar
        def _(act):
            batch_norm_coefficients(g, None, act, s, 1, moments, scale, shift)
            act.wait_ge(s["bn_step"], 6)

            def norm(i, b):
                act.wait_ge(s["z_loaded"][b], i * 16 + 16)
                act.wait_ge(s["residual_added"][b], i)
                act.activation(normed[b][:, :], z_in[b][:, :], ACT.Identity, bias=shift[:, 0:1],
                               scale=scale[:, 0:1]).then_inc(s["z_normed"][b], 1)

            norm(0, 0)

            def body(n, i, b, last):
                if not last:
                    norm(i + b, 1 - b)
                act.wait_ge(s["row_moments"], n + 1)
                act.wait_ge(s["normed"][1 - b], i + b)
                act.activation(root[:, :, :], row_moments[:, :, 1:2], ACT.Sqrt,
                               bias=g.eps_col[:, 0:1]).then_inc(s["rooted"], 1)
                act.wait_ge(s["shifts_ready"], n + 1)
                act.wait_ge(s["out_stored"][b], i * 16)
                for r in range(ROWS):
                    row = slice(r * D, (r + 1) * D)
                    last_row = act.activation(rows_out[b][:, row], total[b][:, row], ACT.Identity,
                                              bias=minus_mean[:, r, :], scale=inverse[:, r, :])
                last_row.then_inc(s["normed"][b], 1)

            over_blocks(g, act, body)

        @block.tensor
        def _(pe):
            def body(n, i, b, last):
                pe.wait_ge(s["z_normed"][b], i + 1)
                pe.wait_ge(s["residual_added"][1 - b], i + b)
                for h in range(2):
                    for r in range(4):
                        at = (4 * h + r) * D
                        mm = pe.transpose(ps_turn[h][:, r * D:(r + 1) * D], normed[b][:, at:at + D], g.ident[:, :])
                mm.then_inc(s["z_turned"], 1)

            over_blocks(g, pe, body)

        @block.vector
        def _(dve):
            batch_norm_coefficients(g, dve, None, s, 1, moments, scale, shift)

            def body(n, i, b, last):
                dve.wait_ge(s["z_turned"], n + 1)
                dve.wait_ge(s["x1_loaded"][b], i * 16 + 16)
                dve.wait_ge(s["shifts_ready"], n)
                dve.wait_ge(s["normed"][b], i)
                for h in range(2):
                    cols = slice(h * HALF, (h + 1) * HALF)
                    add = dve.tensor_tensor(total[b][:, cols], ps_turn[h][:, :], x1_in[b][:, cols], ALU.add)
                add.then_inc(s["residual_added"][b], 1)
                dve.wait_ge(s["residual_added"][b], i + 1)
                row_statistics(g, dve, s, total[b], stats, row_moments, n)
                dve.wait_ge(s["rooted"], n + 1)
                dve.reciprocal(inverse[:, :, :], root[:, :, :]).then_inc(s["inverted"], 1)
                dve.wait_ge(s["inverted"], n + 1)
                dve.scalar_tensor_tensor(out=minus_mean[:, :, :], in0=row_moments[:, :, 0:1], scalar=-1.0,
                                         in1=inverse[:, :, :], op0=ALU.mult,
                                         op1=ALU.mult).then_inc(s["shifts_ready"], 1)

            over_blocks(g, dve, body)

        @block.gpsimd
        def _(pool):
            def store(n, i, b, last):
                pool.wait_ge(s["normed"][b], i + 1)
                gate(g, pool)
                for a, z in pieces if last else [(0, P)]:
                    pool.dma_start(rows_of(g.out, n * BLOCK + a * ROWS, (z - a) * ROWS), rows_out[b][a:z, :]
                                   ).then_inc(s["out_stored"][b], 16)

            over_blocks(g, pool, store)
            pool.wait_ge(s["out_stored"][0], 16 * (g.BLOCKS // 2 + len(pieces)))
            pool.wait_ge(s["out_stored"][1], 16 * (g.BLOCKS // 2))


def gnn_then_transformer(nc, **args):
    with ExitStack() as ctx:
        g = Graph(nc, ctx, args)

        def sems(prefix, pairs="", singles="", quads=""):
            made = {n: [ctx.enter_context(nc.semaphore(f"{prefix}_{n}{b}")) for b in range(2)] for n in pairs.split()}
            made |= {n: [[ctx.enter_context(nc.semaphore(f"{prefix}_{n}{b}{h}")) for h in range(2)] for b in range(2)]
                     for n in quads.split()}
            return made | {n: ctx.enter_context(nc.semaphore(f"{prefix}_{n}")) for n in singles.split()}

        setup(g)
        start_sums(g)
        messages = sems("m", "gathered scattered numbers_ready result_ready same_ready targets_loaded turn_copied "
                             "ends_turned hidden_ready hidden_summed",
                        "messages_ready messages_summed combined zeros_stored")
        nodes = sems("u", "rectified sums_loaded h_stored h_turned h_copied sum_ready h_projected sums_stored")
        with nc.sbuf_tensor("zeros", [P, TILES * AT], F32) as zeros:
            with nc.Block() as block:
                @block.vector
                def _(dve):
                    dve.memset(zeros[:, :], 0.0)
            pass_messages(g, messages, 0, g.x, zeros[:, :])
        for k in range(1, 3):
            update_nodes(g, nodes, k - 1)
            pass_messages(g, messages, k, g.h_table[:, :])
        finish_messages(g, sems("f", "sums_loaded x_loaded x1_stored x1_copied residual_added q_copied kv_copied "
                                     "qkv_ready q_stored kv_stored",
                                "row_stats row_moments rooted inverted normed", "x1_turned"))
        attend(g, sems("t", "gathered scattered numbers_ready result_ready same_ready targets_loaded edges_loaded",
                       "edges_turned edges_copied edges_used edges_projected values_weighted combined clipped "
                       "weights_ready multiplied scored scaled"))
        finish_attention(g, sems("y", "sums_loaded x1_loaded y_copied y_stored y_summed measured",
                                 "mean_ready weights_summed inverted", "y_turned"))
        feed_forward(g, sems("z", "y_loaded y_normed ff_hidden ff_rectified0 ff_rectified1 z_ready ff_out z_stored z_measured",
                             "bn_step"))
        finish_output(g, sems("o", "z_loaded x1_loaded z_normed out_stored residual_added normed",
                              "bn_step z_turned row_stats row_moments rooted inverted shifts_ready"))


_INS = ['x', 'src', 'dst', 'edge_attr_128', 'L0_gnn_Wm1', 'L0_gnn_bm1', 'L0_gnn_Wm2', 'L0_gnn_bm2', 'L0_gnn_Wn',
        'L0_gnn_bn', 'L1_gnn_WQ', 'L1_gnn_WK', 'L1_gnn_WV', 'L1_gnn_WE', 'L1_gnn_gamma1', 'L1_gnn_beta1',
        'L1_gnn_gamma2', 'L1_gnn_beta2', 'L1_gnn_W1', 'L1_gnn_b1', 'L1_gnn_W2', 'L1_gnn_b2']


def kernel(**inputs):
    import numpy as _np
    import concourse.bacc as _bacc
    from concourse import mybir as _mybir
    from concourse.bass_utils import run_bass_kernel_spmd as _run

    nc = _bacc.Bacc("TRN2", target_bir_lowering=False, num_devices=1)
    arrays, args = {}, {}
    for name in _INS:
        a = _np.ascontiguousarray(inputs[name])
        arrays[f"in_{name}_dram"] = a
        args[name] = nc.dram_tensor(f"in_{name}_dram", a.shape, _mybir.dt.from_np(a.dtype),
                                    kind="ExternalInput").ap()
    args["out"] = nc.dram_tensor("out_dram", inputs["x"].shape, _mybir.dt.float32, kind="ExternalOutput").ap()
    gnn_then_transformer(nc, **args)
    r = _run(nc, [arrays], core_ids=[0])
    return r.results[0]["out_dram"]
```

```python
from contextlib import ExitStack

import concourse.bass as bass
from concourse import mybir

F32 = mybir.dt.float32
I32 = mybir.dt.int32
ALU = mybir.AluOpType
ACT = mybir.ActivationFunctionType
AX = mybir.AxisListType

P = 128
D = 128
ROWS = 8
BLOCK = P * ROWS
HALF = BLOCK // 2
TILES = 4
GROUP = P * TILES
CHUNKS = 3
WINDOW = P * CHUNKS
HEADS = 8
DH = D // HEADS
AT = D + HEADS
LN_EPS = 1e-5
BN_EPS = 1e-5
ATTN_EPS = 1e-6
CLIP = 5.0


def rows_of(table, first, n=BLOCK, rows=ROWS):
    return table[bass.ds(first, n), :].rearrange("(p r) c -> p (r c)", r=rows)


def parts_of(n):
    whole = n - n % 16
    return [(a, b) for a, b in ((0, whole), (whole, n)) if b > a]


def gate(g, eng):
    eng.sem_inc(g.gates[eng.engine], 1)


class Graph:

    def __init__(self, nc, ctx, args):
        self.nc = nc
        self.x = args["x"]
        self.src = args["src"]
        self.dst = args["dst"]
        self.edge_attr_128 = args["edge_attr_128"]
        self.L0_gnn_Wm1 = args["L0_gnn_Wm1"]
        self.L0_gnn_bm1 = args["L0_gnn_bm1"]
        self.L0_gnn_Wm2 = args["L0_gnn_Wm2"]
        self.L0_gnn_bm2 = args["L0_gnn_bm2"]
        self.L0_gnn_Wn = args["L0_gnn_Wn"]
        self.L0_gnn_bn = args["L0_gnn_bn"]
        self.L1_gnn_WQ = args["L1_gnn_WQ"]
        self.L1_gnn_WK = args["L1_gnn_WK"]
        self.L1_gnn_WV = args["L1_gnn_WV"]
        self.L1_gnn_WE = args["L1_gnn_WE"]
        self.L1_gnn_gamma1 = args["L1_gnn_gamma1"]
        self.L1_gnn_beta1 = args["L1_gnn_beta1"]
        self.L1_gnn_gamma2 = args["L1_gnn_gamma2"]
        self.L1_gnn_beta2 = args["L1_gnn_beta2"]
        self.L1_gnn_W1 = args["L1_gnn_W1"]
        self.L1_gnn_b1 = args["L1_gnn_b1"]
        self.L1_gnn_W2 = args["L1_gnn_W2"]
        self.L1_gnn_b2 = args["L1_gnn_b2"]
        self.out = args["out"]
        self.N = self.x.shape[0]
        self.E = self.src.shape[0]
        self.BLOCKS = -(-self.N // BLOCK)
        self.GROUPS = -(-self.E // GROUP)
        self.NP = self.BLOCKS * BLOCK
        self.EP = self.GROUPS * GROUP
        self.QUARTER = self.GROUPS * P
        self.TAIL_PARTS = (self.N - (self.BLOCKS - 1) * BLOCK) // ROWS
        self.TAIL_EDGES = self.E - 3 * self.QUARTER - (self.GROUPS - 2) * P
        self.FILL_ROW = self.N
        self.SPARE_ROWS = self.NP
        assert self.N % ROWS == 0 and self.BLOCKS % 2 == 1 and self.BLOCKS > 2
        assert self.GROUPS == 2 * self.BLOCKS and 0 < self.TAIL_EDGES < P
        assert self.FILL_ROW < self.NP and self.N >= WINDOW

        def dram(name, shape, dt=F32):
            return nc.dram_tensor(name, shape, dt)

        self.gates = {eng.engine: ctx.enter_context(nc.semaphore(f"gate{n}"))
                      for n, eng in enumerate((nc.gpsimd, nc.sync, nc.vector))}
        self.h_table = dram("h_table", (self.NP, D))
        self.sums = dram("sums", (self.NP + GROUP, D))
        self.attn_sums = dram("attn_sums", (self.NP + GROUP, AT))
        self.x1_table = dram("x1_table", (self.NP, D))
        self.q_table = dram("q_table", (self.NP, D))
        self.kv_table = dram("kv_table", (self.NP, 2 * D))
        self.turned_table = dram("turned_table", (self.BLOCKS * P, BLOCK))
        self.offset_table = dram("offset_table", (self.EP,), I32)
        self.base_table = dram("base_table", (self.GROUPS * TILES,), I32)

        def sb(name, shape, dt=F32):
            return ctx.enter_context(nc.sbuf_tensor(name, shape, dt))

        self.ident = sb("ident", [P, P])
        self.Wm1_sb = sb("Wm1_sb", [P, 2, 2 * D])
        self.Wm2n_sb = sb("Wm2n_sb", [P, 2, D])
        self.Wna_sb = sb("Wna_sb", [P, D])
        self.Wqkv_sb = sb("Wqkv_sb", [P, 3 * D])
        self.WE_sb = sb("WE_sb", [P, D])
        self.W1_sb = sb("W1_sb", [P, 2 * D])
        self.W2_sb = sb("W2_sb", [P, 2, D])
        self.bm1_col = sb("bm1_col", [P, 2])
        self.b1_col = sb("b1_col", [P, 2])
        self.b2_col = sb("b2_col", [P, 1])
        self.bn_all = sb("bn_all", [P, D])
        self.bm2n_all = sb("bm2n_all", [P, D])
        self.gammas = sb("gammas", [P, 2])
        self.betas = sb("betas", [P, 2])
        self.eps_col = sb("eps_col", [P, 1])
        self.gather_rows = sb("gather_rows", [P, self.GROUPS + 2, 2 * TILES], I32)
        self.scatter_rows = sb("scatter_rows", [P, self.GROUPS, TILES], I32)
        self.dst_col = sb("dst_col", [P, self.GROUPS, TILES])
        self.offset_col = sb("offset_col", [P, self.GROUPS, TILES])
        self.bases = sb("bases", [1, self.GROUPS * TILES], I32)
        self.windowed = sb("windowed", [1, 1], I32)
        self.window_row = sb("window_row", [P, CHUNKS])
        self.feature_stats = sb("feature_stats", [P, self.GROUPS, 6])


def setup(g):
    nc = g.nc
    G = g.GROUPS
    with ExitStack() as ctx:
        def sb(name, shape, dt=F32):
            return ctx.enter_context(nc.sbuf_tensor(name, shape, dt))

        sems = []

        def sem(name):
            sems.append(nc.alloc_semaphore(name))
            return sems[-1]

        Wm2_rows = sb("Wm2_rows", [P, 2, D])
        Wm2_turned = sb("Wm2_turned", [P, 2 * D])
        Wnb = sb("Wnb", [P, D])
        bm2_col = sb("bm2_col", [P, 1])
        bm2_wide = sb("bm2_wide", [P, P])
        ones = sb("ones", [P, P])
        edge_rows = sb("edge_rows", [P, 2, GROUP], I32)
        edge_rows_f = sb("edge_rows_f", [P, 2, GROUP])
        base_rows = sb("base_rows", [P, TILES])
        base_rows_i = sb("base_rows_i", [P, TILES], I32)
        offsets = sb("offsets", [P, GROUP])
        offsets_i = sb("offsets_i", [P, GROUP], I32)
        beyond = sb("beyond", [P, GROUP])
        outside = sb("outside", [P, GROUP])
        outside_real = sb("outside_real", [P, GROUP])
        misses = sb("misses", [P, 1])
        highest = sb("highest", [P, TILES])
        lowest = sb("lowest", [P, TILES])
        crossed = sb("crossed", [P, TILES - 1])
        crossings = sb("crossings", [P, 1])
        window_row_i = sb("window_row_i", [P, CHUNKS], I32)
        clipped = sb("clipped", [P, TILES, G])
        ps_offsets = ctx.enter_context(nc.psum_tensor("ps_offsets", [P, TILES, P], F32))
        ps_misses = ctx.enter_context(nc.psum_tensor("ps_misses", [P, 1], F32))
        ps_edges = ctx.enter_context(nc.psum_tensor("ps_edges", [P, 2, TILES, P], F32))
        ps_turn = ctx.enter_context(nc.psum_tensor("ps_turn", [P, 512], F32))
        ps_fold = ctx.enter_context(nc.psum_tensor("ps_fold", [P, 512], F32))

        filled = sem("filled")
        ones_ready = sem("ones_ready")
        ident_ready = sem("ident_ready")
        ends_loaded = sem("ends_loaded")
        window_rows_made = sem("window_rows_made")
        bases_ready = sem("bases_ready")
        offsets_ready = sem("offsets_ready")
        offsets_written = sem("offsets_written")
        bases_written = sem("bases_written")
        bases_loaded = sem("bases_loaded")
        misses_ready = sem("misses_ready")
        misses_summed = sem("misses_summed")
        weights_loaded = sem("weights_loaded")
        ends_converted = sem("ends_converted")
        ends_turned = sem("ends_turned")
        dst_clipped = sem("dst_clipped")
        rows_ready = sem("rows_ready")
        wm2_turned = sem("wm2_turned")
        fold_inputs = sem("fold_inputs")
        folded = sem("folded")
        fold_copied = sem("fold_copied")
        block = ctx.enter_context(nc.Block())

        def column(v):
            return v.rearrange("(a p) -> p a", p=P)

        loads = [
            (Wm2_rows[:, :, :], g.L0_gnn_Wm2.rearrange("(a p) n -> p a n", p=P)),
            (Wnb[:, :], g.L0_gnn_Wn[D:2 * D, :]),
            (bm2_col[:, :], column(g.L0_gnn_bm2)),
            (g.Wna_sb[:, :], g.L0_gnn_Wn[0:D, :]),
            (g.Wm1_sb[:, :, :], g.L0_gnn_Wm1.rearrange("(a p) n -> p a n", p=P)),
            (g.bm1_col[:, :], column(g.L0_gnn_bm1)),
            (g.bn_all[:, :], g.L0_gnn_bn.partition_broadcast(P)),
            (g.Wqkv_sb[:, 0:D], g.L1_gnn_WQ),
            (g.Wqkv_sb[:, D:2 * D], g.L1_gnn_WK),
            (g.Wqkv_sb[:, 2 * D:3 * D], g.L1_gnn_WV),
            (g.WE_sb[:, :], g.L1_gnn_WE),
            (g.W1_sb[:, :], g.L1_gnn_W1),
            (g.W2_sb[:, :, :], g.L1_gnn_W2.rearrange("(a p) n -> p a n", p=P)),
            (g.b1_col[:, :], column(g.L1_gnn_b1)),
            (g.b2_col[:, :], column(g.L1_gnn_b2)),
            (g.gammas[:, 0:1], column(g.L1_gnn_gamma1)),
            (g.gammas[:, 1:2], column(g.L1_gnn_gamma2)),
            (g.betas[:, 0:1], column(g.L1_gnn_beta1)),
            (g.betas[:, 1:2], column(g.L1_gnn_beta2)),
        ]

        @block.sync
        def _(sp):
            sp.wait_ge(filled, 2)
            for k, ends in enumerate((g.src, g.dst)):
                sp.dma_start(edge_rows[0:G, k, 0:3 * P].rearrange("g (j q) -> g j q", q=P),
                             ends[0:3 * g.QUARTER].rearrange("(j g q) -> g j q", j=3, q=P)
                             ).then_inc(ends_loaded, 16)
                sp.dma_start(edge_rows[0:G - 2, k, 3 * P:GROUP],
                             ends[3 * g.QUARTER:g.E - g.TAIL_EDGES].rearrange("(g q) -> g q", q=P)
                             ).then_inc(ends_loaded, 16)
                sp.dma_start(edge_rows[G - 2:G - 1, k, 3 * P:3 * P + g.TAIL_EDGES],
                             ends[g.E - g.TAIL_EDGES:g.E].rearrange("(g q) -> g q", g=1)
                             ).then_inc(ends_loaded, 16)
            sp.wait_ge(offsets_ready, 2)
            gate(g, sp)
            sp.dma_start(g.offset_table.rearrange("(g e) -> g e", e=GROUP), offsets_i[0:G, :]
                         ).then_inc(offsets_written, 16)
            sp.wait_ge(bases_ready, 2)
            gate(g, sp)
            sp.dma_start(g.base_table.rearrange("(g j) -> g j", j=TILES), base_rows_i[0:G, :]
                         ).then_inc(bases_written, 16)
            sp.wait_ge(bases_written, 16)
            gate(g, sp)
            sp.dma_start(g.bases[:, :], g.base_table.rearrange("(a t) -> a t", a=1)).then_inc(bases_loaded, 16)
            sp.wait_ge(offsets_written, 16)
            sp.wait_ge(bases_loaded, 16)

        @block.gpsimd
        def _(pool):
            pool.memset(ones[:, :], 1.0).then_inc(ones_ready, 1)
            pool.wait_ge(ones_ready, 1)
            pool.affine_select(out=g.ident[:, :], in_=ones[:, :], compare_op=ALU.is_equal, fill=0.0, base=0,
                               pattern=[[-1, P]], channel_multiplier=1).then_inc(ident_ready, 1)
            pool.iota(window_row_i[:, :], pattern=[[1, CHUNKS]], base=0,
                      channel_multiplier=CHUNKS).then_inc(window_rows_made, 1)

        @block.scalar
        def _(act):
            for to, of in loads:
                act.dma_start(to, of, allow_slow_non_contiguous=True).then_inc(weights_loaded, 16)
            act.wait_ge(weights_loaded, 16 * len(loads))
            act.wait_ge(ones_ready, 1)
            act.activation(bm2_wide[:, :], ones[:, :], ACT.Copy, scale=bm2_col[:, 0:1]).then_inc(fold_inputs, 1)
            act.wait_ge(wm2_turned, 1)
            act.copy(Wm2_turned[:, :], ps_turn[:, 0:2 * D]).then_inc(fold_inputs, 1)

        @block.tensor
        def _(pe):
            pe.wait_ge(ident_ready, 1)
            pe.wait_ge(ends_converted, 1)
            for k in range(2):
                for j in range(TILES):
                    last = pe.transpose(ps_edges[:, k, j, 0:G], edge_rows_f[0:G, k, j * P:(j + 1) * P],
                                        g.ident[0:G, 0:G])
            last.then_inc(ends_turned, 1)
            pe.wait_ge(offsets_ready, 1)
            for j in range(TILES):
                last = pe.transpose(ps_offsets[:, j, 0:G], offsets[0:G, j * P:(j + 1) * P], g.ident[0:G, 0:G])
            last.then_inc(ends_turned, 1)
            pe.wait_ge(misses_ready, 6)
            pe.matmul(ps_misses[0:1, 0:1], misses[0:G, :], ones[0:G, 0:1], start=True, stop=False)
            pe.matmul(ps_misses[0:1, 0:1], crossings[0:G, :], ones[0:G, 0:1], start=False,
                      stop=True).then_inc(misses_summed, 1)
            pe.wait_ge(weights_loaded, 16 * len(loads))
            for m in range(2):
                last = pe.transpose(ps_turn[:, m * D:(m + 1) * D], Wm2_rows[:, m, :], g.ident[:, :])
            last.then_inc(wm2_turned, 1)
            pe.wait_ge(fold_inputs, 2)
            for m in range(2):
                pe.matmul(ps_fold[:, m * D:(m + 1) * D], Wm2_turned[:, m * D:(m + 1) * D], Wnb[:, :],
                          start=True, stop=True)
            pe.matmul(ps_fold[:, 2 * D:3 * D], bm2_wide[:, :], Wnb[:, :], start=True, stop=True).then_inc(folded, 1)

        @block.vector
        def _(dve):
            dve.memset(edge_rows[:, 0, :], 0).then_inc(filled, 1)
            dve.memset(edge_rows[:, 1, :], g.FILL_ROW).then_inc(filled, 1)
            dve.memset(g.eps_col[:, :], LN_EPS)
            dve.memset(g.gather_rows[:, :, :], 0).then_inc(rows_ready, 1)
            dve.wait_ge(ends_loaded, 96)
            dve.tensor_copy(edge_rows_f[0:G, :, :], edge_rows[0:G, :, :]).then_inc(ends_converted, 1)
            dve.wait_ge(ends_converted, 1)
            dve.tensor_scalar(base_rows[0:G, :], edge_rows_f[0:G, 1, 0:GROUP:P], float(g.N - WINDOW), None,
                              ALU.min).then_inc(bases_ready, 1)
            dve.wait_ge(bases_ready, 1)
            dve.tensor_copy(base_rows_i[0:G, :], base_rows[0:G, :]).then_inc(bases_ready, 1)
            dve.tensor_tensor(offsets[0:G, :].rearrange("p (j q) -> p j q", q=P),
                              edge_rows_f[0:G, 1, :].rearrange("p (j q) -> p j q", q=P),
                              base_rows[0:G, :].unsqueeze(2).broadcast_to([G, TILES, P]),
                              ALU.subtract).then_inc(offsets_ready, 1)
            dve.wait_ge(offsets_ready, 1)
            dve.tensor_copy(offsets_i[0:G, :], offsets[0:G, :]).then_inc(offsets_ready, 1)
            dve.tensor_scalar(beyond[0:G, :], offsets[0:G, :], float(WINDOW - 1), None,
                              ALU.is_gt).then_inc(misses_ready, 1)
            dve.wait_ge(misses_ready, 1)
            dve.scalar_tensor_tensor(out=outside[0:G, :], in0=offsets[0:G, :], scalar=0.0, in1=beyond[0:G, :],
                                     op0=ALU.is_lt, op1=ALU.max).then_inc(misses_ready, 1)
            dve.wait_ge(misses_ready, 2)
            dve.scalar_tensor_tensor(out=outside_real[0:G, :], in0=edge_rows_f[0:G, 1, :],
                                     scalar=float(g.FILL_ROW), in1=outside[0:G, :], op0=ALU.is_lt, op1=ALU.mult,
                                     accum_out=misses[0:G, :]).then_inc(misses_ready, 1)
            by_edge = edge_rows_f[0:G, 1, :].rearrange("p (j q) -> p j q", q=P)
            dve.tensor_reduce(highest[0:G, :], by_edge, AX.X, ALU.max).then_inc(misses_ready, 1)
            dve.tensor_reduce(lowest[0:G, :], by_edge, AX.X, ALU.min).then_inc(misses_ready, 1)
            dve.wait_ge(misses_ready, 5)
            dve.scalar_tensor_tensor(out=crossed[0:G, :], in0=highest[0:G, 0:TILES - 1], scalar=1.0,
                                     in1=lowest[0:G, 1:TILES], op0=ALU.mult, op1=ALU.is_ge,
                                     accum_out=crossings[0:G, :]).then_inc(misses_ready, 1)
            dve.wait_ge(misses_summed, 1)
            dve.tensor_scalar(g.windowed[:, :], ps_misses[0:1, 0:1], 0.0, None, ALU.is_equal)
            dve.wait_ge(window_rows_made, 1)
            dve.tensor_copy(g.window_row[:, :], window_row_i[:, :])
            dve.wait_ge(ends_turned, 2)
            dve.tensor_copy(g.offset_col[:, :, :].rearrange("p g t -> p t g"), ps_offsets[:, :, 0:G])
            dve.wait_ge(rows_ready, 1)
            by_tile = g.gather_rows[:, 0:G, :].rearrange("p g t -> p t g")
            dve.tensor_copy(by_tile[:, 0:TILES, :], ps_edges[:, 0, :, 0:G])
            dve.tensor_copy(g.dst_col[:, :, :].rearrange("p g t -> p t g"), ps_edges[:, 1, :, 0:G])
            dve.tensor_scalar(clipped[:, :, :], ps_edges[:, 1, :, 0:G], float(g.N - 1), None,
                              ALU.min).then_inc(dst_clipped, 1)
            dve.wait_ge(dst_clipped, 1)
            dve.tensor_copy(by_tile[:, TILES:2 * TILES, :], clipped[:, :, :])
            dve.wait_ge(folded, 1)
            dve.tensor_copy(g.Wm2n_sb[:, :, :], ps_fold[:, 0:2 * D].rearrange("p (a n) -> p a n", a=2))
            dve.tensor_copy(g.bm2n_all[:, :], ps_fold[:, 2 * D:3 * D]).then_inc(fold_copied, 1)
    nc.clear_and_free_semaphores(sems)
    nc.all_engine_barrier()


def start_sums(g):
    nc = g.nc
    with ExitStack() as ctx:
        def sb(name, shape, dt=F32):
            return ctx.enter_context(nc.sbuf_tensor(name, shape, dt))

        sems = []

        def sem(name):
            sems.append(nc.alloc_semaphore(name))
            return sems[-1]

        x_in = [sb(f"x_in{b}", [P, BLOCK]) for b in range(2)]
        turned = [sb(f"turned{h}", [P, HALF]) for h in range(2)]
        new_sums = [sb(f"new_sums{b}", [P, BLOCK]) for b in range(2)]
        offsets = [sb(f"offsets{h}", [P, GROUP], I32) for h in range(2)]
        earlier = sb("earlier", [P, P])
        ones = sb("ones_a", [P, P])
        spare_i = sb("spare_i", [P, TILES], I32)
        spare = sb("spare", [P, TILES])
        matches = sb("matches", [P, TILES, P])
        repeats = sb("repeats", [P, g.GROUPS, TILES])
        shift = sb("shift", [P, g.GROUPS, TILES])
        moved = sb("moved", [P, g.GROUPS, TILES])
        ps_turn = [ctx.enter_context(nc.psum_tensor(f"ps_turn_a{h}", [P, 512], F32)) for h in range(2)]
        ps_sum = [ctx.enter_context(nc.psum_tensor(f"ps_sum_a{h}", [P, 512], F32)) for h in range(2)]

        x_loaded = [sem(f"x_loaded{b}") for b in range(2)]
        x_turned = [[sem(f"x_turned{b}{h}") for h in range(2)] for b in range(2)]
        x_copied = [sem(f"x_copied{h}") for h in range(2)]
        projected = [sem(f"projected{h}") for h in range(2)]
        bias_added = [sem(f"bias_added{h}") for h in range(2)]
        sums_stored = [sem(f"sums_stored{b}") for b in range(2)]
        offsets_loaded = [sem(f"offsets_loaded{h}") for h in range(2)]
        counted = [sem(f"counted{h}") for h in range(2)]
        earlier_ready = sem("earlier_ready")
        spare_ready = sem("spare_ready")
        pieces = parts_of(g.TAIL_PARTS)
        block = ctx.enter_context(nc.Block())

        @block.sync
        def _(sp):
            def load(i, b, last=False):
                n = i * 2 + b
                sp.wait_ge(x_turned[b][1], i)
                gate(g, sp)
                if last:
                    for a, z in pieces:
                        sp.dma_start(x_in[b][a:z, :], rows_of(g.x, n * BLOCK + a * ROWS, (z - a) * ROWS)
                                     ).then_inc(x_loaded[b], 16)
                else:
                    sp.dma_start(x_in[b][:, :], rows_of(g.x, n * BLOCK)).then_inc(x_loaded[b], 16)
                for h in range(2):
                    sp.wait_ge(counted[h], n)
                    gate(g, sp)
                    sp.dma_start(offsets[h][:, :], g.offset_table[bass.ds(n * BLOCK + h * GROUP, GROUP)]
                                 .partition_broadcast(P)).then_inc(offsets_loaded[h], 16)

            with sp.Fori(0, g.BLOCKS // 2) as i:
                load(i, 0)
                load(i, 1)
            load(g.BLOCKS // 2, 0, last=True)

        @block.tensor
        def _(pe):
            def body(i, b, last=False):
                n = i * 2 + b
                pe.wait_ge(x_loaded[b], i * 16 + 16 * (len(pieces) if last else 1))
                for h in range(2):
                    pe.wait_ge(x_copied[h], n)
                    for r in range(4):
                        at = (4 * h + r) * D
                        mm = pe.transpose(ps_turn[h][:, r * P:(r + 1) * P], x_in[b][:, at:at + D], g.ident[:, :])
                    mm.then_inc(x_turned[b][h], 1)
                for h in range(2):
                    pe.wait_ge(x_copied[h], n + 1)
                    pe.wait_ge(bias_added[h], n)
                    for r in range(4):
                        mm = pe.matmul(ps_sum[h][:, r * D:(r + 1) * D], turned[h][:, r * P:(r + 1) * P],
                                       g.Wna_sb[:, :], start=True, stop=True)
                    mm.then_inc(projected[h], 1)

            with pe.Fori(0, g.BLOCKS // 2) as i:
                body(i, 0)
                body(i, 1)
            body(g.BLOCKS // 2, 0, last=True)

        @block.scalar
        def _(act):
            def body(i, b):
                n = i * 2 + b
                for h in range(2):
                    act.wait_ge(x_turned[b][h], i + 1)
                    act.copy(turned[h][:, :], ps_turn[h][:, :]).then_inc(x_copied[h], 1)

            with act.Fori(0, g.BLOCKS // 2) as i:
                body(i, 0)
                body(i, 1)
            body(g.BLOCKS // 2, 0)

        @block.vector
        def _(dve):
            dve.wait_ge(earlier_ready, 2)

            def body(i, b):
                n = i * 2 + b
                for h in range(2):
                    dve.wait_ge(offsets_loaded[h], n * 16 + 16)
                    dve.wait_ge(counted[1 - h], n + h)
                    for j in range(TILES):
                        at = dve.scalar_tensor_tensor(
                            out=matches[:, j, :], in0=offsets[h][:, j * P:(j + 1) * P],
                            scalar=g.offset_col[:, bass.ds(n * 2 + h, 1), j], in1=earlier[:, :],
                            op0=ALU.is_equal, op1=ALU.mult, accum_out=repeats[:, bass.ds(n * 2 + h, 1), j])
                    at.then_inc(counted[h], 1)
                    dve.wait_ge(projected[h], n + 1)
                    dve.wait_ge(sums_stored[b], i * 16)
                    dve.tensor_tensor(
                        new_sums[b][:, h * HALF:(h + 1) * HALF].rearrange("p (r c) -> p r c", c=D),
                        ps_sum[h][:, :].rearrange("p (r c) -> p r c", c=D),
                        g.bn_all[:, :].unsqueeze(1).broadcast_to([P, 4, D]), ALU.add).then_inc(bias_added[h], 1)

            with dve.Fori(0, g.BLOCKS // 2) as i:
                body(i, 0)
                body(i, 1)
            body(g.BLOCKS // 2, 0)
            dve.wait_ge(earlier_ready, 3)
            dve.tensor_copy(spare[:, :], spare_i[:, :]).then_inc(spare_ready, 1)
            dve.wait_ge(spare_ready, 1)
            dve.tensor_tensor(shift[:, :, :], spare[:, :].unsqueeze(1).broadcast_to([P, g.GROUPS, TILES]),
                              g.dst_col[:, :, :], ALU.subtract).then_inc(spare_ready, 1)
            dve.wait_ge(spare_ready, 2)
            dve.wait_ge(counted[1], g.BLOCKS)
            dve.scalar_tensor_tensor(out=moved[:, :, :], in0=repeats[:, :, :], scalar=1.0, in1=shift[:, :, :],
                                     op0=ALU.min, op1=ALU.mult).then_inc(spare_ready, 1)
            dve.wait_ge(spare_ready, 3)
            dve.tensor_tensor(g.scatter_rows[:, :, :], moved[:, :, :], g.dst_col[:, :, :], ALU.add)

        @block.gpsimd
        def _(pool):
            pool.memset(ones[:, :], 1.0).then_inc(earlier_ready, 1)
            pool.wait_ge(earlier_ready, 1)
            pool.affine_select(out=earlier[:, :], in_=ones[:, :], compare_op=ALU.is_gt, fill=0.0, base=0,
                               pattern=[[-1, P]], channel_multiplier=1).then_inc(earlier_ready, 1)
            pool.iota(spare_i[:, :], pattern=[[P, TILES]], base=g.SPARE_ROWS, channel_multiplier=1).then_inc(earlier_ready, 1)

            def store(i, b):
                n = i * 2 + b
                for h in range(2):
                    pool.wait_ge(bias_added[h], n + 1)
                gate(g, pool)
                pool.dma_start(rows_of(g.sums, n * BLOCK), new_sums[b][:, :]).then_inc(sums_stored[b], 16)

            with pool.Fori(0, g.BLOCKS // 2) as i:
                store(i, 0)
                store(i, 1)
            store(g.BLOCKS // 2, 0)
            for b in range(2):
                pool.wait_ge(sums_stored[b], 16 * ((g.BLOCKS + 1 - b) // 2))
    nc.clear_and_free_semaphores(sems)
    nc.all_engine_barrier()


def update_nodes(g, s, k):
    nc = g.nc
    n0 = k * g.BLOCKS
    slot0 = [k * ((g.BLOCKS + 1 - b) // 2) for b in range(2)]
    with ExitStack() as ctx:
        def sb(name, shape):
            return ctx.enter_context(nc.sbuf_tensor(f"{name}_u{k}", shape, F32))

        sums_in = [sb(f"sums_in{b}", [P, BLOCK]) for b in range(2)]
        h_out = [sb(f"h_out{b}", [P, BLOCK]) for b in range(2)]
        turned = [sb(f"turned{h}", [P, HALF]) for h in range(2)]
        new_sums = [sb(f"new_sums{b}", [P, BLOCK]) for b in range(2)]
        ps_turn = [ctx.enter_context(nc.psum_tensor(f"ps_turn_u{k}{h}", [P, 512], F32)) for h in range(2)]
        ps_sum = [ctx.enter_context(nc.psum_tensor(f"ps_sum_u{k}{h}", [P, 512], F32)) for h in range(2)]
        block = ctx.enter_context(nc.Block())

        def over_blocks(eng, body):
            with eng.Fori(0, g.BLOCKS // 2) as i:
                body(i * 2, i, 0)
                body(i * 2 + 1, i, 1)
            body(g.BLOCKS - 1, g.BLOCKS // 2, 0)

        @block.sync
        def _(sp):
            def load(n, i, b):
                sp.wait_ge(s["rectified"][b], i + slot0[b])
                gate(g, sp)
                sp.dma_start(sums_in[b][:, :], rows_of(g.sums, n * BLOCK)).then_inc(s["sums_loaded"][b], 16)

            over_blocks(sp, load)

        @block.scalar
        def _(act):
            def body(n, i, b):
                act.wait_ge(s["sums_loaded"][b], (i + slot0[b]) * 16 + 16)
                act.wait_ge(s["h_stored"][b], (i + slot0[b]) * 16)
                act.activation(h_out[b][:, :], sums_in[b][:, :], ACT.Relu).then_inc(s["rectified"][b], 1)
                for h in range(2):
                    act.wait_ge(s["h_turned"][h], n + n0 + 1)
                    act.copy(turned[h][:, :], ps_turn[h][:, :]).then_inc(s["h_copied"][h], 1)

            over_blocks(act, body)

        @block.tensor
        def _(pe):
            def body(n, i, b):
                pe.wait_ge(s["rectified"][b], i + slot0[b] + 1)
                for h in range(2):
                    pe.wait_ge(s["h_copied"][h], n + n0)
                    for r in range(4):
                        at = (4 * h + r) * D
                        mm = pe.transpose(ps_turn[h][:, r * P:(r + 1) * P], h_out[b][:, at:at + D], g.ident[:, :])
                    mm.then_inc(s["h_turned"][h], 1)
                for h in range(2):
                    pe.wait_ge(s["h_copied"][h], n + n0 + 1)
                    pe.wait_ge(s["sum_ready"][h], n + n0)
                    for r in range(4):
                        mm = pe.matmul(ps_sum[h][:, r * D:(r + 1) * D], turned[h][:, r * P:(r + 1) * P],
                                       g.Wna_sb[:, :], start=True, stop=True)
                    mm.then_inc(s["h_projected"][h], 1)

            over_blocks(pe, body)

        @block.vector
        def _(dve):
            def body(n, i, b):
                for h in range(2):
                    dve.wait_ge(s["h_projected"][h], n + n0 + 1)
                    dve.wait_ge(s["sums_stored"][b], (i + slot0[b]) * 16)
                    dve.tensor_tensor(
                        new_sums[b][:, h * HALF:(h + 1) * HALF].rearrange("p (r c) -> p r c", c=D),
                        ps_sum[h][:, :].rearrange("p (r c) -> p r c", c=D),
                        g.bn_all[:, :].unsqueeze(1).broadcast_to([P, 4, D]), ALU.add).then_inc(s["sum_ready"][h], 1)

            over_blocks(dve, body)

        @block.gpsimd
        def _(pool):
            def store(n, i, b):
                pool.wait_ge(s["rectified"][b], i + slot0[b] + 1)
                gate(g, pool)
                pool.dma_start(rows_of(g.h_table, n * BLOCK), h_out[b][:, :]).then_inc(s["h_stored"][b], 16)
                for h in range(2):
                    pool.wait_ge(s["sum_ready"][h], n + n0 + 1)
                gate(g, pool)
                pool.dma_start(rows_of(g.sums, n * BLOCK), new_sums[b][:, :]).then_inc(s["sums_stored"][b], 16)

            over_blocks(pool, store)
            for b in range(2):
                done = 16 * (slot0[b] + (g.BLOCKS + 1 - b) // 2)
                pool.wait_ge(s["h_stored"][b], done)
                pool.wait_ge(s["sums_stored"][b], done)


def in_its_form(g, eng, general, windowed):
    flag = eng.value_load(g.windowed[0:1, 0:1], min_val=0, max_val=1)
    with eng.If(flag > 0):
        windowed(eng)
    with eng.Else():
        general(eng)


def gather_rows_of(g, s, pool, b, j, gathers):
    for into, table, index in gathers(b, j):
        pool.indirect_dma_start(out=into, out_offset=None, in_=table,
                                in_offset=bass.IndirectOffsetOnAxis(ap=index, axis=0)
                                ).then_inc(s["gathered"][b], 16)


def scatter_tile(g, s, pool, b, j, scatter):
    table, index, rows_in = scatter(b, j)
    pool.indirect_dma_start(out=table, out_offset=bass.IndirectOffsetOnAxis(ap=index, axis=0),
                            in_=rows_in, in_offset=None, compute_op=ALU.add).then_inc(s["scattered"][b][j], 16)


def scatter_in_turn(g, s, pool, runs, i, b, j, scatter):
    if j:
        pool.wait_ge(s["scattered"][b][j - 1], (i + runs) * 16 + 16)
    else:
        pool.wait_ge(s["scattered"][1 - b][TILES - 1], (i + runs + b) * 16)
    gate(g, pool)
    scatter_tile(g, s, pool, b, j, scatter)


def wait_for_scatters(s, eng, b, groups):
    for j in range(TILES):
        eng.wait_ge(s["scattered"][b][j], 16 * groups)


def gather_and_scatter(g, s, pool, runs, gathers, scatter, n_pairs):
    def step(i, with_scatter):
        for b in range(2):
            pool.wait_ge(s["numbers_ready"][b], i + runs + runs // n_pairs + 1)
            gate(g, pool)
            for j in range(TILES):
                gather_rows_of(g, s, pool, b, j, gathers)
                if with_scatter:
                    if j == 0:
                        pool.wait_ge(s["result_ready"][b], i + runs)
                        gate(g, pool)
                    scatter_in_turn(g, s, pool, runs, i - 1, b, j, scatter)

    step(0, False)
    with pool.Fori(1, n_pairs) as i:
        step(i, True)
    for b in range(2):
        pool.wait_ge(s["result_ready"][b], n_pairs + runs)
        gate(g, pool)
        for j in range(TILES):
            scatter_in_turn(g, s, pool, runs, n_pairs - 1, b, j, scatter)
    for b in range(2):
        wait_for_scatters(s, pool, b, n_pairs + runs)


def gather_and_scatter_windowed(g, s, pool, runs, gathers, scatter, n_pairs):
    def scatter_group(i, b):
        pool.wait_ge(s["result_ready"][b], i + runs + 1)
        wait_for_scatters(s, pool, 1 - b, i + runs + b)
        gate(g, pool)
        for j in range(TILES):
            scatter_tile(g, s, pool, b, j, scatter)

    def step(i, b, with_scatter):
        pool.wait_ge(s["numbers_ready"][b], i + runs + runs // n_pairs + 1)
        gate(g, pool)
        for j in range(TILES):
            gather_rows_of(g, s, pool, b, j, gathers)
        if with_scatter:
            scatter_group(i - 2 + b, 1 - b)

    step(0, 0, False)
    step(0, 1, False)
    step(1, 0, False)
    step(1, 1, True)
    with pool.Fori(2, n_pairs) as i:
        step(i, 0, True)
        step(i, 1, True)
    scatter_group(n_pairs - 2, 1)
    scatter_group(n_pairs - 1, 0)
    scatter_group(n_pairs - 1, 1)
    for b in range(2):
        wait_for_scatters(s, pool, b, n_pairs + runs)


def load_windows(g, s, sp, runs, i, b, table, windows):
    sp.wait_ge(s["target_rows_picked"][b], i + runs)
    gate(g, sp)
    for j in range(TILES):
        base = sp.value_load(g.bases[0:1, bass.ds(i * 2 * TILES + b * TILES + j, 1)], min_val=0,
                             max_val=g.N - WINDOW)
        sp.dma_start(windows[b][:, j, :], table[bass.ds(base, WINDOW), :].rearrange("(p c) f -> p (c f)", c=CHUNKS)
                     ).then_inc(s["windows_loaded"][b], 16)


def load_offsets(g, s, sp, runs, i, b, offsets):
    sp.wait_ge(s["same_ready"][b], i + runs)
    gate(g, sp)
    sp.dma_start(offsets[b][:, :], g.offset_table[bass.ds(i * 2 * GROUP + b * GROUP, GROUP)]
                 .partition_broadcast(P)).then_inc(s["offsets_loaded"][b], 16)


def find_same(g, s, dve, runs, i, b, offsets, same):
    dve.wait_ge(s["offsets_loaded"][b], (i + runs) * 16 + 16)
    dve.wait_ge(s["result_ready"][b], i + runs)
    dve.tensor_tensor(same[b][:, :, :], offsets[b][:, :].rearrange("p (j q) -> p j q", q=P),
                      g.offset_col[:, bass.ds(i * 2 + b, 1), :].rearrange("p a t -> p (a t)")
                      .unsqueeze(2).broadcast_to([P, TILES, P]),
                      ALU.is_equal).then_inc(s["same_ready"][b], 1)


def find_target_rows(g, s, dve, runs, i, b, offsets, target_row):
    dve.wait_ge(s["offsets_loaded"][b], (i + runs) * 16 + 16)
    dve.wait_ge(s["target_rows_picked"][b], i + runs)
    for c in range(CHUNKS):
        last = dve.tensor_scalar(target_row[b][:, c, :], offsets[b][:, :], g.window_row[:, c:c + 1], None,
                                 ALU.is_equal)
    last.then_inc(s["target_rows_found"][b], 1)


def pass_messages(g, s, k, table, zeros=None):
    nc = g.nc
    PAIRS = g.GROUPS // 2
    runs = k * PAIRS
    with ExitStack() as ctx:
        def sb(name, shape, dt=F32):
            return ctx.enter_context(nc.sbuf_tensor(f"{name}_m{k}", shape, dt))

        def ps(name):
            return ctx.enter_context(nc.psum_tensor(f"{name}_m{k}", [P, 512], F32))

        gathered = [[sb(f"gathered{b}{e}", [P, TILES, D]) for e in range(2)] for b in range(2)]
        numbers = [sb(f"numbers{b}", [P, 2 * TILES], I32) for b in range(2)]
        targets_to = [sb(f"targets_to{b}", [P, TILES], I32) for b in range(2)]
        turned = [sb(f"turned{e}", [P, GROUP]) for e in range(2)]
        hidden = [sb(f"hidden{m}", [P, GROUP]) for m in range(2)]
        messages = sb("messages", [P, TILES, D])
        result = [sb(f"result{b}", [P, TILES, D]) for b in range(2)]
        offsets = [sb(f"offsets{b}", [P, GROUP], I32) for b in range(2)]
        same = [sb(f"same{b}", [P, TILES, P]) for b in range(2)]
        ps_turn = [ps(f"ps_turn{e}") for e in range(2)]
        ps_hidden = [ps(f"ps_hidden{m}") for m in range(2)]
        ps_msg = ps("ps_msg")
        ps_sum = ps("ps_sum")
        windows = [sb(f"windows{b}", [P, TILES, CHUNKS * D]) for b in range(2)]
        target_row = [sb(f"target_row{b}", [P, CHUNKS, GROUP]) for b in range(2)]
        block = ctx.enter_context(nc.Block())

        @block.gpsimd
        def _(pool):
            def source(b, j):
                return gathered[b][0][:, j, :], table, numbers[b][:, j:j + 1]

            def target(b, j):
                return gathered[b][1][:, j, :], table, numbers[b][:, TILES + j:TILES + j + 1]

            def result_of(b, j):
                return g.sums[:, :], targets_to[b][:, j:j + 1], result[b][:, j, :]

            in_its_form(
                g, pool,
                lambda eng: gather_and_scatter(g, s, eng, runs, lambda b, j: [source(b, j), target(b, j)],
                                               result_of, PAIRS),
                lambda eng: gather_and_scatter_windowed(g, s, eng, runs, lambda b, j: [source(b, j)],
                                                        result_of, PAIRS))

        @block.sync
        def _(sp):
            def zero(i, b):
                if zeros is not None:
                    sp.dma_start(rows_of(g.attn_sums, i * 2 * GROUP + b * GROUP, GROUP, TILES),
                                 zeros).then_inc(s["zeros_stored"], 16)

            def general(sp):
                with sp.Fori(0, PAIRS) as i:
                    for b in range(2):
                        load_offsets(g, s, sp, runs, i, b, offsets)
                        zero(i, b)

            def windowed(sp):
                with sp.Fori(0, PAIRS) as i:
                    for b in range(2):
                        load_offsets(g, s, sp, runs, i, b, offsets)
                        load_windows(g, s, sp, runs, i, b, table, windows)
                        zero(i, b)

            in_its_form(g, sp, general, windowed)
            if zeros is not None:
                sp.wait_ge(s["zeros_stored"], 32 + 16 * g.GROUPS)

        @block.tensor
        def _(pe):
            def turn(b, e, done):
                for j in range(TILES):
                    mm = pe.transpose(ps_turn[e][:, j * P:(j + 1) * P], gathered[b][e][:, j, :], g.ident[:, :])
                mm.then_inc(done, 1)

            def first_layer(i, b):
                n = (i + runs) * 2 + b
                for e in range(2):
                    pe.wait_ge(s["turn_copied"][e], n + 1)
                for m in range(2):
                    pe.wait_ge(s["hidden_ready"][m], n)
                    for e in range(2):
                        mm = pe.matmul(ps_hidden[m][:, :], g.Wm1_sb[:, e, m * D:(m + 1) * D], turned[e][:, :],
                                       start=(e == 0), stop=(e == 1))
                    mm.then_inc(s["hidden_summed"][m], 1)

            def second_layer(i, b):
                n = (i + runs) * 2 + b
                for m in range(2):
                    pe.wait_ge(s["hidden_ready"][m], n + 1)
                pe.wait_ge(s["messages_ready"], n)
                for j in range(TILES):
                    for m in range(2):
                        mm = pe.matmul(ps_msg[:, j * D:(j + 1) * D], hidden[m][:, j * P:(j + 1) * P],
                                       g.Wm2n_sb[:, m, :], start=(m == 0), stop=(m == 1))
                mm.then_inc(s["messages_summed"], 1)

            def combine(i, b):
                n = (i + runs) * 2 + b
                pe.wait_ge(s["messages_ready"], n + 1)
                pe.wait_ge(s["same_ready"][b], i + runs + 1)
                pe.wait_ge(s["result_ready"][1 - b], i + runs + b)
                for j in range(TILES):
                    mm = pe.matmul(ps_sum[:, j * D:(j + 1) * D], same[b][:, j, :], messages[:, j, :],
                                   start=True, stop=True)
                mm.then_inc(s["combined"], 1)

            def general(pe):
                with pe.Fori(0, PAIRS) as i:
                    for b in range(2):
                        pe.wait_ge(s["gathered"][b], (i + runs) * 128 + 128)
                        for e in range(2):
                            pe.wait_ge(s["turn_copied"][e], (i + runs) * 2 + b)
                            turn(b, e, s["ends_turned"][e])
                        first_layer(i, b)
                        second_layer(i, b)
                        combine(i, b)

            def turn_sources(i, b):
                pe.wait_ge(s["gathered"][b], (i + runs) * 64 + 64)
                pe.wait_ge(s["turn_copied"][0], (i + runs) * 2 + b)
                turn(b, 0, s["ends_turned"][0])

            def pick_targets(i, b, tiles):
                if tiles[0] == 0:
                    pe.wait_ge(s["turn_copied"][1], (i + runs) * 2 + b)
                    pe.wait_ge(s["target_rows_found"][b], i + runs + 1)
                    pe.wait_ge(s["windows_loaded"][b], (i + runs) * 64 + 64)
                for j in tiles:
                    for c in range(CHUNKS):
                        mm = pe.matmul(ps_turn[1][:, j * P:(j + 1) * P], windows[b][:, j, c * D:(c + 1) * D],
                                       target_row[b][:, c, j * P:(j + 1) * P], start=(c == 0),
                                       stop=(c == CHUNKS - 1))
                if tiles[-1] == TILES - 1:
                    mm.then_inc(s["target_rows_picked"][b], 1)

            def windowed(pe):
                def step(i, b, last):
                    then = (i + b, 1 - b)
                    first_layer(i, b)
                    if not last:
                        turn_sources(*then)
                        pick_targets(*then, [0, 1])
                    second_layer(i, b)
                    if not last:
                        pick_targets(*then, [2, 3])
                    combine(i, b)

                turn_sources(0, 0)
                pick_targets(0, 0, [0, 1, 2, 3])
                with pe.Fori(0, PAIRS - 1) as i:
                    step(i, 0, False)
                    step(i, 1, False)
                step(PAIRS - 1, 0, False)
                step(PAIRS - 1, 1, True)

            in_its_form(g, pe, general, windowed)

        @block.scalar
        def _(act):
            def copy_sources(i, b):
                act.wait_ge(s["ends_turned"][0], (i + runs) * 2 + b + 1)
                act.copy(turned[0][:, :], ps_turn[0][:, :]).then_inc(s["turn_copied"][0], 1)

            def next_numbers(i, b):
                act.copy(numbers[b][:, :], g.gather_rows[:, bass.ds(i * 2 + (b + 2), 1), :]
                         .rearrange("p a t -> p (a t)")).then_inc(s["numbers_ready"][b], 1)

            def first_hidden(i, b):
                act.wait_ge(s["hidden_summed"][0], (i + runs) * 2 + b + 1)
                act.activation(hidden[0][:, :], ps_hidden[0][:, :], ACT.Relu,
                               bias=g.bm1_col[:, 0:1]).then_inc(s["hidden_ready"][0], 1)

            def copy_result(i, b):
                wait_for_scatters(s, act, b, i + runs)
                act.copy(targets_to[b][:, :], g.scatter_rows[:, bass.ds(i * 2 + b, 1), :]
                         .rearrange("p a t -> p (a t)"))
                act.wait_ge(s["combined"], (i + runs) * 2 + b + 1)
                act.copy(result[b][:, :, :].rearrange("p j c -> p (j c)"),
                         ps_sum[:, :]).then_inc(s["result_ready"][b], 1)

            def general(act):
                with act.Fori(0, PAIRS) as i:
                    for b in range(2):
                        copy_sources(i, b)
                        act.wait_ge(s["ends_turned"][1], (i + runs) * 2 + b + 1)
                        next_numbers(i, b)
                        first_hidden(i, b)
                        copy_result(i, b)

            def windowed(act):
                def step(i, b, last):
                    first_hidden(i, b)
                    if not last:
                        copy_sources(i + b, 1 - b)
                        next_numbers(i + b, 1 - b)
                    copy_result(i, b)

                copy_sources(0, 0)
                next_numbers(0, 0)
                with act.Fori(0, PAIRS - 1) as i:
                    step(i, 0, False)
                    step(i, 1, False)
                step(PAIRS - 1, 0, False)
                step(PAIRS - 1, 1, True)

            for b in range(2):
                act.copy(numbers[b][:, :], g.gather_rows[:, b, :]).then_inc(s["numbers_ready"][b], 1)
            in_its_form(g, act, general, windowed)

        @block.vector
        def _(dve):
            def second_hidden(i, b):
                dve.wait_ge(s["hidden_summed"][1], (i + runs) * 2 + b + 1)
                dve.tensor_scalar(hidden[1][:, :], ps_hidden[1][:, :], g.bm1_col[:, 1:2], 0.0, ALU.add,
                                  ALU.max).then_inc(s["hidden_ready"][1], 1)

            def copy_targets():
                dve.tensor_copy(turned[1][:, :], ps_turn[1][:, :]).then_inc(s["turn_copied"][1], 1)

            def add_bias(i, b):
                dve.wait_ge(s["messages_summed"], (i + runs) * 2 + b + 1)
                dve.tensor_tensor(messages[:, :, :], ps_msg[:, :].rearrange("p (j c) -> p j c", c=D),
                                  g.bm2n_all[:, :].unsqueeze(1).broadcast_to([P, TILES, D]),
                                  ALU.add).then_inc(s["messages_ready"], 1)

            def general(dve):
                with dve.Fori(0, PAIRS) as i:
                    for b in range(2):
                        find_same(g, s, dve, runs, i, b, offsets, same)
                        dve.wait_ge(s["ends_turned"][1], (i + runs) * 2 + b + 1)
                        copy_targets()
                        second_hidden(i, b)
                        add_bias(i, b)

            def windowed(dve):
                def step(i, b, remain):
                    second_hidden(i, b)
                    if remain > 0:
                        find_same(g, s, dve, runs, i + b, 1 - b, offsets, same)
                    add_bias(i, b)
                    if remain > 0:
                        dve.wait_ge(s["target_rows_picked"][1 - b], i + b + runs + 1)
                        copy_targets()
                    if remain > 1:
                        find_target_rows(g, s, dve, runs, i + 1, b, offsets, target_row)

                find_target_rows(g, s, dve, runs, 0, 0, offsets, target_row)
                find_same(g, s, dve, runs, 0, 0, offsets, same)
                find_target_rows(g, s, dve, runs, 0, 1, offsets, target_row)
                dve.wait_ge(s["target_rows_picked"][0], runs + 1)
                copy_targets()
                with dve.Fori(0, PAIRS - 1) as i:
                    step(i, 0, 3)
                    step(i, 1, 2)
                step(PAIRS - 1, 0, 1)
                step(PAIRS - 1, 1, 0)

            in_its_form(g, dve, general, windowed)


def over_blocks(g, eng, body):
    with eng.Fori(0, g.BLOCKS // 2) as i:
        body(i * 2, i, 0, False)
        body(i * 2 + 1, i, 1, False)
    body(g.BLOCKS - 1, g.BLOCKS // 2, 0, True)


def row_statistics(g, dve, s, total, stats, moments, n):
    for r in range(ROWS):
        last = dve.bn_stats(stats[:, r, :], total[:, r * D:(r + 1) * D])
    last.then_inc(s["row_stats"], 1)
    dve.wait_ge(s["row_stats"], n + 1)
    gate(g, dve)
    for r in range(ROWS):
        last = dve.bn_aggr(moments[:, r, :], stats[:, r, :])
    last.then_inc(s["row_moments"], 1)


def finish_messages(g, s):
    nc = g.nc
    with ExitStack() as ctx:
        def sb(name, shape, dt=F32):
            return ctx.enter_context(nc.sbuf_tensor(f"{name}_f", shape, dt))

        def ps(name, n=512):
            return ctx.enter_context(nc.psum_tensor(f"{name}_f", [P, n], F32))

        sums_in = [sb(f"sums_in{b}", [P, BLOCK]) for b in range(2)]
        x_in = [sb(f"x_in{b}", [P, BLOCK]) for b in range(2)]
        total = sb("total", [P, BLOCK])
        stats = sb("stats", [P, ROWS, 6])
        moments = sb("moments", [P, ROWS, 2])
        inverse = sb("inverse", [P, ROWS, 1])
        x1 = [sb(f"x1{b}", [P, BLOCK]) for b in range(2)]
        turned = [sb(f"turned{h}", [P, HALF]) for h in range(2)]
        q_out = [sb(f"q_out{b}", [P, BLOCK]) for b in range(2)]
        kv_out = [sb(f"kv_out{b}", [P, 2 * BLOCK]) for b in range(2)]
        ps_turn = [ps(f"ps_turn{h}") for h in range(2)]
        ps_q = [ps(f"ps_q{h}") for h in range(2)]
        ps_kv = [ps(f"ps_kv{h}", 1024) for h in range(2)]
        pieces = parts_of(g.TAIL_PARTS)
        block = ctx.enter_context(nc.Block())

        @block.sync
        def _(sp):
            def load(n, i, b, last):
                sp.wait_ge(s["residual_added"][b], i)
                gate(g, sp)
                sp.dma_start(sums_in[b][:, :], rows_of(g.sums, n * BLOCK)).then_inc(s["sums_loaded"][b], 16)
                for a, z in pieces if last else [(0, P)]:
                    sp.dma_start(x_in[b][a:z, :], rows_of(g.x, n * BLOCK + a * ROWS, (z - a) * ROWS)
                                 ).then_inc(s["x_loaded"][b], 16)

            over_blocks(g, sp, load)

        @block.vector
        def _(dve):
            def body(n, i, b, last):
                dve.wait_ge(s["sums_loaded"][b], i * 16 + 16)
                dve.wait_ge(s["x_loaded"][b], i * 16 + 16 * (len(pieces) if last else 1))
                dve.wait_ge(s["normed"], n)
                dve.scalar_tensor_tensor(out=total[:, :], in0=sums_in[b][:, :], scalar=0.0, in1=x_in[b][:, :],
                                         op0=ALU.max, op1=ALU.add).then_inc(s["residual_added"][b], 1)
                dve.wait_ge(s["x1_stored"][b], i * 16)
                dve.wait_ge(s["x1_turned"][b][1], i)
                dve.wait_ge(s["residual_added"][b], i + 1)
                row_statistics(g, dve, s, total, stats, moments, n)
                dve.wait_ge(s["rooted"], n + 1)
                dve.reciprocal(inverse[:, :, :], inverse[:, :, :]).then_inc(s["inverted"], 1)
                dve.wait_ge(s["inverted"], n + 1)
                for r in range(ROWS):
                    row = slice(r * D, (r + 1) * D)
                    last_row = dve.tensor_scalar(x1[b][:, row], total[:, row], moments[:, r, 0:1],
                                                 inverse[:, r, :], ALU.subtract, ALU.mult)
                last_row.then_inc(s["normed"], 1)

            over_blocks(g, dve, body)

        @block.tensor
        def _(pe):
            def body(n, i, b, last):
                pe.wait_ge(s["normed"], n + 1)
                for h in range(2):
                    pe.wait_ge(s["x1_copied"][h], n)
                    for r in range(4):
                        at = (4 * h + r) * D
                        mm = pe.transpose(ps_turn[h][:, r * P:(r + 1) * P], x1[b][:, at:at + D], g.ident[:, :])
                    mm.then_inc(s["x1_turned"][b][h], 1)
                for h in range(2):
                    pe.wait_ge(s["x1_copied"][h], n + 1)
                    pe.wait_ge(s["q_copied"][h], n)
                    pe.wait_ge(s["kv_copied"][h], n)
                    for r in range(4):
                        lhs = turned[h][:, r * P:(r + 1) * P]
                        pe.matmul(ps_q[h][:, r * D:(r + 1) * D], lhs, g.Wqkv_sb[:, 0:D], start=True, stop=True)
                        mm = pe.matmul(ps_kv[h][:, r * 2 * D:(r + 1) * 2 * D], lhs, g.Wqkv_sb[:, D:3 * D],
                                       start=True, stop=True)
                    mm.then_inc(s["qkv_ready"][h], 1)

            over_blocks(g, pe, body)

        @block.scalar
        def _(act):
            def root(n):
                act.wait_ge(s["row_moments"], n + 1)
                act.wait_ge(s["normed"], n)
                act.activation(inverse[:, :, :], moments[:, :, 1:2], ACT.Sqrt,
                               bias=g.eps_col[:, 0:1]).then_inc(s["rooted"], 1)

            root(0)

            def body(n, i, b, last):
                for h in range(2):
                    act.wait_ge(s["x1_turned"][b][h], i + 1)
                    act.copy(turned[h][:, :], ps_turn[h][:, :]).then_inc(s["x1_copied"][h], 1)
                if not last:
                    root(n + 1)
                for h in range(2):
                    act.wait_ge(s["qkv_ready"][h], n + 1)
                    act.wait_ge(s["q_stored"][b], i * 16)
                    act.copy(q_out[b][:, h * HALF:(h + 1) * HALF], ps_q[h][:, :]).then_inc(s["q_copied"][h], 1)
                    act.wait_ge(s["kv_stored"][b], i * 16)
                    act.copy(kv_out[b][:, h * BLOCK:(h + 1) * BLOCK], ps_kv[h][:, :]).then_inc(s["kv_copied"][h], 1)

            over_blocks(g, act, body)

        @block.gpsimd
        def _(pool):
            def store(n, i, b, last):
                pool.wait_ge(s["normed"], n + 1)
                gate(g, pool)
                pool.dma_start(rows_of(g.x1_table, n * BLOCK), x1[b][:, :]).then_inc(s["x1_stored"][b], 16)
                for h in range(2):
                    pool.wait_ge(s["kv_copied"][h], n + 1)
                gate(g, pool)
                pool.dma_start(rows_of(g.q_table, n * BLOCK), q_out[b][:, :]).then_inc(s["q_stored"][b], 16)
                pool.dma_start(rows_of(g.kv_table, n * BLOCK), kv_out[b][:, :]).then_inc(s["kv_stored"][b], 16)

            over_blocks(g, pool, store)
            for b in range(2):
                done = 16 * ((g.BLOCKS + 1 - b) // 2)
                for name in ("x1_stored", "q_stored", "kv_stored"):
                    pool.wait_ge(s[name][b], done)


def attend(g, s):
    nc = g.nc
    PAIRS = g.GROUPS // 2
    with ExitStack() as ctx:
        def sb(name, shape, dt=F32):
            return ctx.enter_context(nc.sbuf_tensor(f"{name}_t", shape, dt))

        def ps(name, n=512):
            return ctx.enter_context(nc.psum_tensor(f"{name}_t", [P, n], F32))

        q_in = [sb(f"q_in{b}", [P, TILES, D]) for b in range(2)]
        kv_in = [sb(f"kv_in{b}", [P, TILES, 2 * D]) for b in range(2)]
        numbers = [sb(f"numbers{b}", [P, 2 * TILES], I32) for b in range(2)]
        targets_to = [sb(f"targets_to{b}", [P, TILES], I32) for b in range(2)]
        edges_in = [sb(f"edges_in{b}", [P, TILES, D]) for b in range(2)]
        turned = sb("turned", [P, GROUP])
        qk = sb("qk", [P, TILES, D])
        qke = sb("qke", [P, TILES, D])
        score = sb("score", [P, TILES * HEADS])
        low = sb("low", [P, TILES * HEADS])
        clipped = sb("clipped", [P, TILES * HEADS])
        messages = sb("messages", [P, TILES, AT])
        result = [sb(f"result{b}", [P, TILES, AT]) for b in range(2)]
        offsets = [sb(f"offsets{b}", [P, GROUP], I32) for b in range(2)]
        same = [sb(f"same{b}", [P, TILES, P]) for b in range(2)]
        ps_turn = ps("ps_turn")
        ps_edge = ps("ps_edge")
        ps_sum = [ps(f"ps_sum{u}") for u in range(2)]
        windows = [sb(f"windows{b}", [P, TILES, CHUNKS * D]) for b in range(2)]
        target_row = [sb(f"target_row{b}", [P, CHUNKS, GROUP]) for b in range(2)]
        ps_q = ps("ps_q")
        block = ctx.enter_context(nc.Block())

        @block.gpsimd
        def _(pool):
            def source(b, j):
                return kv_in[b][:, j, :], g.kv_table[:, :], numbers[b][:, j:j + 1]

            def target(b, j):
                return q_in[b][:, j, :], g.q_table[:, :], numbers[b][:, TILES + j:TILES + j + 1]

            def result_of(b, j):
                return g.attn_sums[:, :], targets_to[b][:, j:j + 1], result[b][:, j, :]

            in_its_form(
                g, pool,
                lambda eng: gather_and_scatter(g, s, eng, 0, lambda b, j: [source(b, j), target(b, j)],
                                               result_of, PAIRS),
                lambda eng: gather_and_scatter_windowed(g, s, eng, 0, lambda b, j: [source(b, j)],
                                                        result_of, PAIRS))

        @block.sync
        def _(sp):
            def load_edges(i, b, last=False):
                n = i * 2 + b
                sp.wait_ge(s["edges_turned"], i * 2)
                gate(g, sp)
                sp.dma_start(edges_in[b][:, 0:3, :],
                             g.edge_attr_128[0:3 * g.QUARTER, :].rearrange("(j e) c -> e j c", j=3)
                             [bass.ds(n * P, P), :, :]).then_inc(s["edges_loaded"][b], 16)
                if last and b:
                    sp.dma_start(edges_in[b][:, 3, :], g.edge_attr_128[g.E - P:g.E, :]
                                 ).then_inc(s["edges_loaded"][b], 16)
                else:
                    count = g.TAIL_EDGES if last else P
                    sp.dma_start(edges_in[b][0:count, 3, :],
                                 g.edge_attr_128[bass.ds(n * P + 3 * g.QUARTER, count), :]
                                 ).then_inc(s["edges_loaded"][b], 16)

            def load(i, b, windowed, last=False):
                load_offsets(g, s, sp, 0, i, b, offsets)
                if windowed:
                    load_windows(g, s, sp, 0, i, b, g.q_table, windows)
                load_edges(i, b, last)

            def over_pairs(windowed):
                with sp.Fori(0, PAIRS - 1) as i:
                    load(i, 0, windowed)
                    load(i, 1, windowed)
                load(PAIRS - 1, 0, windowed, last=True)
                load(PAIRS - 1, 1, windowed, last=True)

            in_its_form(g, sp, lambda _: over_pairs(False), lambda _: over_pairs(True))

        @block.tensor
        def _(pe):
            def project_edges(i, b):
                n = i * 2 + b
                pe.wait_ge(s["edges_loaded"][b], i * 32 + 32)
                pe.wait_ge(s["edges_copied"], n)
                for j in range(TILES):
                    mm = pe.transpose(ps_turn[:, j * P:(j + 1) * P], edges_in[b][:, j, :], g.ident[:, :])
                mm.then_inc(s["edges_turned"], 1)
                pe.wait_ge(s["edges_copied"], n + 1)
                pe.wait_ge(s["edges_used"], n)
                for j in range(TILES):
                    mm = pe.matmul(ps_edge[:, j * D:(j + 1) * D], turned[:, j * P:(j + 1) * P], g.WE_sb[:, :],
                                   start=True, stop=True)
                mm.then_inc(s["edges_projected"], 1)

            def combine(i, b):
                pe.wait_ge(s["values_weighted"], i * 2 + b + 1)
                pe.wait_ge(s["same_ready"][b], i + 1)
                pe.wait_ge(s["result_ready"][1 - b], i + b)
                for j in range(TILES):
                    at = (j % 2) * AT
                    mm = pe.matmul(ps_sum[j // 2][:, at:at + AT], same[b][:, j, :], messages[:, j, :],
                                   start=True, stop=True)
                mm.then_inc(s["combined"], 1)

            def general(pe):
                with pe.Fori(0, PAIRS) as i:
                    for b in range(2):
                        project_edges(i, b)
                        combine(i, b)

            def pick_queries(i, b):
                pe.wait_ge(s["multiplied"], i * 2 + b)
                pe.wait_ge(s["target_rows_found"][b], i + 1)
                pe.wait_ge(s["windows_loaded"][b], i * 64 + 64)
                for j in range(TILES):
                    for c in range(CHUNKS):
                        mm = pe.matmul(ps_q[:, j * D:(j + 1) * D], target_row[b][:, c, j * P:(j + 1) * P],
                                       windows[b][:, j, c * D:(c + 1) * D], start=(c == 0),
                                       stop=(c == CHUNKS - 1))
                mm.then_inc(s["target_rows_picked"][b], 1)

            def windowed(pe):
                def step(i, b, last):
                    if not last:
                        pick_queries(i + b, 1 - b)
                        project_edges(i + b, 1 - b)
                    combine(i, b)

                pick_queries(0, 0)
                project_edges(0, 0)
                with pe.Fori(0, PAIRS - 1) as i:
                    step(i, 0, False)
                    step(i, 1, False)
                step(PAIRS - 1, 0, False)
                step(PAIRS - 1, 1, True)

            in_its_form(g, pe, general, windowed)

        @block.scalar
        def _(act):
            def copy_edges(i, b):
                act.wait_ge(s["edges_turned"], i * 2 + b + 1)
                act.copy(turned[:, :], ps_turn[:, :]).then_inc(s["edges_copied"], 1)

            def weigh(i, b):
                n = i * 2 + b
                act.wait_ge(s["clipped"], n + 1)
                act.wait_ge(s["combined"], n)
                act.activation(messages[:, :, D:AT], clipped[:, :].rearrange("p (j h) -> p j h", h=HEADS),
                               ACT.Exp).then_inc(s["weights_ready"], 1)
                act.wait_ge(s["values_weighted"], n + 1)
                act.copy(numbers[b][:, :], g.gather_rows[:, bass.ds(i * 2 + (b + 2), 1), :]
                         .rearrange("p a t -> p (a t)")).then_inc(s["numbers_ready"][b], 1)

            def copy_result(i, b):
                wait_for_scatters(s, act, b, i)
                act.copy(targets_to[b][:, :], g.scatter_rows[:, bass.ds(i * 2 + b, 1), :]
                         .rearrange("p a t -> p (a t)"))
                act.wait_ge(s["combined"], i * 2 + b + 1)
                for u in range(2):
                    last = act.copy(result[b][:, 2 * u:2 * u + 2, :].rearrange("p j c -> p (j c)"),
                                    ps_sum[u][:, 0:2 * AT])
                last.then_inc(s["result_ready"][b], 1)

            def general(act):
                with act.Fori(0, PAIRS) as i:
                    for b in range(2):
                        copy_edges(i, b)
                        weigh(i, b)
                        copy_result(i, b)

            def windowed(act):
                def step(i, b, last):
                    if not last:
                        copy_edges(i + b, 1 - b)
                    weigh(i, b)
                    copy_result(i, b)

                copy_edges(0, 0)
                with act.Fori(0, PAIRS - 1) as i:
                    step(i, 0, False)
                    step(i, 1, False)
                step(PAIRS - 1, 0, False)
                step(PAIRS - 1, 1, True)

            for b in range(2):
                act.copy(numbers[b][:, :], g.gather_rows[:, b, :]).then_inc(s["numbers_ready"][b], 1)
            in_its_form(g, act, general, windowed)

        @block.vector
        def _(dve):
            def multiply_general(i, b):
                dve.wait_ge(s["gathered"][b], i * 128 + 128)
                dve.wait_ge(s["edges_used"], i * 2 + b)
                dve.tensor_tensor(qk[:, :, :], q_in[b][:, :, :], kv_in[b][:, :, 0:D],
                                  ALU.mult).then_inc(s["multiplied"], 1)

            def multiply_windowed(i, b):
                dve.wait_ge(s["gathered"][b], i * 64 + 64)
                dve.wait_ge(s["target_rows_picked"][b], i + 1)
                dve.wait_ge(s["edges_used"], i * 2 + b)
                dve.tensor_tensor(qk[:, :, :], ps_q[:, :].rearrange("p (j c) -> p j c", c=D), kv_in[b][:, :, 0:D],
                                  ALU.mult).then_inc(s["multiplied"], 1)

            def weigh_values(n, b):
                dve.wait_ge(s["multiplied"], n + 1)
                dve.wait_ge(s["edges_projected"], n + 1)
                dve.wait_ge(s["scored"], n)
                dve.tensor_tensor(qke[:, :, :], qk[:, :, :], ps_edge[:, :].rearrange("p (j c) -> p j c", c=D),
                                  ALU.mult).then_inc(s["edges_used"], 1)
                dve.wait_ge(s["edges_used"], n + 1)
                dve.wait_ge(s["scaled"], n)
                dve.tensor_reduce(score[:, :], qke[:, :, :].rearrange("p j (h c) -> p (j h) c", h=HEADS),
                                  AX.X, ALU.add).then_inc(s["scored"], 1)
                dve.wait_ge(s["scored"], n + 1)
                dve.wait_ge(s["clipped"], n)
                dve.tensor_scalar(low[:, :], score[:, :], DH ** -0.5, CLIP, ALU.mult,
                                  ALU.min).then_inc(s["scaled"], 1)
                dve.wait_ge(s["scaled"], n + 1)
                dve.wait_ge(s["weights_ready"], n)
                dve.tensor_scalar(clipped[:, :], low[:, :], -CLIP, None, ALU.max).then_inc(s["clipped"], 1)
                dve.wait_ge(s["weights_ready"], n + 1)
                dve.tensor_tensor(
                    messages[:, :, 0:D].rearrange("p j (h c) -> p j h c", h=HEADS),
                    kv_in[b][:, :, D:2 * D].rearrange("p j (h c) -> p j h c", h=HEADS),
                    messages[:, :, D:AT].unsqueeze(3).broadcast_to([P, TILES, HEADS, DH]),
                    ALU.mult).then_inc(s["values_weighted"], 1)

            def general(dve):
                with dve.Fori(0, PAIRS) as i:
                    for b in range(2):
                        find_same(g, s, dve, 0, i, b, offsets, same)
                        multiply_general(i, b)
                        weigh_values(i * 2 + b, b)

            def windowed(dve):
                def step(i, b, remain):
                    multiply_windowed(i, b)
                    if remain > 0:
                        find_same(g, s, dve, 0, i + b, 1 - b, offsets, same)
                    weigh_values(i * 2 + b, b)
                    if remain > 1:
                        find_target_rows(g, s, dve, 0, i + 1, b, offsets, target_row)

                find_target_rows(g, s, dve, 0, 0, 0, offsets, target_row)
                find_same(g, s, dve, 0, 0, 0, offsets, same)
                find_target_rows(g, s, dve, 0, 0, 1, offsets, target_row)
                with dve.Fori(0, PAIRS - 1) as i:
                    step(i, 0, 3)
                    step(i, 1, 2)
                step(PAIRS - 1, 0, 1)
                step(PAIRS - 1, 1, 0)

            in_its_form(g, dve, general, windowed)


def measure(g, dve, turned, n, h, last):
    half = turned[:, h * HALF:(h + 1) * HALF]
    if last:
        half = half.rearrange("p (r q) -> p r q", q=P)[:, :, 0:g.TAIL_PARTS]
    return dve.bn_stats(g.feature_stats[:, bass.ds(n * 2 + h, 1), :].rearrange("p a k -> p (a k)"), half)


def finish_attention(g, s):
    nc = g.nc
    with ExitStack() as ctx:
        def sb(name, shape, dt=F32):
            return ctx.enter_context(nc.sbuf_tensor(f"{name}_y", shape, dt))

        sums_in = [sb(f"sums_in{b}", [P, ROWS * AT]) for b in range(2)]
        x1_in = [sb(f"x1_in{b}", [P, BLOCK]) for b in range(2)]
        weight = sb("weight", [P, ROWS, HEADS])
        inverse = sb("inverse", [P, ROWS, HEADS])
        mean_v = sb("mean_v", [P, BLOCK])
        y = [sb(f"y{b}", [P, BLOCK]) for b in range(2)]
        turned = [sb(f"turned{b}", [P, BLOCK]) for b in range(2)]
        ps_turn = [ctx.enter_context(nc.psum_tensor(f"ps_turn_y{h}", [P, 512], F32)) for h in range(2)]
        block = ctx.enter_context(nc.Block())

        @block.sync
        def _(sp):
            def load(n, i, b, last):
                sp.wait_ge(s["y_summed"][b], i)
                gate(g, sp)
                sp.dma_start(sums_in[b][:, :], rows_of(g.attn_sums, n * BLOCK)).then_inc(s["sums_loaded"][b], 16)
                sp.dma_start(x1_in[b][:, :], rows_of(g.x1_table, n * BLOCK)).then_inc(s["x1_loaded"][b], 16)

            over_blocks(g, sp, load)

        @block.vector
        def _(dve):
            def body(n, i, b):
                rows = sums_in[b][:, :].rearrange("p (r c) -> p r c", c=AT)
                dve.wait_ge(s["sums_loaded"][b], i * 16 + 16)
                dve.wait_ge(s["mean_ready"], n)
                dve.tensor_scalar(weight[:, :, :], rows[:, :, D:AT], ATTN_EPS, None,
                                  ALU.add).then_inc(s["weights_summed"], 1)
                dve.wait_ge(s["weights_summed"], n + 1)
                dve.reciprocal(inverse[:, :, :], weight[:, :, :]).then_inc(s["inverted"], 1)
                dve.wait_ge(s["inverted"], n + 1)
                dve.wait_ge(s["y_summed"][1 - b], i + b)
                dve.tensor_tensor(mean_v[:, :].rearrange("p (r h c) -> p r h c", r=ROWS, h=HEADS),
                                  rows[:, :, 0:D].rearrange("p r (h c) -> p r h c", h=HEADS),
                                  inverse[:, :, :].unsqueeze(3).broadcast_to([P, ROWS, HEADS, DH]),
                                  ALU.mult).then_inc(s["mean_ready"], 1)
                dve.wait_ge(s["mean_ready"], n + 1)
                dve.wait_ge(s["x1_loaded"][b], i * 16 + 16)
                dve.wait_ge(s["y_turned"][b][1], i)
                dve.tensor_tensor(y[b][:, :], mean_v[:, :], x1_in[b][:, :], ALU.add).then_inc(s["y_summed"][b], 1)

            def measure_block(n, i, b, last=False):
                for h in range(2):
                    dve.wait_ge(s["y_copied"][h], n + 1)
                    measured = measure(g, dve, turned[b], n, h, last)
                measured.then_inc(s["measured"][b], 1)

            body(0, 0, 0)
            with dve.Fori(0, g.BLOCKS // 2) as i:
                body(i * 2 + 1, i, 1)
                measure_block(i * 2, i, 0)
                body(i * 2 + 2, i + 1, 0)
                measure_block(i * 2 + 1, i, 1)
            measure_block(g.BLOCKS - 1, g.BLOCKS // 2, 0, last=True)

        @block.tensor
        def _(pe):
            def body(n, i, b, last):
                pe.wait_ge(s["y_summed"][b], i + 1)
                for h in range(2):
                    pe.wait_ge(s["y_copied"][h], n)
                    for r in range(4):
                        at = (4 * h + r) * D
                        mm = pe.transpose(ps_turn[h][:, r * P:(r + 1) * P], y[b][:, at:at + D], g.ident[:, :])
                    mm.then_inc(s["y_turned"][b][h], 1)

            over_blocks(g, pe, body)

        @block.scalar
        def _(act):
            def body(n, i, b, last):
                for h in range(2):
                    act.wait_ge(s["y_turned"][b][h], i + 1)
                    act.wait_ge(s["y_stored"][b], i * 16)
                    act.wait_ge(s["measured"][b], i)
                    act.copy(turned[b][:, h * HALF:(h + 1) * HALF], ps_turn[h][:, :]).then_inc(s["y_copied"][h], 1)

            over_blocks(g, act, body)

        @block.gpsimd
        def _(pool):
            def store(n, i, b, last):
                for h in range(2):
                    pool.wait_ge(s["y_copied"][h], n + 1)
                gate(g, pool)
                pool.dma_start(g.turned_table[bass.ds(n * P, P), :], turned[b][:, :]).then_inc(s["y_stored"][b], 16)

            over_blocks(g, pool, store)
            for b in range(2):
                pool.wait_ge(s["y_stored"][b], 16 * ((g.BLOCKS + 1 - b) // 2))


def batch_norm_coefficients(g, dve, act, s, which, moments, scale, shift):
    if act is not None:
        act.wait_ge(s["bn_step"], 1)
        act.activation(scale[:, :], moments[:, 1:2], ACT.Sqrt, bias=g.eps_col[:, 0:1]).then_inc(s["bn_step"], 1)
        return
    gamma, beta = g.gammas[:, which:which + 1], g.betas[:, which:which + 1]
    dve.bn_aggr(moments[:, :], g.feature_stats[:, :, :].rearrange("p a k -> p (a k)")).then_inc(s["bn_step"], 1)
    dve.wait_ge(s["bn_step"], 2)
    dve.reciprocal(scale[:, :], scale[:, :]).then_inc(s["bn_step"], 1)
    dve.wait_ge(s["bn_step"], 3)
    dve.tensor_tensor(scale[:, :], scale[:, :], gamma, ALU.mult).then_inc(s["bn_step"], 1)
    dve.wait_ge(s["bn_step"], 4)
    dve.tensor_tensor(shift[:, :], moments[:, 0:1], scale[:, :], ALU.mult).then_inc(s["bn_step"], 1)
    dve.wait_ge(s["bn_step"], 5)
    dve.tensor_tensor(shift[:, :], beta, shift[:, :], ALU.subtract).then_inc(s["bn_step"], 1)


def feed_forward(g, s):
    nc = g.nc
    with ExitStack() as ctx:
        def sb(name, shape, dt=F32):
            return ctx.enter_context(nc.sbuf_tensor(f"{name}_z", shape, dt))

        def ps(name):
            return ctx.enter_context(nc.psum_tensor(f"{name}_z", [P, 512], F32))

        moments = sb("moments", [P, 2])
        scale = sb("scale", [P, 1])
        shift = sb("shift", [P, 1])
        y_in = [sb(f"y_in{b}", [P, BLOCK]) for b in range(2)]
        h_in = [sb(f"h_in{b}", [P, BLOCK]) for b in range(2)]
        hidden = [[sb(f"hidden{h}{m}", [P, HALF]) for m in range(2)] for h in range(2)]
        z = [sb(f"z{b}", [P, BLOCK]) for b in range(2)]
        ps_hidden = [[ps(f"ps_hidden{h}{m}") for m in range(2)] for h in range(2)]
        ps_out = [ps(f"ps_out{h}") for h in range(2)]
        block = ctx.enter_context(nc.Block())

        @block.sync
        def _(sp):
            def load(n, i, b, last):
                sp.wait_ge(s["y_normed"][b], i)
                gate(g, sp)
                sp.dma_start(y_in[b][:, :], g.turned_table[bass.ds(n * P, P), :]).then_inc(s["y_loaded"][b], 16)

            over_blocks(g, sp, load)

        @block.scalar
        def _(act):
            batch_norm_coefficients(g, None, act, s, 0, moments, scale, shift)
            act.wait_ge(s["bn_step"], 6)

            def body(n, i, b, last):
                act.wait_ge(s["y_loaded"][b], i * 16 + 16)
                act.wait_ge(s["z_measured"][b], i)
                act.activation(h_in[b][:, :], y_in[b][:, :], ACT.Identity, bias=shift[:, 0:1],
                               scale=scale[:, 0:1]).then_inc(s["y_normed"][b], 1)
                for h in range(2):
                    act.wait_ge(s["ff_hidden"][h], n + 1)
                    act.activation(hidden[h][0][:, :], ps_hidden[h][0][:, :], ACT.Relu,
                                   bias=g.b1_col[:, 0:1]).then_inc(s["ff_rectified0"][h], 1)

            over_blocks(g, act, body)

        @block.tensor
        def _(pe):
            def body(n, i, b, last):
                pe.wait_ge(s["y_normed"][b], i + 1)
                for h in range(2):
                    pe.wait_ge(s["ff_rectified0"][h], n)
                    pe.wait_ge(s["ff_rectified1"][h], n)
                    for m in range(2):
                        mm = pe.matmul(ps_hidden[h][m][:, :], g.W1_sb[:, m * D:(m + 1) * D],
                                       h_in[b][:, h * HALF:(h + 1) * HALF], start=True, stop=True)
                    mm.then_inc(s["ff_hidden"][h], 1)
                for h in range(2):
                    pe.wait_ge(s["ff_rectified0"][h], n + 1)
                    pe.wait_ge(s["ff_rectified1"][h], n + 1)
                    pe.wait_ge(s["z_ready"][h], n)
                    for m in range(2):
                        mm = pe.matmul(ps_out[h][:, :], g.W2_sb[:, m, :], hidden[h][m][:, :],
                                       start=(m == 0), stop=(m == 1))
                    mm.then_inc(s["ff_out"][h], 1)

            over_blocks(g, pe, body)

        @block.vector
        def _(dve):
            batch_norm_coefficients(g, dve, None, s, 0, moments, scale, shift)

            def body(n, i, b, last):
                for h in range(2):
                    dve.wait_ge(s["ff_hidden"][h], n + 1)
                    dve.tensor_scalar(hidden[h][1][:, :], ps_hidden[h][1][:, :], g.b1_col[:, 1:2], 0.0, ALU.add,
                                      ALU.max).then_inc(s["ff_rectified1"][h], 1)
                for h in range(2):
                    dve.wait_ge(s["ff_out"][h], n + 1)
                    dve.wait_ge(s["z_stored"][b], i * 16)
                    cols = slice(h * HALF, (h + 1) * HALF)
                    dve.scalar_tensor_tensor(out=z[b][:, cols], in0=ps_out[h][:, :], scalar=g.b2_col[:, 0:1],
                                             in1=h_in[b][:, cols], op0=ALU.add,
                                             op1=ALU.add).then_inc(s["z_ready"][h], 1)
                for h in range(2):
                    dve.wait_ge(s["z_ready"][h], n + 1)
                    measured = measure(g, dve, z[b], n, h, last)
                measured.then_inc(s["z_measured"][b], 1)

            over_blocks(g, dve, body)

        @block.gpsimd
        def _(pool):
            def store(n, i, b, last):
                for h in range(2):
                    pool.wait_ge(s["z_ready"][h], n + 1)
                gate(g, pool)
                pool.dma_start(g.turned_table[bass.ds(n * P, P), :], z[b][:, :]).then_inc(s["z_stored"][b], 16)

            over_blocks(g, pool, store)
            for b in range(2):
                pool.wait_ge(s["z_stored"][b], 16 * ((g.BLOCKS + 1 - b) // 2))


def finish_output(g, s):
    nc = g.nc
    with ExitStack() as ctx:
        def sb(name, shape, dt=F32):
            return ctx.enter_context(nc.sbuf_tensor(f"{name}_o", shape, dt))

        moments = sb("bn_moments", [P, 2])
        scale = sb("scale", [P, 1])
        shift = sb("shift", [P, 1])
        z_in = [sb(f"z_in{b}", [P, BLOCK]) for b in range(2)]
        x1_in = [sb(f"x1_in{b}", [P, BLOCK]) for b in range(2)]
        normed = [sb(f"normed{b}", [P, BLOCK]) for b in range(2)]
        total = [sb(f"total{b}", [P, BLOCK]) for b in range(2)]
        stats = sb("stats", [P, ROWS, 6])
        row_moments = sb("moments", [P, ROWS, 2])
        root = sb("root", [P, ROWS, 1])
        inverse = sb("inverse", [P, ROWS, 1])
        minus_mean = sb("minus_mean", [P, ROWS, 1])
        rows_out = [sb(f"rows_out{b}", [P, BLOCK]) for b in range(2)]
        ps_turn = [ctx.enter_context(nc.psum_tensor(f"ps_turn_o{h}", [P, 512], F32)) for h in range(2)]
        pieces = parts_of(g.TAIL_PARTS)
        block = ctx.enter_context(nc.Block())

        @block.sync
        def _(sp):
            def load(n, i, b, last):
                sp.wait_ge(s["z_normed"][b], i)
                gate(g, sp)
                sp.dma_start(z_in[b][:, :], g.turned_table[bass.ds(n * P, P), :]).then_inc(s["z_loaded"][b], 16)
                sp.wait_ge(s["residual_added"][b], i)
                gate(g, sp)
                sp.dma_start(x1_in[b][:, :], rows_of(g.x1_table, n * BLOCK)).then_inc(s["x1_loaded"][b], 16)

            over_blocks(g, sp, load)

        @block.scalar
        def _(act):
            batch_norm_coefficients(g, None, act, s, 1, moments, scale, shift)
            act.wait_ge(s["bn_step"], 6)

            def norm(i, b):
                act.wait_ge(s["z_loaded"][b], i * 16 + 16)
                act.wait_ge(s["residual_added"][b], i)
                act.activation(normed[b][:, :], z_in[b][:, :], ACT.Identity, bias=shift[:, 0:1],
                               scale=scale[:, 0:1]).then_inc(s["z_normed"][b], 1)

            norm(0, 0)

            def body(n, i, b, last):
                if not last:
                    norm(i + b, 1 - b)
                act.wait_ge(s["row_moments"], n + 1)
                act.wait_ge(s["normed"][1 - b], i + b)
                act.activation(root[:, :, :], row_moments[:, :, 1:2], ACT.Sqrt,
                               bias=g.eps_col[:, 0:1]).then_inc(s["rooted"], 1)
                act.wait_ge(s["shifts_ready"], n + 1)
                act.wait_ge(s["out_stored"][b], i * 16)
                for r in range(ROWS):
                    row = slice(r * D, (r + 1) * D)
                    last_row = act.activation(rows_out[b][:, row], total[b][:, row], ACT.Identity,
                                              bias=minus_mean[:, r, :], scale=inverse[:, r, :])
                last_row.then_inc(s["normed"][b], 1)

            over_blocks(g, act, body)

        @block.tensor
        def _(pe):
            def body(n, i, b, last):
                pe.wait_ge(s["z_normed"][b], i + 1)
                pe.wait_ge(s["residual_added"][1 - b], i + b)
                for h in range(2):
                    for r in range(4):
                        at = (4 * h + r) * D
                        mm = pe.transpose(ps_turn[h][:, r * D:(r + 1) * D], normed[b][:, at:at + D], g.ident[:, :])
                mm.then_inc(s["z_turned"], 1)

            over_blocks(g, pe, body)

        @block.vector
        def _(dve):
            batch_norm_coefficients(g, dve, None, s, 1, moments, scale, shift)

            def body(n, i, b, last):
                dve.wait_ge(s["z_turned"], n + 1)
                dve.wait_ge(s["x1_loaded"][b], i * 16 + 16)
                dve.wait_ge(s["shifts_ready"], n)
                dve.wait_ge(s["normed"][b], i)
                for h in range(2):
                    cols = slice(h * HALF, (h + 1) * HALF)
                    add = dve.tensor_tensor(total[b][:, cols], ps_turn[h][:, :], x1_in[b][:, cols], ALU.add)
                add.then_inc(s["residual_added"][b], 1)
                dve.wait_ge(s["residual_added"][b], i + 1)
                row_statistics(g, dve, s, total[b], stats, row_moments, n)
                dve.wait_ge(s["rooted"], n + 1)
                dve.reciprocal(inverse[:, :, :], root[:, :, :]).then_inc(s["inverted"], 1)
                dve.wait_ge(s["inverted"], n + 1)
                dve.scalar_tensor_tensor(out=minus_mean[:, :, :], in0=row_moments[:, :, 0:1], scalar=-1.0,
                                         in1=inverse[:, :, :], op0=ALU.mult,
                                         op1=ALU.mult).then_inc(s["shifts_ready"], 1)

            over_blocks(g, dve, body)

        @block.gpsimd
        def _(pool):
            def store(n, i, b, last):
                pool.wait_ge(s["normed"][b], i + 1)
                gate(g, pool)
                for a, z in pieces if last else [(0, P)]:
                    pool.dma_start(rows_of(g.out, n * BLOCK + a * ROWS, (z - a) * ROWS), rows_out[b][a:z, :]
                                   ).then_inc(s["out_stored"][b], 16)

            over_blocks(g, pool, store)
            pool.wait_ge(s["out_stored"][0], 16 * (g.BLOCKS // 2 + len(pieces)))
            pool.wait_ge(s["out_stored"][1], 16 * (g.BLOCKS // 2))


def gnn_then_transformer(nc, **args):
    with ExitStack() as ctx:
        g = Graph(nc, ctx, args)

        cleared = []

        def cleared_sem(name):
            cleared.append(nc.alloc_semaphore(name))
            return cleared[-1]

        def clear():
            nc.clear_and_free_semaphores(list(cleared))
            cleared.clear()
            nc.all_engine_barrier()

        def sems(prefix, pairs="", singles="", quads="", tiles=""):
            made = {n: [cleared_sem(f"{prefix}_{n}{b}") for b in range(2)] for n in pairs.split()}
            made |= {n: [[cleared_sem(f"{prefix}_{n}{b}{h}") for h in range(2)] for b in range(2)]
                     for n in quads.split()}
            made |= {n: [[cleared_sem(f"{prefix}_{n}{b}{j}") for j in range(TILES)] for b in range(2)]
                     for n in tiles.split()}
            return made | {n: cleared_sem(f"{prefix}_{n}") for n in singles.split()}

        setup(g)
        start_sums(g)
        messages = sems("m", "gathered numbers_ready result_ready same_ready offsets_loaded turn_copied "
                             "ends_turned hidden_ready hidden_summed windows_loaded target_rows_found "
                             "target_rows_picked",
                        "messages_ready messages_summed combined zeros_made zeros_stored", tiles="scattered")
        nodes = sems("u", "rectified sums_loaded h_stored h_turned h_copied sum_ready h_projected sums_stored")
        with nc.sbuf_tensor("zeros", [P, TILES * AT], F32) as zeros:
            with nc.Block() as block:
                @block.vector
                def _(dve):
                    dve.memset(zeros[:, :], 0.0).then_inc(messages["zeros_made"], 1)

                @block.sync
                def _(sp):
                    sp.wait_ge(messages["zeros_made"], 1)
                    gate(g, sp)
                    sp.dma_start(rows_of(g.sums, g.SPARE_ROWS, GROUP, TILES), zeros[:, 0:TILES * D]
                                 ).then_inc(messages["zeros_stored"], 16)
                    sp.dma_start(rows_of(g.attn_sums, g.SPARE_ROWS, GROUP, TILES), zeros[:, :]
                                 ).then_inc(messages["zeros_stored"], 16)
                    sp.wait_ge(messages["zeros_stored"], 32)
            pass_messages(g, messages, 0, g.x, zeros[:, :])
        for k in range(1, 3):
            update_nodes(g, nodes, k - 1)
            pass_messages(g, messages, k, g.h_table[:, :])
        clear()
        finish_messages(g, sems("f", "sums_loaded x_loaded x1_stored x1_copied residual_added q_copied kv_copied "
                                     "qkv_ready q_stored kv_stored",
                                "row_stats row_moments rooted inverted normed", "x1_turned"))
        attend(g, sems("t", "gathered numbers_ready result_ready same_ready offsets_loaded edges_loaded "
                            "windows_loaded target_rows_found target_rows_picked",
                       "edges_turned edges_copied edges_used edges_projected values_weighted combined clipped "
                       "weights_ready multiplied scored scaled", tiles="scattered"))
        clear()
        finish_attention(g, sems("y", "sums_loaded x1_loaded y_copied y_stored y_summed measured",
                                 "mean_ready weights_summed inverted", "y_turned"))
        feed_forward(g, sems("z", "y_loaded y_normed ff_hidden ff_rectified0 ff_rectified1 z_ready ff_out z_stored z_measured",
                             "bn_step"))
        finish_output(g, sems("o", "z_loaded x1_loaded z_normed out_stored residual_added normed",
                              "bn_step z_turned row_stats row_moments rooted inverted shifts_ready"))


_INS = ['x', 'src', 'dst', 'edge_attr_128', 'L0_gnn_Wm1', 'L0_gnn_bm1', 'L0_gnn_Wm2', 'L0_gnn_bm2', 'L0_gnn_Wn',
        'L0_gnn_bn', 'L1_gnn_WQ', 'L1_gnn_WK', 'L1_gnn_WV', 'L1_gnn_WE', 'L1_gnn_gamma1', 'L1_gnn_beta1',
        'L1_gnn_gamma2', 'L1_gnn_beta2', 'L1_gnn_W1', 'L1_gnn_b1', 'L1_gnn_W2', 'L1_gnn_b2']


def kernel(**inputs):
    import numpy as _np
    import concourse.bacc as _bacc
    from concourse import mybir as _mybir
    from concourse.bass_utils import run_bass_kernel_spmd as _run

    nc = _bacc.Bacc("TRN2", target_bir_lowering=False, num_devices=1)
    arrays, args = {}, {}
    for name in _INS:
        a = _np.ascontiguousarray(inputs[name])
        arrays[f"in_{name}_dram"] = a
        args[name] = nc.dram_tensor(f"in_{name}_dram", a.shape, _mybir.dt.from_np(a.dtype),
                                    kind="ExternalInput").ap()
    args["out"] = nc.dram_tensor("out_dram", inputs["x"].shape, _mybir.dt.float32, kind="ExternalOutput").ap()
    gnn_then_transformer(nc, **args)
    r = _run(nc, [arrays], core_ids=[0])
    return r.results[0]["out_dram"]
```

```python
from contextlib import ExitStack

import concourse.bass as bass
from concourse import mybir

F32 = mybir.dt.float32
I32 = mybir.dt.int32
ALU = mybir.AluOpType
ACT = mybir.ActivationFunctionType
AX = mybir.AxisListType

P = 128
D = 128
ROWS = 8
BLOCK = P * ROWS
HALF = BLOCK // 2
TILES = 4
GROUP = P * TILES
CHUNKS = 3
WINDOW = P * CHUNKS
HEADS = 8
DH = D // HEADS
AT = D + HEADS
LN_EPS = 1e-5
BN_EPS = 1e-5
ATTN_EPS = 1e-6
CLIP = 5.0


def rows_of(table, first, n=BLOCK, rows=ROWS):
    return table[bass.ds(first, n), :].rearrange("(p r) c -> p (r c)", r=rows)


def parts_of(n):
    whole = n - n % 16
    return [(a, b) for a, b in ((0, whole), (whole, n)) if b > a]


def loop(eng, first, end):
    if end > first:
        yield first
    if end > first + 1:
        with eng.Fori(first + 1, end) as i:
            yield i


def gate(g, eng):
    eng.sem_inc(g.gates[eng.engine], 1)


class Graph:

    def __init__(self, nc, ctx, args):
        self.nc = nc
        self.x = args["x"]
        self.src = args["src"]
        self.dst = args["dst"]
        self.edge_attr_128 = args["edge_attr_128"]
        self.L0_gnn_Wm1 = args["L0_gnn_Wm1"]
        self.L0_gnn_bm1 = args["L0_gnn_bm1"]
        self.L0_gnn_Wm2 = args["L0_gnn_Wm2"]
        self.L0_gnn_bm2 = args["L0_gnn_bm2"]
        self.L0_gnn_Wn = args["L0_gnn_Wn"]
        self.L0_gnn_bn = args["L0_gnn_bn"]
        self.L1_gnn_WQ = args["L1_gnn_WQ"]
        self.L1_gnn_WK = args["L1_gnn_WK"]
        self.L1_gnn_WV = args["L1_gnn_WV"]
        self.L1_gnn_WE = args["L1_gnn_WE"]
        self.L1_gnn_gamma1 = args["L1_gnn_gamma1"]
        self.L1_gnn_beta1 = args["L1_gnn_beta1"]
        self.L1_gnn_gamma2 = args["L1_gnn_gamma2"]
        self.L1_gnn_beta2 = args["L1_gnn_beta2"]
        self.L1_gnn_W1 = args["L1_gnn_W1"]
        self.L1_gnn_b1 = args["L1_gnn_b1"]
        self.L1_gnn_W2 = args["L1_gnn_W2"]
        self.L1_gnn_b2 = args["L1_gnn_b2"]
        self.out = args["out"]
        self.N = self.x.shape[0]
        self.E = self.src.shape[0]
        self.BLOCKS = -(-self.N // BLOCK)
        self.GROUPS = -(-self.E // GROUP)
        self.NP = self.BLOCKS * BLOCK
        self.EP = self.GROUPS * GROUP
        self.QUARTER = self.GROUPS * P
        self.TAIL_PARTS = (self.N - (self.BLOCKS - 1) * BLOCK) // ROWS
        self.RESIDENT = min(34, self.BLOCKS - 3)
        self.TAIL_EDGES = self.E - 3 * self.QUARTER - (self.GROUPS - 2) * P
        self.FILL_ROW = self.N
        self.SPARE_ROWS = self.NP
        assert self.N % ROWS == 0 and self.BLOCKS % 2 == 1 and self.BLOCKS > 2
        assert self.GROUPS == 2 * self.BLOCKS and 0 < self.TAIL_EDGES < P
        assert self.FILL_ROW < self.NP and self.N >= WINDOW

        def dram(name, shape, dt=F32):
            return nc.dram_tensor(name, shape, dt)

        self.gates = {eng.engine: ctx.enter_context(nc.semaphore(f"gate{n}"))
                      for n, eng in enumerate((nc.gpsimd, nc.sync, nc.vector))}
        self.sums = [dram(f"sums{t}", (self.NP + GROUP, D)) for t in range(2)]
        self.attn_sums = dram("attn_sums", (self.NP + GROUP, AT))
        self.x1_table = dram("x1_table", (self.NP, D))
        self.turned_table = dram("turned_table", (self.BLOCKS * P, BLOCK))
        self.offset_table = dram("offset_table", (self.EP,), I32)
        self.base_table = dram("base_table", (self.GROUPS * TILES,), I32)

        def sb(name, shape, dt=F32):
            return ctx.enter_context(nc.sbuf_tensor(name, shape, dt))

        self.ident = sb("ident", [P, P])
        self.Wm1_sb = sb("Wm1_sb", [P, 2, 2 * D])
        self.Wm2n_sb = sb("Wm2n_sb", [P, 2, D])
        self.Wna_sb = sb("Wna_sb", [P, D])
        self.Wqkv_sb = sb("Wqkv_sb", [P, 3 * D])
        self.WE_sb = sb("WE_sb", [P, D])
        self.W1_sb = sb("W1_sb", [P, 2 * D])
        self.W2_sb = sb("W2_sb", [P, 2, D])
        self.bm1_col = sb("bm1_col", [P, 2])
        self.b1_col = sb("b1_col", [P, 2])
        self.b2_col = sb("b2_col", [P, 1])
        self.bn_all = sb("bn_all", [P, D])
        self.bm2n_all = sb("bm2n_all", [P, D])
        self.gammas = sb("gammas", [P, 2])
        self.betas = sb("betas", [P, 2])
        self.eps_col = sb("eps_col", [P, 1])
        self.gather_rows = sb("gather_rows", [P, self.GROUPS + 2, 2 * TILES], I32)
        self.scatter_rows = sb("scatter_rows", [P, self.GROUPS, TILES], I32)
        self.dst_col = sb("dst_col", [P, self.GROUPS, TILES])
        self.offset_col = sb("offset_col", [P, self.GROUPS, TILES])
        self.bases = sb("bases", [1, self.GROUPS * TILES], I32)
        self.windowed = sb("windowed", [1, 1], I32)
        self.window_row = sb("window_row", [P, CHUNKS])
        self.earlier = sb("earlier", [P, P])
        self.to_spare = sb("to_spare", [P, self.GROUPS, TILES])
        self.feature_stats = sb("feature_stats", [P, self.GROUPS, 6])


def setup(g):
    nc = g.nc
    G = g.GROUPS
    with ExitStack() as ctx:
        def sb(name, shape, dt=F32):
            return ctx.enter_context(nc.sbuf_tensor(name, shape, dt))

        sems = []

        def sem(name):
            sems.append(nc.alloc_semaphore(name))
            return sems[-1]

        Wm2_rows = sb("Wm2_rows", [P, 2, D])
        Wm2_turned = sb("Wm2_turned", [P, 2 * D])
        Wnb = sb("Wnb", [P, D])
        bm2_col = sb("bm2_col", [P, 1])
        bm2_wide = sb("bm2_wide", [P, P])
        ones = sb("ones", [P, P])
        edge_rows = sb("edge_rows", [P, 2, GROUP], I32)
        edge_rows_f = sb("edge_rows_f", [P, 2, GROUP])
        base_rows = sb("base_rows", [P, TILES])
        base_rows_i = sb("base_rows_i", [P, TILES], I32)
        offsets = sb("offsets", [P, GROUP])
        offsets_i = sb("offsets_i", [P, GROUP], I32)
        beyond = sb("beyond", [P, GROUP])
        outside = sb("outside", [P, GROUP])
        outside_real = sb("outside_real", [P, GROUP])
        misses = sb("misses", [P, 1])
        highest = sb("highest", [P, TILES])
        lowest = sb("lowest", [P, TILES])
        crossed = sb("crossed", [P, TILES - 1])
        crossings = sb("crossings", [P, 1])
        window_row_i = sb("window_row_i", [P, CHUNKS], I32)
        clipped = sb("clipped", [P, TILES, G])
        ps_offsets = ctx.enter_context(nc.psum_tensor("ps_offsets", [P, TILES, P], F32))
        ps_misses = ctx.enter_context(nc.psum_tensor("ps_misses", [P, 1], F32))
        ps_edges = ctx.enter_context(nc.psum_tensor("ps_edges", [P, 2, TILES, P], F32))
        ps_turn = ctx.enter_context(nc.psum_tensor("ps_turn", [P, 512], F32))
        ps_fold = ctx.enter_context(nc.psum_tensor("ps_fold", [P, 512], F32))

        filled = sem("filled")
        ones_ready = sem("ones_ready")
        ident_ready = sem("ident_ready")
        ends_loaded = sem("ends_loaded")
        window_rows_made = sem("window_rows_made")
        bases_ready = sem("bases_ready")
        offsets_ready = sem("offsets_ready")
        offsets_written = sem("offsets_written")
        bases_written = sem("bases_written")
        bases_loaded = sem("bases_loaded")
        misses_ready = sem("misses_ready")
        misses_summed = sem("misses_summed")
        weights_loaded = sem("weights_loaded")
        ends_converted = sem("ends_converted")
        ends_turned = sem("ends_turned")
        dst_clipped = sem("dst_clipped")
        rows_ready = sem("rows_ready")
        wm2_turned = sem("wm2_turned")
        fold_inputs = sem("fold_inputs")
        folded = sem("folded")
        fold_copied = sem("fold_copied")
        block = ctx.enter_context(nc.Block())

        def column(v):
            return v.rearrange("(a p) -> p a", p=P)

        loads = [
            (Wm2_rows[:, :, :], g.L0_gnn_Wm2.rearrange("(a p) n -> p a n", p=P)),
            (Wnb[:, :], g.L0_gnn_Wn[D:2 * D, :]),
            (bm2_col[:, :], column(g.L0_gnn_bm2)),
            (g.Wna_sb[:, :], g.L0_gnn_Wn[0:D, :]),
            (g.Wm1_sb[:, :, :], g.L0_gnn_Wm1.rearrange("(a p) n -> p a n", p=P)),
            (g.bm1_col[:, :], column(g.L0_gnn_bm1)),
            (g.bn_all[:, :], g.L0_gnn_bn.partition_broadcast(P)),
            (g.Wqkv_sb[:, 0:D], g.L1_gnn_WQ),
            (g.Wqkv_sb[:, D:2 * D], g.L1_gnn_WK),
            (g.Wqkv_sb[:, 2 * D:3 * D], g.L1_gnn_WV),
            (g.WE_sb[:, :], g.L1_gnn_WE),
            (g.W1_sb[:, :], g.L1_gnn_W1),
            (g.W2_sb[:, :, :], g.L1_gnn_W2.rearrange("(a p) n -> p a n", p=P)),
            (g.b1_col[:, :], column(g.L1_gnn_b1)),
            (g.b2_col[:, :], column(g.L1_gnn_b2)),
            (g.gammas[:, 0:1], column(g.L1_gnn_gamma1)),
            (g.gammas[:, 1:2], column(g.L1_gnn_gamma2)),
            (g.betas[:, 0:1], column(g.L1_gnn_beta1)),
            (g.betas[:, 1:2], column(g.L1_gnn_beta2)),
        ]

        @block.sync
        def _(sp):
            sp.wait_ge(filled, 2)
            for k, ends in enumerate((g.src, g.dst)):
                sp.dma_start(edge_rows[0:G, k, 0:3 * P].rearrange("g (j q) -> g j q", q=P),
                             ends[0:3 * g.QUARTER].rearrange("(j g q) -> g j q", j=3, q=P)
                             ).then_inc(ends_loaded, 16)
                sp.dma_start(edge_rows[0:G - 2, k, 3 * P:GROUP],
                             ends[3 * g.QUARTER:g.E - g.TAIL_EDGES].rearrange("(g q) -> g q", q=P)
                             ).then_inc(ends_loaded, 16)
                sp.dma_start(edge_rows[G - 2:G - 1, k, 3 * P:3 * P + g.TAIL_EDGES],
                             ends[g.E - g.TAIL_EDGES:g.E].rearrange("(g q) -> g q", g=1)
                             ).then_inc(ends_loaded, 16)
            sp.wait_ge(offsets_ready, 2)
            gate(g, sp)
            sp.dma_start(g.offset_table.rearrange("(g e) -> g e", e=GROUP), offsets_i[0:G, :]
                         ).then_inc(offsets_written, 16)
            sp.wait_ge(bases_ready, 2)
            gate(g, sp)
            sp.dma_start(g.base_table.rearrange("(g j) -> g j", j=TILES), base_rows_i[0:G, :]
                         ).then_inc(bases_written, 16)
            sp.wait_ge(bases_written, 16)
            gate(g, sp)
            sp.dma_start(g.bases[:, :], g.base_table.rearrange("(a t) -> a t", a=1)).then_inc(bases_loaded, 16)
            sp.wait_ge(offsets_written, 16)
            sp.wait_ge(bases_loaded, 16)

        @block.gpsimd
        def _(pool):
            pool.memset(ones[:, :], 1.0).then_inc(ones_ready, 1)
            pool.wait_ge(ones_ready, 1)
            pool.affine_select(out=g.ident[:, :], in_=ones[:, :], compare_op=ALU.is_equal, fill=0.0, base=0,
                               pattern=[[-1, P]], channel_multiplier=1).then_inc(ident_ready, 1)
            pool.iota(window_row_i[:, :], pattern=[[1, CHUNKS]], base=0,
                      channel_multiplier=CHUNKS).then_inc(window_rows_made, 1)

        @block.scalar
        def _(act):
            for to, of in loads:
                act.dma_start(to, of, allow_slow_non_contiguous=True).then_inc(weights_loaded, 16)
            act.wait_ge(weights_loaded, 16 * len(loads))
            act.wait_ge(ones_ready, 1)
            act.activation(bm2_wide[:, :], ones[:, :], ACT.Copy, scale=bm2_col[:, 0:1]).then_inc(fold_inputs, 1)
            act.wait_ge(wm2_turned, 1)
            act.copy(Wm2_turned[:, :], ps_turn[:, 0:2 * D]).then_inc(fold_inputs, 1)

        @block.tensor
        def _(pe):
            pe.wait_ge(ident_ready, 1)
            pe.wait_ge(ends_converted, 1)
            for k in range(2):
                for j in range(TILES):
                    last = pe.transpose(ps_edges[:, k, j, 0:G], edge_rows_f[0:G, k, j * P:(j + 1) * P],
                                        g.ident[0:G, 0:G])
            last.then_inc(ends_turned, 1)
            pe.wait_ge(offsets_ready, 1)
            for j in range(TILES):
                last = pe.transpose(ps_offsets[:, j, 0:G], offsets[0:G, j * P:(j + 1) * P], g.ident[0:G, 0:G])
            last.then_inc(ends_turned, 1)
            pe.wait_ge(misses_ready, 6)
            pe.matmul(ps_misses[0:1, 0:1], misses[0:G, :], ones[0:G, 0:1], start=True, stop=False)
            pe.matmul(ps_misses[0:1, 0:1], crossings[0:G, :], ones[0:G, 0:1], start=False,
                      stop=True).then_inc(misses_summed, 1)
            pe.wait_ge(weights_loaded, 16 * len(loads))
            for m in range(2):
                last = pe.transpose(ps_turn[:, m * D:(m + 1) * D], Wm2_rows[:, m, :], g.ident[:, :])
            last.then_inc(wm2_turned, 1)
            pe.wait_ge(fold_inputs, 2)
            for m in range(2):
                pe.matmul(ps_fold[:, m * D:(m + 1) * D], Wm2_turned[:, m * D:(m + 1) * D], Wnb[:, :],
                          start=True, stop=True)
            pe.matmul(ps_fold[:, 2 * D:3 * D], bm2_wide[:, :], Wnb[:, :], start=True, stop=True).then_inc(folded, 1)

        @block.vector
        def _(dve):
            dve.memset(edge_rows[:, 0, :], 0).then_inc(filled, 1)
            dve.memset(edge_rows[:, 1, :], g.FILL_ROW).then_inc(filled, 1)
            dve.memset(g.eps_col[:, :], LN_EPS)
            dve.memset(g.gather_rows[:, :, :], 0).then_inc(rows_ready, 1)
            dve.wait_ge(ends_loaded, 96)
            dve.tensor_copy(edge_rows_f[0:G, :, :], edge_rows[0:G, :, :]).then_inc(ends_converted, 1)
            dve.wait_ge(ends_converted, 1)
            dve.tensor_scalar(base_rows[0:G, :], edge_rows_f[0:G, 1, 0:GROUP:P], float(g.N - WINDOW), None,
                              ALU.min).then_inc(bases_ready, 1)
            dve.wait_ge(bases_ready, 1)
            dve.tensor_copy(base_rows_i[0:G, :], base_rows[0:G, :]).then_inc(bases_ready, 1)
            dve.tensor_tensor(offsets[0:G, :].rearrange("p (j q) -> p j q", q=P),
                              edge_rows_f[0:G, 1, :].rearrange("p (j q) -> p j q", q=P),
                              base_rows[0:G, :].unsqueeze(2).broadcast_to([G, TILES, P]),
                              ALU.subtract).then_inc(offsets_ready, 1)
            dve.wait_ge(offsets_ready, 1)
            dve.tensor_copy(offsets_i[0:G, :], offsets[0:G, :]).then_inc(offsets_ready, 1)
            dve.tensor_scalar(beyond[0:G, :], offsets[0:G, :], float(WINDOW - 1), None,
                              ALU.is_gt).then_inc(misses_ready, 1)
            dve.wait_ge(misses_ready, 1)
            dve.scalar_tensor_tensor(out=outside[0:G, :], in0=offsets[0:G, :], scalar=0.0, in1=beyond[0:G, :],
                                     op0=ALU.is_lt, op1=ALU.max).then_inc(misses_ready, 1)
            dve.wait_ge(misses_ready, 2)
            dve.scalar_tensor_tensor(out=outside_real[0:G, :], in0=edge_rows_f[0:G, 1, :],
                                     scalar=float(g.FILL_ROW), in1=outside[0:G, :], op0=ALU.is_lt, op1=ALU.mult,
                                     accum_out=misses[0:G, :]).then_inc(misses_ready, 1)
            by_edge = edge_rows_f[0:G, 1, :].rearrange("p (j q) -> p j q", q=P)
            dve.tensor_reduce(highest[0:G, :], by_edge, AX.X, ALU.max).then_inc(misses_ready, 1)
            dve.tensor_reduce(lowest[0:G, :], by_edge, AX.X, ALU.min).then_inc(misses_ready, 1)
            dve.wait_ge(misses_ready, 5)
            dve.scalar_tensor_tensor(out=crossed[0:G, :], in0=highest[0:G, 0:TILES - 1], scalar=1.0,
                                     in1=lowest[0:G, 1:TILES], op0=ALU.mult, op1=ALU.is_ge,
                                     accum_out=crossings[0:G, :]).then_inc(misses_ready, 1)
            dve.wait_ge(misses_summed, 1)
            dve.tensor_scalar(g.windowed[:, :], ps_misses[0:1, 0:1], 0.0, None, ALU.is_equal)
            dve.wait_ge(window_rows_made, 1)
            dve.tensor_copy(g.window_row[:, :], window_row_i[:, :])
            dve.wait_ge(ends_turned, 2)
            dve.tensor_copy(g.offset_col[:, :, :].rearrange("p g t -> p t g"), ps_offsets[:, :, 0:G])
            dve.wait_ge(rows_ready, 1)
            by_tile = g.gather_rows[:, 0:G, :].rearrange("p g t -> p t g")
            dve.tensor_copy(by_tile[:, 0:TILES, :], ps_edges[:, 0, :, 0:G])
            dve.tensor_copy(g.dst_col[:, :, :].rearrange("p g t -> p t g"), ps_edges[:, 1, :, 0:G])
            dve.tensor_scalar(clipped[:, :, :], ps_edges[:, 1, :, 0:G], float(g.N - 1), None,
                              ALU.min).then_inc(dst_clipped, 1)
            dve.wait_ge(dst_clipped, 1)
            dve.tensor_copy(by_tile[:, TILES:2 * TILES, :], clipped[:, :, :])
            dve.wait_ge(folded, 1)
            dve.tensor_copy(g.Wm2n_sb[:, :, :], ps_fold[:, 0:2 * D].rearrange("p (a n) -> p a n", a=2))
            dve.tensor_copy(g.bm2n_all[:, :], ps_fold[:, 2 * D:3 * D]).then_inc(fold_copied, 1)
    nc.clear_and_free_semaphores(sems)
    nc.all_engine_barrier()


def start_sums(g):
    nc = g.nc
    with ExitStack() as ctx:
        def sb(name, shape, dt=F32):
            return ctx.enter_context(nc.sbuf_tensor(name, shape, dt))

        sems = []

        def sem(name):
            sems.append(nc.alloc_semaphore(name))
            return sems[-1]

        x_in = [sb(f"x_in{b}", [P, BLOCK]) for b in range(2)]
        turned = [sb(f"turned{h}", [P, HALF]) for h in range(2)]
        new_sums = [sb(f"new_sums{b}", [P, BLOCK]) for b in range(2)]
        ones = sb("ones_a", [P, P])
        spare_i = sb("spare_i", [P, TILES], I32)
        spare = sb("spare", [P, TILES])
        ps_turn = [ctx.enter_context(nc.psum_tensor(f"ps_turn_a{h}", [P, 512], F32)) for h in range(2)]
        ps_sum = [ctx.enter_context(nc.psum_tensor(f"ps_sum_a{h}", [P, 512], F32)) for h in range(2)]

        x_loaded = [sem(f"x_loaded{b}") for b in range(2)]
        x_turned = [[sem(f"x_turned{b}{h}") for h in range(2)] for b in range(2)]
        x_copied = [sem(f"x_copied{h}") for h in range(2)]
        projected = [sem(f"projected{h}") for h in range(2)]
        bias_added = [sem(f"bias_added{h}") for h in range(2)]
        sums_stored = [sem(f"sums_stored{b}") for b in range(2)]
        earlier_ready = sem("earlier_ready")
        spare_ready = sem("spare_ready")
        pieces = parts_of(g.TAIL_PARTS)
        block = ctx.enter_context(nc.Block())

        @block.sync
        def _(sp):
            def load(i, b, last=False):
                n = i * 2 + b
                sp.wait_ge(x_turned[b][1], i)
                gate(g, sp)
                if last:
                    for a, z in pieces:
                        sp.dma_start(x_in[b][a:z, :], rows_of(g.x, n * BLOCK + a * ROWS, (z - a) * ROWS)
                                     ).then_inc(x_loaded[b], 16)
                else:
                    sp.dma_start(x_in[b][:, :], rows_of(g.x, n * BLOCK)).then_inc(x_loaded[b], 16)

            for i in loop(sp, 0, g.BLOCKS // 2):
                load(i, 0)
                load(i, 1)
            load(g.BLOCKS // 2, 0, last=True)

        @block.tensor
        def _(pe):
            def body(i, b, last=False):
                n = i * 2 + b
                pe.wait_ge(x_loaded[b], i * 16 + 16 * (len(pieces) if last else 1))
                for h in range(2):
                    pe.wait_ge(x_copied[h], n)
                    for r in range(4):
                        at = (4 * h + r) * D
                        mm = pe.transpose(ps_turn[h][:, r * P:(r + 1) * P], x_in[b][:, at:at + D], g.ident[:, :])
                    mm.then_inc(x_turned[b][h], 1)
                for h in range(2):
                    pe.wait_ge(x_copied[h], n + 1)
                    pe.wait_ge(bias_added[h], n)
                    for r in range(4):
                        mm = pe.matmul(ps_sum[h][:, r * D:(r + 1) * D], turned[h][:, r * P:(r + 1) * P],
                                       g.Wna_sb[:, :], start=True, stop=True)
                    mm.then_inc(projected[h], 1)

            for i in loop(pe, 0, g.BLOCKS // 2):
                body(i, 0)
                body(i, 1)
            body(g.BLOCKS // 2, 0, last=True)

        @block.scalar
        def _(act):
            def body(i, b):
                n = i * 2 + b
                for h in range(2):
                    act.wait_ge(x_turned[b][h], i + 1)
                    act.copy(turned[h][:, :], ps_turn[h][:, :]).then_inc(x_copied[h], 1)

            for i in loop(act, 0, g.BLOCKS // 2):
                body(i, 0)
                body(i, 1)
            body(g.BLOCKS // 2, 0)

        @block.vector
        def _(dve):
            def body(i, b):
                n = i * 2 + b
                for h in range(2):
                    dve.wait_ge(projected[h], n + 1)
                    dve.wait_ge(sums_stored[b], i * 16)
                    dve.tensor_tensor(
                        new_sums[b][:, h * HALF:(h + 1) * HALF].rearrange("p (r c) -> p r c", c=D),
                        ps_sum[h][:, :].rearrange("p (r c) -> p r c", c=D),
                        g.bn_all[:, :].unsqueeze(1).broadcast_to([P, 4, D]), ALU.add).then_inc(bias_added[h], 1)

            for i in loop(dve, 0, g.BLOCKS // 2):
                body(i, 0)
                body(i, 1)
            body(g.BLOCKS // 2, 0)
            dve.wait_ge(earlier_ready, 3)
            dve.tensor_copy(spare[:, :], spare_i[:, :]).then_inc(spare_ready, 1)
            dve.wait_ge(spare_ready, 1)
            dve.tensor_tensor(g.to_spare[:, :, :], spare[:, :].unsqueeze(1).broadcast_to([P, g.GROUPS, TILES]),
                              g.dst_col[:, :, :], ALU.subtract)

        @block.gpsimd
        def _(pool):
            pool.memset(ones[:, :], 1.0).then_inc(earlier_ready, 1)
            pool.wait_ge(earlier_ready, 1)
            pool.affine_select(out=g.earlier[:, :], in_=ones[:, :], compare_op=ALU.is_gt, fill=0.0, base=0,
                               pattern=[[-1, P]], channel_multiplier=1).then_inc(earlier_ready, 1)
            pool.iota(spare_i[:, :], pattern=[[P, TILES]], base=g.SPARE_ROWS,
                      channel_multiplier=1).then_inc(earlier_ready, 1)

            def store(i, b):
                n = i * 2 + b
                for h in range(2):
                    pool.wait_ge(bias_added[h], n + 1)
                gate(g, pool)
                pool.dma_start(rows_of(g.sums[0], n * BLOCK), new_sums[b][:, :]).then_inc(sums_stored[b], 16)

            for i in loop(pool, 0, g.BLOCKS // 2):
                store(i, 0)
                store(i, 1)
            store(g.BLOCKS // 2, 0)
            for b in range(2):
                pool.wait_ge(sums_stored[b], 16 * ((g.BLOCKS + 1 - b) // 2))
    nc.clear_and_free_semaphores(sems)
    nc.all_engine_barrier()


def update_nodes(g, s, k):
    nc = g.nc
    n0 = k * g.BLOCKS
    slot0 = [k * ((g.BLOCKS + 1 - b) // 2) for b in range(2)]
    with ExitStack() as ctx:
        def sb(name, shape):
            return ctx.enter_context(nc.sbuf_tensor(f"{name}_u{k}", shape, F32))

        sums_in = [sb(f"sums_in{b}", [P, BLOCK]) for b in range(2)]
        turned = [sb(f"turned{h}", [P, HALF]) for h in range(2)]
        new_sums = [sb(f"new_sums{b}", [P, BLOCK]) for b in range(2)]
        ps_turn = [ctx.enter_context(nc.psum_tensor(f"ps_turn_u{k}{h}", [P, 512], F32)) for h in range(2)]
        ps_sum = [ctx.enter_context(nc.psum_tensor(f"ps_sum_u{k}{h}", [P, 512], F32)) for h in range(2)]
        block = ctx.enter_context(nc.Block())

        def over_blocks(eng, body):
            for i in loop(eng, 0, g.BLOCKS // 2):
                body(i * 2, i, 0)
                body(i * 2 + 1, i, 1)
            body(g.BLOCKS - 1, g.BLOCKS // 2, 0)

        @block.sync
        def _(sp):
            def load(n, i, b):
                sp.wait_ge(s["h_turned"][b][1], i + slot0[b])
                gate(g, sp)
                sp.dma_start(sums_in[b][:, :], rows_of(g.sums[k % 2], n * BLOCK)).then_inc(s["sums_loaded"][b], 16)

            over_blocks(sp, load)

        @block.scalar
        def _(act):
            def body(n, i, b):
                for h in range(2):
                    act.wait_ge(s["h_turned"][b][h], i + slot0[b] + 1)
                    act.activation(turned[h][:, :], ps_turn[h][:, :], ACT.Relu).then_inc(s["h_copied"][h], 1)

            over_blocks(act, body)

        @block.tensor
        def _(pe):
            def body(n, i, b):
                pe.wait_ge(s["sums_loaded"][b], (i + slot0[b]) * 16 + 16)
                for h in range(2):
                    pe.wait_ge(s["h_copied"][h], n + n0)
                    for r in range(4):
                        at = (4 * h + r) * D
                        mm = pe.transpose(ps_turn[h][:, r * P:(r + 1) * P], sums_in[b][:, at:at + D], g.ident[:, :])
                    mm.then_inc(s["h_turned"][b][h], 1)
                for h in range(2):
                    pe.wait_ge(s["h_copied"][h], n + n0 + 1)
                    pe.wait_ge(s["sum_ready"][h], n + n0)
                    for r in range(4):
                        mm = pe.matmul(ps_sum[h][:, r * D:(r + 1) * D], turned[h][:, r * P:(r + 1) * P],
                                       g.Wna_sb[:, :], start=True, stop=True)
                    mm.then_inc(s["h_projected"][h], 1)

            over_blocks(pe, body)

        @block.vector
        def _(dve):
            def body(n, i, b):
                for h in range(2):
                    dve.wait_ge(s["h_projected"][h], n + n0 + 1)
                    dve.wait_ge(s["sums_stored"][b], (i + slot0[b]) * 16)
                    dve.tensor_tensor(
                        new_sums[b][:, h * HALF:(h + 1) * HALF].rearrange("p (r c) -> p r c", c=D),
                        ps_sum[h][:, :].rearrange("p (r c) -> p r c", c=D),
                        g.bn_all[:, :].unsqueeze(1).broadcast_to([P, 4, D]), ALU.add).then_inc(s["sum_ready"][h], 1)

            over_blocks(dve, body)

        @block.gpsimd
        def _(pool):
            def store(n, i, b):
                for h in range(2):
                    pool.wait_ge(s["sum_ready"][h], n + n0 + 1)
                gate(g, pool)
                pool.dma_start(rows_of(g.sums[(k + 1) % 2], n * BLOCK), new_sums[b][:, :]).then_inc(s["sums_stored"][b], 16)

            over_blocks(pool, store)
            for b in range(2):
                done = 16 * (slot0[b] + (g.BLOCKS + 1 - b) // 2)
                pool.wait_ge(s["sums_stored"][b], done)


def in_its_form(g, eng, general, windowed):
    flag = eng.value_load(g.windowed[0:1, 0:1], min_val=0, max_val=1)
    with eng.If(flag > 0):
        windowed(eng)
    with eng.Else():
        general(eng)


def gather_rows_of(g, s, pool, b, j, gathers):
    for into, table, index in gathers(b, j):
        pool.indirect_dma_start(out=into, out_offset=None, in_=table,
                                in_offset=bass.IndirectOffsetOnAxis(ap=index, axis=0)
                                ).then_inc(s["gathered"][b], 16)


def scatter_tile(g, s, pool, b, j, scatter):
    table, index, rows_in = scatter(b, j)
    pool.indirect_dma_start(out=table, out_offset=bass.IndirectOffsetOnAxis(ap=index, axis=0),
                            in_=rows_in, in_offset=None, compute_op=ALU.add).then_inc(s["scattered"][b][j], 16)


def scatter_in_turn(g, s, pool, runs, i, b, j, scatter):
    if j:
        pool.wait_ge(s["scattered"][b][j - 1], (i + runs) * 16 + 16)
    else:
        pool.wait_ge(s["scattered"][1 - b][TILES - 1], (i + runs + b) * 16)
    gate(g, pool)
    scatter_tile(g, s, pool, b, j, scatter)


def wait_for_scatters(s, eng, b, groups):
    for j in range(TILES):
        eng.wait_ge(s["scattered"][b][j], 16 * groups)


def gather_and_scatter(g, s, pool, runs, gathers, scatter, n_pairs):
    def step(i, with_scatter):
        for b in range(2):
            pool.wait_ge(s["numbers_ready"][b], i + runs + runs // n_pairs + 1)
            gate(g, pool)
            for j in range(TILES):
                gather_rows_of(g, s, pool, b, j, gathers)
                if with_scatter:
                    if j == 0:
                        pool.wait_ge(s["result_ready"][b], i + runs)
                        gate(g, pool)
                    scatter_in_turn(g, s, pool, runs, i - 1, b, j, scatter)

    step(0, False)
    for i in loop(pool, 1, n_pairs):
        step(i, True)
    for b in range(2):
        pool.wait_ge(s["result_ready"][b], n_pairs + runs)
        gate(g, pool)
        for j in range(TILES):
            scatter_in_turn(g, s, pool, runs, n_pairs - 1, b, j, scatter)
    for b in range(2):
        wait_for_scatters(s, pool, b, n_pairs + runs)


def gather_and_scatter_windowed(g, s, pool, runs, gathers, scatter, n_pairs):
    def scatter_group(i, b):
        pool.wait_ge(s["result_ready"][b], i + runs + 1)
        wait_for_scatters(s, pool, 1 - b, i + runs + b)
        gate(g, pool)
        for j in range(TILES):
            scatter_tile(g, s, pool, b, j, scatter)

    def step(i, b, with_scatter):
        pool.wait_ge(s["numbers_ready"][b], i + runs + runs // n_pairs + 1)
        gate(g, pool)
        for j in range(TILES):
            gather_rows_of(g, s, pool, b, j, gathers)
        if with_scatter:
            scatter_group(i - 2 + b, 1 - b)

    step(0, 0, False)
    step(0, 1, False)
    step(1, 0, False)
    step(1, 1, True)
    for i in loop(pool, 2, n_pairs):
        step(i, 0, True)
        step(i, 1, True)
    scatter_group(n_pairs - 2, 1)
    scatter_group(n_pairs - 1, 0)
    scatter_group(n_pairs - 1, 1)
    for b in range(2):
        wait_for_scatters(s, pool, b, n_pairs + runs)


def load_windows(g, s, sp, runs, i, b, table, windows):
    sp.wait_ge(s["target_rows_picked"][b], i + runs)
    gate(g, sp)
    for j in range(TILES):
        base = sp.value_load(g.bases[0:1, bass.ds(i * 2 * TILES + b * TILES + j, 1)], min_val=0,
                             max_val=g.N - WINDOW)
        sp.dma_start(windows[b][:, j, :], table[bass.ds(base, WINDOW), :].rearrange("(p c) f -> p (c f)", c=CHUNKS)
                     ).then_inc(s["windows_loaded"][b], 16)


def load_offsets(g, s, sp, runs, i, b, offsets):
    sp.wait_ge(s["same_ready"][b], i + runs)
    gate(g, sp)
    sp.dma_start(offsets[b][:, :], g.offset_table[bass.ds(i * 2 * GROUP + b * GROUP, GROUP)]
                 .partition_broadcast(P)).then_inc(s["offsets_loaded"][b], 16)


def find_same(g, s, dve, runs, i, b, offsets, same):
    dve.wait_ge(s["offsets_loaded"][b], (i + runs) * 16 + 16)
    dve.wait_ge(s["result_ready"][b], i + runs)
    dve.tensor_tensor(same[b][:, :, :], offsets[b][:, :].rearrange("p (j q) -> p j q", q=P),
                      g.offset_col[:, bass.ds(i * 2 + b, 1), :].rearrange("p a t -> p (a t)")
                      .unsqueeze(2).broadcast_to([P, TILES, P]),
                      ALU.is_equal).then_inc(s["same_ready"][b], 1)


def find_target_rows(g, s, dve, runs, i, b, offsets, target_row):
    dve.wait_ge(s["offsets_loaded"][b], (i + runs) * 16 + 16)
    dve.wait_ge(s["target_rows_picked"][b], i + runs)
    for c in range(CHUNKS):
        last = dve.tensor_scalar(target_row[b][:, c, :], offsets[b][:, :], g.window_row[:, c:c + 1], None,
                                 ALU.is_equal)
    last.then_inc(s["target_rows_found"][b], 1)


def find_scatter_rows(g, s, dve, i, b, same, matches, repeats, moved):
    n = i * 2 + b
    dve.wait_ge(s["same_ready"][b], i + 1)
    dve.wait_ge(s["rows_found"], n)
    for j in range(TILES):
        last = dve.scalar_tensor_tensor(out=matches[:, j, :], in0=same[b][:, j, :], scalar=1.0,
                                        in1=g.earlier[:, :], op0=ALU.mult, op1=ALU.mult,
                                        accum_out=repeats[:, j:j + 1])
    last.then_inc(s["repeats_counted"], 1)
    dve.wait_ge(s["repeats_counted"], n + 1)
    dve.scalar_tensor_tensor(out=moved[:, :], in0=repeats[:, :], scalar=1.0,
                             in1=g.to_spare[:, bass.ds(n, 1), :].rearrange("p a t -> p (a t)"),
                             op0=ALU.min, op1=ALU.mult).then_inc(s["rows_moved"], 1)
    dve.wait_ge(s["rows_moved"], n + 1)
    dve.tensor_tensor(g.scatter_rows[:, bass.ds(n, 1), :].rearrange("p a t -> p (a t)"), moved[:, :],
                      g.dst_col[:, bass.ds(n, 1), :].rearrange("p a t -> p (a t)"),
                      ALU.add).then_inc(s["rows_found"], 1)


def pass_messages(g, s, k, table, zeros=None):
    nc = g.nc
    PAIRS = g.GROUPS // 2
    runs = k * PAIRS
    with ExitStack() as ctx:
        def sb(name, shape, dt=F32):
            return ctx.enter_context(nc.sbuf_tensor(f"{name}_m{k}", shape, dt))

        def ps(name):
            return ctx.enter_context(nc.psum_tensor(f"{name}_m{k}", [P, 512], F32))

        gathered = [[sb(f"gathered{b}{e}", [P, TILES, D]) for e in range(2)] for b in range(2)]
        numbers = [sb(f"numbers{b}", [P, 2 * TILES], I32) for b in range(2)]
        targets_to = [sb(f"targets_to{b}", [P, TILES], I32) for b in range(2)]
        turned = [sb(f"turned{e}", [P, GROUP]) for e in range(2)]
        hidden = [sb(f"hidden{m}", [P, GROUP]) for m in range(2)]
        messages = sb("messages", [P, TILES, D])
        result = [sb(f"result{b}", [P, TILES, D]) for b in range(2)]
        offsets = [sb(f"offsets{b}", [P, GROUP], I32) for b in range(2)]
        same = [sb(f"same{b}", [P, TILES, P]) for b in range(2)]
        ps_turn = [ps(f"ps_turn{e}") for e in range(2)]
        ps_hidden = [ps(f"ps_hidden{m}") for m in range(2)]
        ps_msg = ps("ps_msg")
        ps_sum = ps("ps_sum")
        matches = sb("matches", [P, TILES, P])
        repeats = sb("repeats", [P, TILES])
        moved = sb("moved", [P, TILES])
        windows = [sb(f"windows{b}", [P, TILES, CHUNKS * D]) for b in range(2)]
        target_row = [sb(f"target_row{b}", [P, CHUNKS, GROUP]) for b in range(2)]
        block = ctx.enter_context(nc.Block())

        @block.gpsimd
        def _(pool):
            def source(b, j):
                return gathered[b][0][:, j, :], table, numbers[b][:, j:j + 1]

            def target(b, j):
                return gathered[b][1][:, j, :], table, numbers[b][:, TILES + j:TILES + j + 1]

            def result_of(b, j):
                return g.sums[k % 2][:, :], targets_to[b][:, j:j + 1], result[b][:, j, :]

            in_its_form(
                g, pool,
                lambda eng: gather_and_scatter(g, s, eng, runs, lambda b, j: [source(b, j), target(b, j)],
                                               result_of, PAIRS),
                lambda eng: gather_and_scatter_windowed(g, s, eng, runs, lambda b, j: [source(b, j)],
                                                        result_of, PAIRS))

        @block.sync
        def _(sp):
            def zero(i, b):
                if zeros is not None:
                    sp.dma_start(rows_of(g.attn_sums, i * 2 * GROUP + b * GROUP, GROUP, TILES),
                                 zeros).then_inc(s["zeros_stored"], 16)

            def general(sp):
                for i in loop(sp, 0, PAIRS):
                    for b in range(2):
                        load_offsets(g, s, sp, runs, i, b, offsets)
                        zero(i, b)

            def windowed(sp):
                for i in loop(sp, 0, PAIRS):
                    for b in range(2):
                        load_offsets(g, s, sp, runs, i, b, offsets)
                        load_windows(g, s, sp, runs, i, b, table, windows)
                        zero(i, b)

            in_its_form(g, sp, general, windowed)
            if zeros is not None:
                sp.wait_ge(s["zeros_stored"], 48 + 16 * g.GROUPS)

        @block.tensor
        def _(pe):
            def turn(b, e, done):
                for j in range(TILES):
                    mm = pe.transpose(ps_turn[e][:, j * P:(j + 1) * P], gathered[b][e][:, j, :], g.ident[:, :])
                mm.then_inc(done, 1)

            def first_layer(i, b):
                n = (i + runs) * 2 + b
                pe.wait_ge(s["turn_copied"][0], n + 1)
                for m in range(2):
                    pe.wait_ge(s["hidden_ready"][m], n)
                    pe.matmul(ps_hidden[m][:, :], g.Wm1_sb[:, 0, m * D:(m + 1) * D], turned[0][:, :],
                              start=True, stop=False)
                pe.wait_ge(s["turn_copied"][1], n + 1)
                for m in range(2):
                    pe.matmul(ps_hidden[m][:, :], g.Wm1_sb[:, 1, m * D:(m + 1) * D], turned[1][:, :],
                              start=False, stop=True).then_inc(s["hidden_summed"][m], 1)

            def second_layer(i, b):
                n = (i + runs) * 2 + b
                for m in range(2):
                    pe.wait_ge(s["hidden_ready"][m], n + 1)
                pe.wait_ge(s["messages_ready"], n)
                for j in range(TILES):
                    for m in range(2):
                        mm = pe.matmul(ps_msg[:, j * D:(j + 1) * D], hidden[m][:, j * P:(j + 1) * P],
                                       g.Wm2n_sb[:, m, :], start=(m == 0), stop=(m == 1))
                mm.then_inc(s["messages_summed"], 1)

            def combine(i, b):
                n = (i + runs) * 2 + b
                pe.wait_ge(s["messages_ready"], n + 1)
                pe.wait_ge(s["same_ready"][b], i + runs + 1)
                pe.wait_ge(s["result_ready"][1 - b], i + runs + b)
                for j in range(TILES):
                    mm = pe.matmul(ps_sum[:, j * D:(j + 1) * D], same[b][:, j, :], messages[:, j, :],
                                   start=True, stop=True)
                mm.then_inc(s["combined"], 1)

            def general(pe):
                for i in loop(pe, 0, PAIRS):
                    for b in range(2):
                        pe.wait_ge(s["gathered"][b], (i + runs) * 128 + 128)
                        for e in range(2):
                            pe.wait_ge(s["turn_copied"][e], (i + runs) * 2 + b)
                            turn(b, e, s["ends_turned"][e])
                        first_layer(i, b)
                        second_layer(i, b)
                        combine(i, b)

            def turn_sources(i, b):
                pe.wait_ge(s["gathered"][b], (i + runs) * 64 + 64)
                pe.wait_ge(s["turn_copied"][0], (i + runs) * 2 + b)
                turn(b, 0, s["ends_turned"][0])

            def pick_targets(i, b, tiles):
                if tiles[0] == 0:
                    pe.wait_ge(s["turn_copied"][1], (i + runs) * 2 + b)
                    pe.wait_ge(s["target_rows_found"][b], i + runs + 1)
                    pe.wait_ge(s["windows_loaded"][b], (i + runs) * 64 + 64)
                for j in tiles:
                    for c in range(CHUNKS):
                        mm = pe.matmul(ps_turn[1][:, j * P:(j + 1) * P], windows[b][:, j, c * D:(c + 1) * D],
                                       target_row[b][:, c, j * P:(j + 1) * P], start=(c == 0),
                                       stop=(c == CHUNKS - 1))
                if tiles[-1] == TILES - 1:
                    mm.then_inc(s["target_rows_picked"][b], 1)

            def windowed(pe):
                def step(i, b, last):
                    then = (i + b, 1 - b)
                    first_layer(i, b)
                    if not last:
                        turn_sources(*then)
                        pick_targets(*then, [0, 1])
                    second_layer(i, b)
                    if not last:
                        pick_targets(*then, [2, 3])
                    combine(i, b)

                turn_sources(0, 0)
                pick_targets(0, 0, [0, 1, 2, 3])
                for i in loop(pe, 0, PAIRS - 1):
                    step(i, 0, False)
                    step(i, 1, False)
                step(PAIRS - 1, 0, False)
                step(PAIRS - 1, 1, True)

            in_its_form(g, pe, general, windowed)

        @block.scalar
        def _(act):
            def copy_sources(i, b):
                act.wait_ge(s["ends_turned"][0], (i + runs) * 2 + b + 1)
                act.activation(turned[0][:, :], ps_turn[0][:, :], ACT.Relu if k else ACT.Copy
                               ).then_inc(s["turn_copied"][0], 1)

            def next_numbers(i, b):
                act.copy(numbers[b][:, :], g.gather_rows[:, bass.ds(i * 2 + (b + 2), 1), :]
                         .rearrange("p a t -> p (a t)")).then_inc(s["numbers_ready"][b], 1)

            def first_hidden(i, b):
                act.wait_ge(s["hidden_summed"][0], (i + runs) * 2 + b + 1)
                act.activation(hidden[0][:, :], ps_hidden[0][:, :], ACT.Relu,
                               bias=g.bm1_col[:, 0:1]).then_inc(s["hidden_ready"][0], 1)

            def copy_result(i, b):
                wait_for_scatters(s, act, b, i + runs)
                if k == 0:
                    act.wait_ge(s["rows_found"], i * 2 + b + 1)
                act.copy(targets_to[b][:, :], g.scatter_rows[:, bass.ds(i * 2 + b, 1), :]
                         .rearrange("p a t -> p (a t)"))
                act.wait_ge(s["combined"], (i + runs) * 2 + b + 1)
                act.copy(result[b][:, :, :].rearrange("p j c -> p (j c)"),
                         ps_sum[:, :]).then_inc(s["result_ready"][b], 1)

            def general(act):
                for i in loop(act, 0, PAIRS):
                    for b in range(2):
                        copy_sources(i, b)
                        act.wait_ge(s["ends_turned"][1], (i + runs) * 2 + b + 1)
                        next_numbers(i, b)
                        first_hidden(i, b)
                        copy_result(i, b)

            def windowed(act):
                def step(i, b, last):
                    first_hidden(i, b)
                    if not last:
                        copy_sources(i + b, 1 - b)
                        next_numbers(i + b, 1 - b)
                    copy_result(i, b)

                copy_sources(0, 0)
                next_numbers(0, 0)
                for i in loop(act, 0, PAIRS - 1):
                    step(i, 0, False)
                    step(i, 1, False)
                step(PAIRS - 1, 0, False)
                step(PAIRS - 1, 1, True)

            for b in range(2):
                act.copy(numbers[b][:, :], g.gather_rows[:, b, :]).then_inc(s["numbers_ready"][b], 1)
            in_its_form(g, act, general, windowed)

        @block.vector
        def _(dve):
            def second_hidden(i, b):
                dve.wait_ge(s["hidden_summed"][1], (i + runs) * 2 + b + 1)
                dve.tensor_scalar(hidden[1][:, :], ps_hidden[1][:, :], g.bm1_col[:, 1:2], 0.0, ALU.add,
                                  ALU.max).then_inc(s["hidden_ready"][1], 1)

            def copy_targets():
                if k:
                    copy = dve.tensor_scalar(turned[1][:, :], ps_turn[1][:, :], 0.0, None, ALU.max)
                else:
                    copy = dve.tensor_copy(turned[1][:, :], ps_turn[1][:, :])
                copy.then_inc(s["turn_copied"][1], 1)

            def add_bias(i, b):
                dve.wait_ge(s["messages_summed"], (i + runs) * 2 + b + 1)
                dve.tensor_tensor(messages[:, :, :], ps_msg[:, :].rearrange("p (j c) -> p j c", c=D),
                                  g.bm2n_all[:, :].unsqueeze(1).broadcast_to([P, TILES, D]),
                                  ALU.add).then_inc(s["messages_ready"], 1)

            def find_rows(i, b):
                if k == 0:
                    find_scatter_rows(g, s, dve, i, b, same, matches, repeats, moved)

            def general(dve):
                for i in loop(dve, 0, PAIRS):
                    for b in range(2):
                        find_same(g, s, dve, runs, i, b, offsets, same)
                        find_rows(i, b)
                        dve.wait_ge(s["ends_turned"][1], (i + runs) * 2 + b + 1)
                        copy_targets()
                        second_hidden(i, b)
                        add_bias(i, b)

            def windowed(dve):
                def step(i, b, remain):
                    second_hidden(i, b)
                    if remain > 0:
                        find_same(g, s, dve, runs, i + b, 1 - b, offsets, same)
                    add_bias(i, b)
                    if remain > 0:
                        dve.wait_ge(s["target_rows_picked"][1 - b], i + b + runs + 1)
                        copy_targets()
                    if remain > 1:
                        find_target_rows(g, s, dve, runs, i + 1, b, offsets, target_row)
                    if remain > 0:
                        find_rows(i + b, 1 - b)

                find_target_rows(g, s, dve, runs, 0, 0, offsets, target_row)
                find_same(g, s, dve, runs, 0, 0, offsets, same)
                find_rows(0, 0)
                find_target_rows(g, s, dve, runs, 0, 1, offsets, target_row)
                dve.wait_ge(s["target_rows_picked"][0], runs + 1)
                copy_targets()
                for i in loop(dve, 0, PAIRS - 1):
                    step(i, 0, 3)
                    step(i, 1, 2)
                step(PAIRS - 1, 0, 1)
                step(PAIRS - 1, 1, 0)

            in_its_form(g, dve, general, windowed)


def over_blocks(g, eng, body):
    for i in loop(eng, 0, g.BLOCKS // 2):
        body(i * 2, i, 0, False)
        body(i * 2 + 1, i, 1, False)
    body(g.BLOCKS - 1, g.BLOCKS // 2, 0, True)


def over_kept_blocks(g, eng, body):
    for first, end, kept in ((0, g.RESIDENT // 2, True), (g.RESIDENT // 2, g.BLOCKS // 2, False)):
        if end > first:
            for i in loop(eng, first, end):
                body(i * 2, i, 0, False, kept)
                body(i * 2 + 1, i, 1, False, kept)
    body(g.BLOCKS - 1, g.BLOCKS // 2, 0, True, False)


def block_of(g, kept, n, buffer):
    return g.kept[:, bass.ds(n, 1), :].rearrange("p a c -> p (a c)") if kept else buffer[:, :]


def row_statistics(g, dve, s, total, stats, moments, n):
    for r in range(ROWS):
        last = dve.bn_stats(stats[:, r, :], total[:, r * D:(r + 1) * D])
    last.then_inc(s["row_stats"], 1)
    dve.wait_ge(s["row_stats"], n + 1)
    gate(g, dve)
    for r in range(ROWS):
        last = dve.bn_aggr(moments[:, r, :], stats[:, r, :])
    last.then_inc(s["row_moments"], 1)


def finish_messages(g, s):
    nc = g.nc
    with ExitStack() as ctx:
        def sb(name, shape):
            return ctx.enter_context(nc.sbuf_tensor(f"{name}_f", shape, F32))

        sums_in = [sb(f"sums_in{b}", [P, BLOCK]) for b in range(2)]
        x_in = [sb(f"x_in{b}", [P, BLOCK]) for b in range(2)]
        total = [sb(f"total{b}", [P, BLOCK]) for b in range(2)]
        stats = sb("stats", [P, ROWS, 6])
        row_moments = sb("moments", [P, ROWS, 2])
        root = sb("root", [P, ROWS, 1])
        inverse = sb("inverse", [P, ROWS, 1])
        minus_mean = sb("minus_mean", [P, ROWS, 1])
        x1 = [sb(f"x1{b}", [P, BLOCK]) for b in range(2)]
        pieces = parts_of(g.TAIL_PARTS)
        block = ctx.enter_context(nc.Block())

        @block.sync
        def _(sp):
            def load(n, i, b, last):
                sp.wait_ge(s["residual_added"][b], i)
                gate(g, sp)
                sp.dma_start(sums_in[b][:, :], rows_of(g.sums[0], n * BLOCK)).then_inc(s["sums_loaded"][b], 16)
                for a, z in pieces if last else [(0, P)]:
                    sp.dma_start(x_in[b][a:z, :], rows_of(g.x, n * BLOCK + a * ROWS, (z - a) * ROWS)
                                 ).then_inc(s["x_loaded"][b], 16)

            over_blocks(g, sp, load)

        @block.vector
        def _(dve):
            def body(n, i, b, last):
                dve.wait_ge(s["sums_loaded"][b], i * 16 + 16)
                dve.wait_ge(s["x_loaded"][b], i * 16 + 16 * (len(pieces) if last else 1))
                dve.wait_ge(s["normed"][b], i)
                dve.scalar_tensor_tensor(out=total[b][:, :], in0=sums_in[b][:, :], scalar=0.0, in1=x_in[b][:, :],
                                         op0=ALU.max, op1=ALU.add).then_inc(s["residual_added"][b], 1)
                dve.wait_ge(s["residual_added"][b], i + 1)
                dve.wait_ge(s["shifts_ready"], n)
                row_statistics(g, dve, s, total[b], stats, row_moments, n)
                dve.wait_ge(s["rooted"], n + 1)
                dve.reciprocal(inverse[:, :, :], root[:, :, :]).then_inc(s["inverted"], 1)
                dve.wait_ge(s["inverted"], n + 1)
                dve.scalar_tensor_tensor(out=minus_mean[:, :, :], in0=row_moments[:, :, 0:1], scalar=-1.0,
                                         in1=inverse[:, :, :], op0=ALU.mult,
                                         op1=ALU.mult).then_inc(s["shifts_ready"], 1)

            over_blocks(g, dve, body)

        @block.scalar
        def _(act):
            def body(n, i, b, last):
                act.wait_ge(s["row_moments"], n + 1)
                act.wait_ge(s["normed"][1 - b], i + b)
                act.activation(root[:, :, :], row_moments[:, :, 1:2], ACT.Sqrt,
                               bias=g.eps_col[:, 0:1]).then_inc(s["rooted"], 1)
                act.wait_ge(s["shifts_ready"], n + 1)
                act.wait_ge(s["x1_stored"][b], i * 16)
                for r in range(ROWS):
                    row = slice(r * D, (r + 1) * D)
                    last_row = act.activation(x1[b][:, row], total[b][:, row], ACT.Identity,
                                              bias=minus_mean[:, r, :], scale=inverse[:, r, :])
                last_row.then_inc(s["normed"][b], 1)

            over_blocks(g, act, body)

        @block.gpsimd
        def _(pool):
            def store(n, i, b, last):
                pool.wait_ge(s["normed"][b], i + 1)
                gate(g, pool)
                pool.dma_start(rows_of(g.x1_table, n * BLOCK), x1[b][:, :]).then_inc(s["x1_stored"][b], 16)

            over_blocks(g, pool, store)
            for b in range(2):
                pool.wait_ge(s["x1_stored"][b], 16 * ((g.BLOCKS + 1 - b) // 2))


def ahead(i, b, by):
    return i + (b + by) // 2, (b + by) % 2


def attend(g, s):
    nc = g.nc
    PAIRS = g.GROUPS // 2
    with ExitStack() as ctx:
        def sb(name, shape, dt=F32):
            return ctx.enter_context(nc.sbuf_tensor(f"{name}_t", shape, dt))

        def ps(name, n=512):
            return ctx.enter_context(nc.psum_tensor(f"{name}_t", [P, n], F32))

        gathered = [[sb(f"gathered{b}{e}", [P, TILES, D]) for e in range(2)] for b in range(2)]
        numbers = [sb(f"numbers{b}", [P, 2 * TILES], I32) for b in range(2)]
        targets_to = [sb(f"targets_to{b}", [P, TILES], I32) for b in range(2)]
        edges_in = [sb(f"edges_in{b}", [P, TILES, D]) for b in range(2)]
        edges_t = sb("edges_t", [P, GROUP])
        sources_t = sb("sources_t", [P, GROUP])
        targets_t = sb("targets_t", [P, GROUP])
        keys_values = [sb(f"keys_values{b}", [P, TILES, 2 * D]) for b in range(2)]
        qk = sb("qk", [P, TILES, D])
        qke = sb("qke", [P, TILES, D])
        score = sb("score", [P, TILES * HEADS])
        low = sb("low", [P, TILES * HEADS])
        clipped = sb("clipped", [P, TILES * HEADS])
        messages = [sb(f"messages{b}", [P, TILES, AT]) for b in range(2)]
        unused = sb("unused", [P, 1])
        result = [sb(f"result{b}", [P, TILES, AT]) for b in range(2)]
        offsets = [sb(f"offsets{b}", [P, GROUP], I32) for b in range(2)]
        same = [sb(f"same{b}", [P, TILES, P]) for b in range(2)]
        windows = [sb(f"windows{b}", [P, TILES, CHUNKS * D]) for b in range(2)]
        target_row = [sb(f"target_row{b}", [P, CHUNKS, GROUP]) for b in range(2)]
        ps_turn = ps("ps_turn")
        ps_target = ps("ps_target")
        ps_edge = ps("ps_edge")
        ps_query = ps("ps_query")
        ps_kv = ps("ps_kv", 1024)
        ps_sum = [ps(f"ps_sum{u}") for u in range(2)]
        block = ctx.enter_context(nc.Block())

        @block.gpsimd
        def _(pool):
            def end(b, j, e):
                at = e * TILES + j
                return gathered[b][e][:, j, :], g.x1_table[:, :], numbers[b][:, at:at + 1]

            def result_of(b, j):
                return g.attn_sums[:, :], targets_to[b][:, j:j + 1], result[b][:, j, :]

            in_its_form(
                g, pool,
                lambda eng: gather_and_scatter(g, s, eng, 0, lambda b, j: [end(b, j, 0), end(b, j, 1)],
                                               result_of, PAIRS),
                lambda eng: gather_and_scatter_windowed(g, s, eng, 0, lambda b, j: [end(b, j, 0)],
                                                        result_of, PAIRS))

        @block.sync
        def _(sp):
            def load_edges(i, b, last=False):
                n = i * 2 + b
                sp.wait_ge(s["edges_turned"][b], i)
                gate(g, sp)
                sp.dma_start(edges_in[b][:, 0:3, :],
                             g.edge_attr_128[0:3 * g.QUARTER, :].rearrange("(j e) c -> e j c", j=3)
                             [bass.ds(n * P, P), :, :]).then_inc(s["edges_loaded"][b], 16)
                if last and b:
                    sp.dma_start(edges_in[b][:, 3, :], g.edge_attr_128[g.E - P:g.E, :]
                                 ).then_inc(s["edges_loaded"][b], 16)
                else:
                    count = g.TAIL_EDGES if last else P
                    sp.dma_start(edges_in[b][0:count, 3, :],
                                 g.edge_attr_128[bass.ds(n * P + 3 * g.QUARTER, count), :]
                                 ).then_inc(s["edges_loaded"][b], 16)

            def load(i, b, windowed, last=False):
                if windowed:
                    load_windows(g, s, sp, 0, i, b, g.x1_table, windows)
                load_edges(i, b, last)
                load_offsets(g, s, sp, 0, i, b, offsets)

            def over_pairs(windowed):
                for i in loop(sp, 0, PAIRS - 1):
                    load(i, 0, windowed)
                    load(i, 1, windowed)
                load(PAIRS - 1, 0, windowed, last=True)
                load(PAIRS - 1, 1, windowed, last=True)

            in_its_form(g, sp, lambda _: over_pairs(False), lambda _: over_pairs(True))

        @block.tensor
        def _(pe):
            def turn(to, of, done):
                for j in range(TILES):
                    mm = pe.transpose(to[:, j * P:(j + 1) * P], of[:, j, :], g.ident[:, :])
                mm.then_inc(done, 1)

            def turn_edges(i, b):
                pe.wait_ge(s["edges_loaded"][b], i * 32 + 32)
                pe.wait_ge(s["sources_copied"], i * 2 + b)
                turn(ps_turn, edges_in[b], s["edges_turned"][b])

            def turn_sources(i, b, gathers):
                pe.wait_ge(s["edges_copied"], i * 2 + b + 1)
                pe.wait_ge(s["gathered"][b], (i + 1) * 16 * TILES * gathers)
                turn(ps_turn, gathered[b][0], s["sources_turned"])

            def turn_targets(i, b):
                pe.wait_ge(s["targets_copied"], i * 2 + b)
                turn(ps_target, gathered[b][1], s["targets_turned"])

            def pick_targets(i, b):
                pe.wait_ge(s["targets_copied"], i * 2 + b)
                pe.wait_ge(s["target_rows_found"][b], i + 1)
                pe.wait_ge(s["windows_loaded"][b], i * 64 + 64)
                for j in range(TILES):
                    for c in range(CHUNKS):
                        mm = pe.matmul(ps_target[:, j * P:(j + 1) * P], windows[b][:, j, c * D:(c + 1) * D],
                                       target_row[b][:, c, j * P:(j + 1) * P], start=(c == 0),
                                       stop=(c == CHUNKS - 1))
                mm.then_inc(s["target_rows_picked"][b], 1)

            def project(i, b):
                n = i * 2 + b
                pe.wait_ge(s["sources_copied"], n + 1)
                pe.wait_ge(s["kv_copied"], n)
                for j in range(TILES):
                    mm = pe.matmul(ps_kv[:, j * 2 * D:(j + 1) * 2 * D], sources_t[:, j * P:(j + 1) * P],
                                   g.Wqkv_sb[:, D:3 * D], start=True, stop=True)
                mm.then_inc(s["kv_projected"], 1)
                pe.wait_ge(s["targets_copied"], n + 1)
                pe.wait_ge(s["multiplied"], n)
                for j in range(TILES):
                    mm = pe.matmul(ps_query[:, j * D:(j + 1) * D], targets_t[:, j * P:(j + 1) * P],
                                   g.Wqkv_sb[:, 0:D], start=True, stop=True)
                mm.then_inc(s["queries_projected"], 1)
                pe.wait_ge(s["edges_used"], n)
                for j in range(TILES):
                    mm = pe.matmul(ps_edge[:, j * D:(j + 1) * D], edges_t[:, j * P:(j + 1) * P], g.WE_sb[:, :],
                                   start=True, stop=True)
                mm.then_inc(s["edges_projected"], 1)

            def combine(i, b):
                pe.wait_ge(s["values_weighted"], i * 2 + b + 1)
                pe.wait_ge(s["same_ready"][b], i + 1)
                pe.wait_ge(s["result_ready"][1 - b], i + b)
                for j in range(TILES):
                    at = (j % 2) * AT
                    mm = pe.matmul(ps_sum[j // 2][:, at:at + AT], same[b][:, j, :], messages[b][:, j, :],
                                   start=True, stop=True)
                mm.then_inc(s["combined"][b], 1)

            def general(pe):
                for i in loop(pe, 0, PAIRS):
                    for b in range(2):
                        turn_edges(i, b)
                        turn_sources(i, b, gathers=2)
                        turn_targets(i, b)
                        project(i, b)
                        combine(i, b)

            def windowed(pe):
                def turn_group(i, b):
                    turn_edges(i, b)
                    pick_targets(i, b)
                    turn_sources(i, b, gathers=1)

                def step(i, b, remain):
                    if remain > 0:
                        project(*ahead(i, b, 1))
                    if remain > 1:
                        turn_group(*ahead(i, b, 2))
                    combine(i, b)

                turn_group(0, 0)
                project(0, 0)
                turn_group(0, 1)
                for i in loop(pe, 0, PAIRS - 1):
                    step(i, 0, 3)
                    step(i, 1, 2)
                step(PAIRS - 1, 0, 1)
                step(PAIRS - 1, 1, 0)

            in_its_form(g, pe, general, windowed)

        @block.scalar
        def _(act):
            def copy_edges(i, b):
                act.wait_ge(s["edges_turned"][b], i + 1)
                act.copy(edges_t[:, :], ps_turn[:, :]).then_inc(s["edges_copied"], 1)

            def copy_sources(i, b):
                act.wait_ge(s["sources_turned"], i * 2 + b + 1)
                act.copy(sources_t[:, :], ps_turn[:, :]).then_inc(s["sources_copied"], 1)

            def next_numbers(i, b):
                act.copy(numbers[b][:, :], g.gather_rows[:, bass.ds(i * 2 + (b + 2), 1), :]
                         .rearrange("p a t -> p (a t)")).then_inc(s["numbers_ready"][b], 1)

            def copy_keys_values(i, b):
                act.wait_ge(s["kv_projected"], i * 2 + b + 1)
                act.wait_ge(s["values_weighted"], i * 2)
                act.copy(keys_values[b][:, :, :].rearrange("p j c -> p (j c)"), ps_kv[:, :]
                         ).then_inc(s["kv_copied"], 1)

            def weigh(i, b):
                act.wait_ge(s["clipped"], i * 2 + b + 1)
                act.wait_ge(s["combined"][b], i)
                act.activation(messages[b][:, :, D:AT], clipped[:, :].rearrange("p (j h) -> p j h", h=HEADS),
                               ACT.Exp).then_inc(s["weights_ready"], 1)

            def copy_result(i, b):
                wait_for_scatters(s, act, b, i)
                act.copy(targets_to[b][:, :], g.scatter_rows[:, bass.ds(i * 2 + b, 1), :]
                         .rearrange("p a t -> p (a t)"))
                act.wait_ge(s["combined"][b], i + 1)
                for u in range(2):
                    last = act.copy(result[b][:, 2 * u:2 * u + 2, :].rearrange("p j c -> p (j c)"),
                                    ps_sum[u][:, 0:2 * AT])
                last.then_inc(s["result_ready"][b], 1)

            def general(act):
                for i in loop(act, 0, PAIRS):
                    for b in range(2):
                        copy_edges(i, b)
                        copy_sources(i, b)
                        act.wait_ge(s["targets_turned"], i * 2 + b + 1)
                        next_numbers(i, b)
                        copy_keys_values(i, b)
                        weigh(i, b)
                        copy_result(i, b)

            def windowed(act):
                def step(i, b, remain):
                    if remain > 0:
                        copy_keys_values(*ahead(i, b, 1))
                    if remain > 1:
                        copy_edges(*ahead(i, b, 2))
                    if remain > 0:
                        weigh(*ahead(i, b, 1))
                    if remain > 1:
                        copy_sources(*ahead(i, b, 2))
                        next_numbers(*ahead(i, b, 2))
                    copy_result(i, b)

                copy_edges(0, 0)
                copy_sources(0, 0)
                next_numbers(0, 0)
                copy_keys_values(0, 0)
                copy_edges(0, 1)
                weigh(0, 0)
                copy_sources(0, 1)
                next_numbers(0, 1)
                for i in loop(act, 0, PAIRS - 1):
                    act.wait_ge(s["table_loaded"], i)
                    act.activation(unused[:, :], g.eps_col[:, :], ACT.Exp).then_inc(s["table_loaded"], 1)
                    step(i, 0, 3)
                    step(i, 1, 2)
                step(PAIRS - 1, 0, 1)
                step(PAIRS - 1, 1, 0)

            for b in range(2):
                act.copy(numbers[b][:, :], g.gather_rows[:, b, :]).then_inc(s["numbers_ready"][b], 1)
            in_its_form(g, act, general, windowed)

        @block.vector
        def _(dve):
            def copy_targets():
                dve.tensor_copy(targets_t[:, :], ps_target[:, :]).then_inc(s["targets_copied"], 1)

            def score_edges(i, b):
                n = i * 2 + b
                dve.wait_ge(s["queries_projected"], n + 1)
                dve.wait_ge(s["kv_copied"], n + 1)
                dve.wait_ge(s["edges_used"], n)
                dve.tensor_tensor(qk[:, :, :], ps_query[:, :].rearrange("p (j c) -> p j c", c=D),
                                  keys_values[b][:, :, 0:D], ALU.mult).then_inc(s["multiplied"], 1)
                dve.wait_ge(s["multiplied"], n + 1)
                dve.wait_ge(s["edges_projected"], n + 1)
                dve.wait_ge(s["scored"], n)
                dve.tensor_tensor(qke[:, :, :], qk[:, :, :], ps_edge[:, :].rearrange("p (j c) -> p j c", c=D),
                                  ALU.mult).then_inc(s["edges_used"], 1)
                dve.wait_ge(s["edges_used"], n + 1)
                dve.wait_ge(s["scaled"], n)
                dve.tensor_reduce(score[:, :], qke[:, :, :].rearrange("p j (h c) -> p (j h) c", h=HEADS),
                                  AX.X, ALU.add).then_inc(s["scored"], 1)
                dve.wait_ge(s["scored"], n + 1)
                dve.wait_ge(s["clipped"], n)
                dve.tensor_scalar(low[:, :], score[:, :], DH ** -0.5, CLIP, ALU.mult,
                                  ALU.min).then_inc(s["scaled"], 1)
                dve.wait_ge(s["scaled"], n + 1)
                dve.wait_ge(s["weights_ready"], n)
                dve.tensor_scalar(clipped[:, :], low[:, :], -CLIP, None, ALU.max).then_inc(s["clipped"], 1)

            def weigh_values(i, b):
                n = i * 2 + b
                dve.wait_ge(s["weights_ready"], n + 1)
                dve.tensor_tensor(
                    messages[b][:, :, 0:D].rearrange("p j (h c) -> p j h c", h=HEADS),
                    keys_values[b][:, :, D:2 * D].rearrange("p j (h c) -> p j h c", h=HEADS),
                    messages[b][:, :, D:AT].unsqueeze(3).broadcast_to([P, TILES, HEADS, DH]),
                    ALU.mult).then_inc(s["values_weighted"], 1)

            def general(dve):
                for i in loop(dve, 0, PAIRS):
                    for b in range(2):
                        find_same(g, s, dve, 0, i, b, offsets, same)
                        dve.wait_ge(s["targets_turned"], i * 2 + b + 1)
                        copy_targets()
                        score_edges(i, b)
                        weigh_values(i, b)

            def windowed(dve):
                def copy_picked(i, b):
                    dve.wait_ge(s["target_rows_picked"][b], i + 1)
                    copy_targets()

                def step(i, b, remain):
                    if remain > 0:
                        find_same(g, s, dve, 0, *ahead(i, b, 1), offsets, same)
                        score_edges(*ahead(i, b, 1))
                        weigh_values(*ahead(i, b, 1))
                    if remain > 1:
                        copy_picked(*ahead(i, b, 2))
                    if remain > 2:
                        find_target_rows(g, s, dve, 0, *ahead(i, b, 3), offsets, target_row)

                find_target_rows(g, s, dve, 0, 0, 0, offsets, target_row)
                find_same(g, s, dve, 0, 0, 0, offsets, same)
                find_target_rows(g, s, dve, 0, 0, 1, offsets, target_row)
                copy_picked(0, 0)
                score_edges(0, 0)
                weigh_values(0, 0)
                copy_picked(0, 1)
                find_target_rows(g, s, dve, 0, 1, 0, offsets, target_row)
                for i in loop(dve, 0, PAIRS - 2):
                    step(i, 0, 5)
                    step(i, 1, 4)
                step(PAIRS - 2, 0, 3)
                step(PAIRS - 2, 1, 2)
                step(PAIRS - 1, 0, 1)
                step(PAIRS - 1, 1, 0)

            in_its_form(g, dve, general, windowed)


def measure(g, dve, turned, n, h, last):
    half = turned[:, h * HALF:(h + 1) * HALF]
    if last:
        half = half.rearrange("p (r q) -> p r q", q=P)[:, :, 0:g.TAIL_PARTS]
    return dve.bn_stats(g.feature_stats[:, bass.ds(n * 2 + h, 1), :].rearrange("p a k -> p (a k)"), half)


def finish_attention(g, s):
    nc = g.nc
    with ExitStack() as ctx:
        def sb(name, shape, dt=F32):
            return ctx.enter_context(nc.sbuf_tensor(f"{name}_y", shape, dt))

        sums_in = [sb(f"sums_in{b}", [P, ROWS * AT]) for b in range(2)]
        x1_in = [sb(f"x1_in{b}", [P, BLOCK]) for b in range(2)]
        weight = sb("weight", [P, ROWS, HEADS])
        inverse = sb("inverse", [P, ROWS, HEADS])
        mean_v = [sb(f"mean_v{b}", [P, BLOCK]) for b in range(2)]
        turned = [sb(f"turned{b}", [P, BLOCK]) for b in range(2)]
        ps_turn = [ctx.enter_context(nc.psum_tensor(f"ps_turn_y{h}", [P, 512], F32)) for h in range(2)]
        block = ctx.enter_context(nc.Block())

        @block.sync
        def _(sp):
            def load(n, i, b, last):
                sp.wait_ge(s["mean_ready"][b], i)
                gate(g, sp)
                sp.dma_start(sums_in[b][:, :], rows_of(g.attn_sums, n * BLOCK)).then_inc(s["sums_loaded"][b], 16)
                sp.wait_ge(s["y_turned"][b][1], i)
                gate(g, sp)
                sp.dma_start(x1_in[b][:, :], rows_of(g.x1_table, n * BLOCK)).then_inc(s["x1_loaded"][b], 16)

            over_blocks(g, sp, load)

        @block.vector
        def _(dve):
            def body(n, i, b):
                rows = sums_in[b][:, :].rearrange("p (r c) -> p r c", c=AT)
                dve.wait_ge(s["sums_loaded"][b], i * 16 + 16)
                dve.wait_ge(s["mean_ready"][1 - b], i + b)
                dve.tensor_scalar(weight[:, :, :], rows[:, :, D:AT], ATTN_EPS, None,
                                  ALU.add).then_inc(s["weights_summed"], 1)
                dve.wait_ge(s["weights_summed"], n + 1)
                dve.reciprocal(inverse[:, :, :], weight[:, :, :]).then_inc(s["inverted"], 1)
                dve.wait_ge(s["inverted"], n + 1)
                dve.wait_ge(s["y_turned"][b][1], i)
                dve.tensor_tensor(mean_v[b][:, :].rearrange("p (r h c) -> p r h c", r=ROWS, h=HEADS),
                                  rows[:, :, 0:D].rearrange("p r (h c) -> p r h c", h=HEADS),
                                  inverse[:, :, :].unsqueeze(3).broadcast_to([P, ROWS, HEADS, DH]),
                                  ALU.mult).then_inc(s["mean_ready"][b], 1)

            def measure_block(n, i, b, last, kept):
                for h in range(2):
                    dve.wait_ge(s["y_copied"][h], n + 1)
                    measured = measure(g, dve, block_of(g, kept, n, turned[b]), n, h, last)
                measured.then_inc(s["measured"][b], 1)

            body(0, 0, 0)
            for first, end, kept in ((0, g.RESIDENT // 2, True), (g.RESIDENT // 2, g.BLOCKS // 2, False)):
                if end > first:
                    for i in loop(dve, first, end):
                        body(i * 2 + 1, i, 1)
                        measure_block(i * 2, i, 0, False, kept)
                        body(i * 2 + 2, i + 1, 0)
                        measure_block(i * 2 + 1, i, 1, False, kept)
            measure_block(g.BLOCKS - 1, g.BLOCKS // 2, 0, True, False)

        @block.tensor
        def _(pe):
            def body(n, i, b, last):
                pe.wait_ge(s["mean_ready"][b], i + 1)
                pe.wait_ge(s["x1_loaded"][b], i * 16 + 16)
                for h in range(2):
                    pe.wait_ge(s["y_copied"][h], n)
                    for r in range(4):
                        at = (4 * h + r) * D
                        to = ps_turn[h][:, r * P:(r + 1) * P]
                        pe.matmul(to, x1_in[b][:, at:at + D], g.ident[:, :], start=True, stop=False)
                        mm = pe.matmul(to, mean_v[b][:, at:at + D], g.ident[:, :], start=False, stop=True)
                    mm.then_inc(s["y_turned"][b][h], 1)

            over_blocks(g, pe, body)

        @block.scalar
        def _(act):
            def body(n, i, b, last, kept):
                for h in range(2):
                    act.wait_ge(s["y_turned"][b][h], i + 1)
                    if not kept:
                        act.wait_ge(s["y_stored"][b], (i - g.RESIDENT // 2) * 16)
                        act.wait_ge(s["measured"][b], i)
                    act.copy(block_of(g, kept, n, turned[b])[:, h * HALF:(h + 1) * HALF],
                             ps_turn[h][:, :]).then_inc(s["y_copied"][h], 1)

            over_kept_blocks(g, act, body)

        @block.gpsimd
        def _(pool):
            def store(n, i, b, last, kept):
                if kept:
                    return
                for h in range(2):
                    pool.wait_ge(s["y_copied"][h], n + 1)
                gate(g, pool)
                pool.dma_start(g.turned_table[bass.ds(n * P, P), :], turned[b][:, :]).then_inc(s["y_stored"][b], 16)

            over_kept_blocks(g, pool, store)
            for b in range(2):
                pool.wait_ge(s["y_stored"][b], 16 * ((g.BLOCKS - g.RESIDENT + 1 - b) // 2))


def batch_norm_coefficients(g, dve, act, s, which, moments, scale, shift):
    if act is not None:
        act.wait_ge(s["bn_step"], 1)
        act.activation(scale[:, :], moments[:, 1:2], ACT.Sqrt, bias=g.eps_col[:, 0:1]).then_inc(s["bn_step"], 1)
        return
    gamma, beta = g.gammas[:, which:which + 1], g.betas[:, which:which + 1]
    dve.bn_aggr(moments[:, :], g.feature_stats[:, :, :].rearrange("p a k -> p (a k)")).then_inc(s["bn_step"], 1)
    dve.wait_ge(s["bn_step"], 2)
    dve.reciprocal(scale[:, :], scale[:, :]).then_inc(s["bn_step"], 1)
    dve.wait_ge(s["bn_step"], 3)
    dve.tensor_tensor(scale[:, :], scale[:, :], gamma, ALU.mult).then_inc(s["bn_step"], 1)
    dve.wait_ge(s["bn_step"], 4)
    dve.tensor_tensor(shift[:, :], moments[:, 0:1], scale[:, :], ALU.mult).then_inc(s["bn_step"], 1)
    dve.wait_ge(s["bn_step"], 5)
    dve.tensor_tensor(shift[:, :], beta, shift[:, :], ALU.subtract).then_inc(s["bn_step"], 1)


def feed_forward(g, s):
    nc = g.nc
    with ExitStack() as ctx:
        def sb(name, shape, dt=F32):
            return ctx.enter_context(nc.sbuf_tensor(f"{name}_z", shape, dt))

        def ps(name):
            return ctx.enter_context(nc.psum_tensor(f"{name}_z", [P, 512], F32))

        moments = sb("moments", [P, 2])
        scale = sb("scale", [P, 1])
        shift = sb("shift", [P, 1])
        y_in = [sb(f"y_in{b}", [P, BLOCK]) for b in range(2)]
        h_in = [sb(f"h_in{b}", [P, BLOCK]) for b in range(2)]
        hidden = [[sb(f"hidden{h}{m}", [P, HALF]) for m in range(2)] for h in range(2)]
        z = [sb(f"z{b}", [P, BLOCK]) for b in range(2)]
        ps_hidden = [[ps(f"ps_hidden{h}{m}") for m in range(2)] for h in range(2)]
        ps_out = [ps(f"ps_out{h}") for h in range(2)]
        block = ctx.enter_context(nc.Block())

        @block.sync
        def _(sp):
            def load(n, i, b, last, kept):
                if kept:
                    return
                sp.wait_ge(s["y_normed"][b], i)
                gate(g, sp)
                sp.dma_start(y_in[b][:, :], g.turned_table[bass.ds(n * P, P), :]).then_inc(s["y_loaded"][b], 16)

            over_kept_blocks(g, sp, load)

        @block.scalar
        def _(act):
            batch_norm_coefficients(g, None, act, s, 0, moments, scale, shift)
            act.wait_ge(s["bn_step"], 6)

            def body(n, i, b, last, kept):
                if not kept:
                    act.wait_ge(s["y_loaded"][b], (i - g.RESIDENT // 2) * 16 + 16)
                act.wait_ge(s["z_measured"][b], i)
                act.activation(h_in[b][:, :], block_of(g, kept, n, y_in[b]), ACT.Identity, bias=shift[:, 0:1],
                               scale=scale[:, 0:1]).then_inc(s["y_normed"][b], 1)
                for h in range(2):
                    act.wait_ge(s["ff_hidden"][h], n + 1)
                    act.activation(hidden[h][0][:, :], ps_hidden[h][0][:, :], ACT.Relu,
                                   bias=g.b1_col[:, 0:1]).then_inc(s["ff_rectified0"][h], 1)

            over_kept_blocks(g, act, body)

        @block.tensor
        def _(pe):
            def body(n, i, b, last):
                pe.wait_ge(s["y_normed"][b], i + 1)
                for h in range(2):
                    pe.wait_ge(s["ff_rectified0"][h], n)
                    pe.wait_ge(s["ff_rectified1"][h], n)
                    for m in range(2):
                        mm = pe.matmul(ps_hidden[h][m][:, :], g.W1_sb[:, m * D:(m + 1) * D],
                                       h_in[b][:, h * HALF:(h + 1) * HALF], start=True, stop=True)
                    mm.then_inc(s["ff_hidden"][h], 1)
                for h in range(2):
                    pe.wait_ge(s["ff_rectified0"][h], n + 1)
                    pe.wait_ge(s["ff_rectified1"][h], n + 1)
                    pe.wait_ge(s["z_ready"][h], n)
                    for m in range(2):
                        mm = pe.matmul(ps_out[h][:, :], g.W2_sb[:, m, :], hidden[h][m][:, :],
                                       start=(m == 0), stop=(m == 1))
                    mm.then_inc(s["ff_out"][h], 1)

            over_blocks(g, pe, body)

        @block.vector
        def _(dve):
            batch_norm_coefficients(g, dve, None, s, 0, moments, scale, shift)

            def body(n, i, b, last, kept):
                z_out = block_of(g, kept, n, z[b])
                for h in range(2):
                    dve.wait_ge(s["ff_hidden"][h], n + 1)
                    dve.tensor_scalar(hidden[h][1][:, :], ps_hidden[h][1][:, :], g.b1_col[:, 1:2], 0.0, ALU.add,
                                      ALU.max).then_inc(s["ff_rectified1"][h], 1)
                for h in range(2):
                    dve.wait_ge(s["ff_out"][h], n + 1)
                    if not kept:
                        dve.wait_ge(s["z_stored"][b], (i - g.RESIDENT // 2) * 16)
                    cols = slice(h * HALF, (h + 1) * HALF)
                    dve.scalar_tensor_tensor(out=z_out[:, cols], in0=ps_out[h][:, :], scalar=g.b2_col[:, 0:1],
                                             in1=h_in[b][:, cols], op0=ALU.add,
                                             op1=ALU.add).then_inc(s["z_ready"][h], 1)
                for h in range(2):
                    dve.wait_ge(s["z_ready"][h], n + 1)
                    measured = measure(g, dve, z_out, n, h, last)
                measured.then_inc(s["z_measured"][b], 1)

            over_kept_blocks(g, dve, body)

        @block.gpsimd
        def _(pool):
            def store(n, i, b, last, kept):
                if kept:
                    return
                for h in range(2):
                    pool.wait_ge(s["z_ready"][h], n + 1)
                gate(g, pool)
                pool.dma_start(g.turned_table[bass.ds(n * P, P), :], z[b][:, :]).then_inc(s["z_stored"][b], 16)

            over_kept_blocks(g, pool, store)
            for b in range(2):
                pool.wait_ge(s["z_stored"][b], 16 * ((g.BLOCKS - g.RESIDENT + 1 - b) // 2))


def finish_output(g, s):
    nc = g.nc
    with ExitStack() as ctx:
        def sb(name, shape, dt=F32):
            return ctx.enter_context(nc.sbuf_tensor(f"{name}_o", shape, dt))

        moments = sb("bn_moments", [P, 2])
        scale = sb("scale", [P, 1])
        shift = sb("shift", [P, 1])
        z_in = [sb(f"z_in{b}", [P, BLOCK]) for b in range(2)]
        x1_in = [sb(f"x1_in{b}", [P, BLOCK]) for b in range(2)]
        normed = [sb(f"normed{b}", [P, BLOCK]) for b in range(2)]
        total = [sb(f"total{b}", [P, BLOCK]) for b in range(2)]
        stats = sb("stats", [P, ROWS, 6])
        row_moments = sb("moments", [P, ROWS, 2])
        root = sb("root", [P, ROWS, 1])
        inverse = sb("inverse", [P, ROWS, 1])
        minus_mean = sb("minus_mean", [P, ROWS, 1])
        rows_out = [sb(f"rows_out{b}", [P, BLOCK]) for b in range(2)]
        ps_turn = [ctx.enter_context(nc.psum_tensor(f"ps_turn_o{h}", [P, 512], F32)) for h in range(2)]
        pieces = parts_of(g.TAIL_PARTS)
        block = ctx.enter_context(nc.Block())

        @block.sync
        def _(sp):
            def load(n, i, b, last, kept):
                if not kept:
                    sp.wait_ge(s["z_normed"][b], i)
                    gate(g, sp)
                    sp.dma_start(z_in[b][:, :], g.turned_table[bass.ds(n * P, P), :]).then_inc(s["z_loaded"][b], 16)
                sp.wait_ge(s["residual_added"][b], i)
                gate(g, sp)
                sp.dma_start(x1_in[b][:, :], rows_of(g.x1_table, n * BLOCK)).then_inc(s["x1_loaded"][b], 16)

            over_kept_blocks(g, sp, load)

        @block.scalar
        def _(act):
            batch_norm_coefficients(g, None, act, s, 1, moments, scale, shift)
            act.wait_ge(s["bn_step"], 6)

            def norm(i, b, kept):
                if not kept:
                    act.wait_ge(s["z_loaded"][b], (i - g.RESIDENT // 2) * 16 + 16)
                act.wait_ge(s["residual_added"][b], i)
                act.activation(normed[b][:, :], block_of(g, kept, i * 2 + b, z_in[b]), ACT.Identity, bias=shift[:, 0:1],
                               scale=scale[:, 0:1]).then_inc(s["z_normed"][b], 1)

            norm(0, 0, True)
            norm(0, 1, True)

            def body(n, i, b, remain, kept):
                act.wait_ge(s["row_moments"], n + 1)
                act.wait_ge(s["normed"][1 - b], i + b)
                act.activation(root[:, :, :], row_moments[:, :, 1:2], ACT.Sqrt,
                               bias=g.eps_col[:, 0:1]).then_inc(s["rooted"], 1)
                if remain > 1:
                    norm(i + 1, b, kept)
                act.wait_ge(s["shifts_ready"], n + 1)
                act.wait_ge(s["out_stored"][b], i * 16)
                for r in range(ROWS):
                    row = slice(r * D, (r + 1) * D)
                    last_row = act.activation(rows_out[b][:, row], total[b][:, row], ACT.Identity,
                                              bias=minus_mean[:, r, :], scale=inverse[:, r, :])
                last_row.then_inc(s["normed"][b], 1)

            for first, end, kept in ((0, g.RESIDENT // 2 - 1, True),
                                     (g.RESIDENT // 2 - 1, g.BLOCKS // 2 - 1, False)):
                if end > first:
                    for i in loop(act, first, end):
                        body(i * 2, i, 0, 4, kept)
                        body(i * 2 + 1, i, 1, 3, kept)
            body(g.BLOCKS - 3, g.BLOCKS // 2 - 1, 0, 2, False)
            body(g.BLOCKS - 2, g.BLOCKS // 2 - 1, 1, 1, False)
            body(g.BLOCKS - 1, g.BLOCKS // 2, 0, 0, False)

        @block.tensor
        def _(pe):
            def body(n, i, b, last):
                pe.wait_ge(s["z_normed"][b], i + 1)
                pe.wait_ge(s["residual_added"][1 - b], i + b)
                for h in range(2):
                    for r in range(4):
                        at = (4 * h + r) * D
                        mm = pe.transpose(ps_turn[h][:, r * D:(r + 1) * D], normed[b][:, at:at + D], g.ident[:, :])
                mm.then_inc(s["z_turned"], 1)

            over_blocks(g, pe, body)

        @block.vector
        def _(dve):
            batch_norm_coefficients(g, dve, None, s, 1, moments, scale, shift)

            def body(n, i, b, last):
                dve.wait_ge(s["z_turned"], n + 1)
                dve.wait_ge(s["x1_loaded"][b], i * 16 + 16)
                dve.wait_ge(s["shifts_ready"], n)
                dve.wait_ge(s["normed"][b], i)
                for h in range(2):
                    cols = slice(h * HALF, (h + 1) * HALF)
                    add = dve.tensor_tensor(total[b][:, cols], ps_turn[h][:, :], x1_in[b][:, cols], ALU.add)
                add.then_inc(s["residual_added"][b], 1)
                dve.wait_ge(s["residual_added"][b], i + 1)
                row_statistics(g, dve, s, total[b], stats, row_moments, n)
                dve.wait_ge(s["rooted"], n + 1)
                dve.reciprocal(inverse[:, :, :], root[:, :, :]).then_inc(s["inverted"], 1)
                dve.wait_ge(s["inverted"], n + 1)
                dve.scalar_tensor_tensor(out=minus_mean[:, :, :], in0=row_moments[:, :, 0:1], scalar=-1.0,
                                         in1=inverse[:, :, :], op0=ALU.mult,
                                         op1=ALU.mult).then_inc(s["shifts_ready"], 1)

            over_blocks(g, dve, body)

        @block.gpsimd
        def _(pool):
            def store(n, i, b, last):
                pool.wait_ge(s["normed"][b], i + 1)
                gate(g, pool)
                for a, z in pieces if last else [(0, P)]:
                    pool.dma_start(rows_of(g.out, n * BLOCK + a * ROWS, (z - a) * ROWS), rows_out[b][a:z, :]
                                   ).then_inc(s["out_stored"][b], 16)

            over_blocks(g, pool, store)
            pool.wait_ge(s["out_stored"][0], 16 * (g.BLOCKS // 2 + len(pieces)))
            pool.wait_ge(s["out_stored"][1], 16 * (g.BLOCKS // 2))


def gnn_then_transformer(nc, **args):
    with ExitStack() as ctx:
        g = Graph(nc, ctx, args)

        cleared = []

        def cleared_sem(name):
            cleared.append(nc.alloc_semaphore(name))
            return cleared[-1]

        def clear():
            nc.clear_and_free_semaphores(list(cleared))
            cleared.clear()
            nc.all_engine_barrier()

        def sems(prefix, pairs="", singles="", quads="", tiles=""):
            made = {n: [cleared_sem(f"{prefix}_{n}{b}") for b in range(2)] for n in pairs.split()}
            made |= {n: [[cleared_sem(f"{prefix}_{n}{b}{h}") for h in range(2)] for b in range(2)]
                     for n in quads.split()}
            made |= {n: [[cleared_sem(f"{prefix}_{n}{b}{j}") for j in range(TILES)] for b in range(2)]
                     for n in tiles.split()}
            return made | {n: cleared_sem(f"{prefix}_{n}") for n in singles.split()}

        setup(g)
        start_sums(g)
        messages = sems("m", "gathered numbers_ready result_ready same_ready offsets_loaded turn_copied "
                             "ends_turned hidden_ready hidden_summed windows_loaded target_rows_found "
                             "target_rows_picked",
                        "messages_ready messages_summed combined zeros_made zeros_stored "
                        "repeats_counted rows_moved rows_found", tiles="scattered")
        nodes = sems("u", "sums_loaded h_copied sum_ready h_projected sums_stored", quads="h_turned")
        with nc.sbuf_tensor("zeros", [P, TILES * AT], F32) as zeros:
            with nc.Block() as block:
                @block.vector
                def _(dve):
                    dve.memset(zeros[:, :], 0.0).then_inc(messages["zeros_made"], 1)

                @block.sync
                def _(sp):
                    sp.wait_ge(messages["zeros_made"], 1)
                    gate(g, sp)
                    for sums in g.sums:
                        sp.dma_start(rows_of(sums, g.SPARE_ROWS, GROUP, TILES), zeros[:, 0:TILES * D]
                                     ).then_inc(messages["zeros_stored"], 16)
                    sp.dma_start(rows_of(g.attn_sums, g.SPARE_ROWS, GROUP, TILES), zeros[:, :]
                                 ).then_inc(messages["zeros_stored"], 16)
                    sp.wait_ge(messages["zeros_stored"], 48)
            pass_messages(g, messages, 0, g.x, zeros[:, :])
        for k in range(1, 3):
            update_nodes(g, nodes, k - 1)
            pass_messages(g, messages, k, g.sums[(k + 1) % 2][:, :])
        clear()
        finish_messages(g, sems("f", "sums_loaded x_loaded x1_stored residual_added normed",
                                "row_stats row_moments rooted inverted shifts_ready"))
        attend(g, sems("t", "gathered numbers_ready result_ready same_ready offsets_loaded edges_loaded "
                            "windows_loaded target_rows_found target_rows_picked edges_turned "
                            "combined",
                       "edges_copied sources_turned sources_copied targets_turned targets_copied kv_projected "
                       "kv_copied queries_projected multiplied edges_projected edges_used scored scaled clipped weights_ready "
                       "values_weighted table_loaded", tiles="scattered"))
        clear()
        g.kept = ctx.enter_context(nc.sbuf_tensor("kept", [P, g.RESIDENT, BLOCK], F32))
        finish_attention(g, sems("y", "sums_loaded x1_loaded y_copied y_stored mean_ready measured",
                                 "weights_summed inverted", "y_turned"))
        feed_forward(g, sems("z", "y_loaded y_normed ff_hidden ff_rectified0 ff_rectified1 z_ready ff_out z_stored z_measured",
                             "bn_step"))
        finish_output(g, sems("o", "z_loaded x1_loaded z_normed out_stored residual_added normed",
                              "bn_step z_turned row_stats row_moments rooted inverted shifts_ready"))


_INS = ['x', 'src', 'dst', 'edge_attr_128', 'L0_gnn_Wm1', 'L0_gnn_bm1', 'L0_gnn_Wm2', 'L0_gnn_bm2', 'L0_gnn_Wn',
        'L0_gnn_bn', 'L1_gnn_WQ', 'L1_gnn_WK', 'L1_gnn_WV', 'L1_gnn_WE', 'L1_gnn_gamma1', 'L1_gnn_beta1',
        'L1_gnn_gamma2', 'L1_gnn_beta2', 'L1_gnn_W1', 'L1_gnn_b1', 'L1_gnn_W2', 'L1_gnn_b2']


def kernel(**inputs):
    import numpy as _np
    import concourse.bacc as _bacc
    from concourse import mybir as _mybir
    from concourse.bass_utils import run_bass_kernel_spmd as _run

    nc = _bacc.Bacc("TRN2", target_bir_lowering=False, num_devices=1)
    arrays, args = {}, {}
    for name in _INS:
        a = _np.ascontiguousarray(inputs[name])
        arrays[f"in_{name}_dram"] = a
        args[name] = nc.dram_tensor(f"in_{name}_dram", a.shape, _mybir.dt.from_np(a.dtype),
                                    kind="ExternalInput").ap()
    args["out"] = nc.dram_tensor("out_dram", inputs["x"].shape, _mybir.dt.float32, kind="ExternalOutput").ap()
    gnn_then_transformer(nc, **args)
    r = _run(nc, [arrays], core_ids=[0])
    return r.results[0]["out_dram"]
```
